# Optimizing a Trainium2 kernel written in Bass

```python
import numpy as np
import jax
import jax.numpy as jnp

def _softmax(x, axis=-1):
    return jax.nn.softmax(x, axis=axis)

def _gelu(x):
    return jax.nn.gelu(x, approximate=True)

def _silu(x):
    return jax.nn.silu(x)

def _sigmoid(x):
    return jax.nn.sigmoid(x)

def _layernorm(x, axis=-1, eps=1e-05):
    m = jnp.mean(x, axis=axis, keepdims=True)
    v = jnp.var(x, axis=axis, keepdims=True)
    return (x - m) / jnp.sqrt(v + eps)

def _scatter_add(tgt, idx, src, axis=0):
    return tgt.at[idx].add(src)

def _segment_sum(src, seg, n):
    return jax.ops.segment_sum(src, seg, n)
kernel_name = 'mk_gnn_preln_d2_gnn_r8_53603a'

def setup_inputs(seed: int=0):
    np.random.seed(seed)
    _w = jnp.asarray

    def _rec_inputs():
        import jax
        import jax.numpy as jnp
        _gk = jax.random.key(seed)
        x = -0.0003713 + 1 * jax.random.normal(jax.random.fold_in(_gk, 1), (6250, 256), jnp.float32)
        src = jax.random.randint(jax.random.fold_in(_gk, 2), (100000,), 0, 6250, jnp.int32)
        dst = jax.random.randint(jax.random.fold_in(_gk, 3), (100000,), 0, 6250, jnp.int32)
        _o = jnp.argsort(dst, stable=True)
        src = src[_o]
        dst = dst[_o]
        edge_attr_16 = -0.00010739 + 0.99994 * jax.random.normal(jax.random.fold_in(_gk, 12), (100000, 16), jnp.float32)
        edge_attr_4 = jax.random.uniform(jax.random.fold_in(_gk, 13), (100000, 4), jnp.float32, 0.0, 1)
        return (x, src, dst, edge_attr_16, edge_attr_4)
    x, src, dst, edge_attr_16, edge_attr_4 = _rec_inputs()

    def _L0_gnn_setup():
        import jax, jax.numpy as jnp
        import numpy as np
        N = 6250
        E = 100000
        IN_DIM = 256
        H = 8
        D = 32
        T = 4
        F = 16
        NEG_SLOPE = 0.2
        key = jax.random.key(seed)
        ks = jax.random.split(key, 9)
        feat = jax.random.normal(ks[0], (N, IN_DIM), dtype=jnp.float32)
        e_pro = jax.random.normal(ks[1], (E, F), dtype=jnp.float32)
        mask = jax.random.uniform(ks[2], (E, T), dtype=jnp.float32)
        W_n = jax.random.normal(ks[3], (IN_DIM, H * D), dtype=jnp.float32) * (1.0 / np.sqrt(IN_DIM))
        attn_l = jax.random.normal(ks[4], (H, D, T), dtype=jnp.float32) * 0.1
        attn_r = jax.random.normal(ks[5], (H, D, T), dtype=jnp.float32) * 0.1
        attn_m = jax.random.normal(ks[6], (H, F, T), dtype=jnp.float32) * 0.1
        src = jax.random.randint(ks[7], (E,), 0, N, dtype=jnp.int32)
        dst = jax.random.randint(ks[8], (E,), 0, N, dtype=jnp.int32)
        return {'feat': feat, 'e_pro': e_pro, 'mask': mask, 'W_n': W_n, 'attn_l': attn_l, 'attn_r': attn_r, 'attn_m': attn_m, 'src': src, 'dst': dst}
    _L0_gnn_all = _L0_gnn_setup()
    _L0_gnn_in = {k: v for k, v in _L0_gnn_all.items() if k in ('W_n', 'attn_l', 'attn_r', 'attn_m')}
    del _L0_gnn_all

    def _L1_gnn_setup():
        import jax, jax.numpy as jnp
        import numpy as np
        N = 6250
        E = 37500
        D = 256
        EPS_NORM = 1e-12
        EPS_LN = 1e-05

        def sage_conv(x, src, dst, pW, pb, lW, lb, rW):
            msg = jax.nn.relu(x @ pW + pb)[src]
            agg = jax.ops.segment_sum(msg, dst, num_segments=N)
            deg = jax.ops.segment_sum(jnp.ones((src.shape[0],), msg.dtype), dst, num_segments=N)
            mean = agg / jnp.maximum(deg, 1.0)[:, None]
            out = mean @ lW + lb + x @ rW
            nrm = jnp.maximum(jnp.linalg.norm(out, axis=-1, keepdims=True), EPS_NORM)
            return out / nrm
        key = jax.random.key(seed)
        ks = jax.random.split(key, 20)
        s = np.float32(1.0 / np.sqrt(D))
        inp = {'x': jax.random.normal(ks[0], (N, D), jnp.float32), 'edge_index': jax.random.randint(ks[1], (2, E), 0, N, dtype=jnp.int64)}
        i = 2
        for l in range(3):
            inp[f'pW{l}'] = jax.random.normal(ks[i + 0], (D, D), jnp.float32) * s
            inp[f'pb{l}'] = jax.random.normal(ks[i + 1], (D,), jnp.float32) * s
            inp[f'lW{l}'] = jax.random.normal(ks[i + 2], (D, D), jnp.float32) * s
            inp[f'lb{l}'] = jax.random.normal(ks[i + 3], (D,), jnp.float32) * s
            inp[f'rW{l}'] = jax.random.normal(ks[i + 4], (D, D), jnp.float32) * s
            i += 5
        inp['ln_w'] = jnp.ones((D,), jnp.float32)
        inp['ln_b'] = jnp.zeros((D,), jnp.float32)
        return inp
    _L1_gnn_all = _L1_gnn_setup()
    _L1_gnn_in = {k: v for k, v in _L1_gnn_all.items() if k in ('pW0', 'pb0', 'lW0', 'lb0', 'rW0', 'pW1', 'pb1', 'lW1', 'lb1', 'rW1', 'pW2', 'pb2', 'lW2', 'lb2', 'rW2', 'ln_w', 'ln_b')}
    del _L1_gnn_all
    return {'x': x, 'src': src, 'dst': dst, 'edge_attr_16': edge_attr_16, 'edge_attr_4': edge_attr_4, 'L0_gnn_W_n': _L0_gnn_in['W_n'], 'L0_gnn_attn_l': _L0_gnn_in['attn_l'], 'L0_gnn_attn_r': _L0_gnn_in['attn_r'], 'L0_gnn_attn_m': _L0_gnn_in['attn_m'], 'L1_gnn_pW0': _L1_gnn_in['pW0'], 'L1_gnn_pb0': _L1_gnn_in['pb0'], 'L1_gnn_lW0': _L1_gnn_in['lW0'], 'L1_gnn_lb0': _L1_gnn_in['lb0'], 'L1_gnn_rW0': _L1_gnn_in['rW0'], 'L1_gnn_pW1': _L1_gnn_in['pW1'], 'L1_gnn_pb1': _L1_gnn_in['pb1'], 'L1_gnn_lW1': _L1_gnn_in['lW1'], 'L1_gnn_lb1': _L1_gnn_in['lb1'], 'L1_gnn_rW1': _L1_gnn_in['rW1'], 'L1_gnn_pW2': _L1_gnn_in['pW2'], 'L1_gnn_pb2': _L1_gnn_in['pb2'], 'L1_gnn_lW2': _L1_gnn_in['lW2'], 'L1_gnn_lb2': _L1_gnn_in['lb2'], 'L1_gnn_rW2': _L1_gnn_in['rW2'], 'L1_gnn_ln_w': _L1_gnn_in['ln_w'], 'L1_gnn_ln_b': _L1_gnn_in['ln_b']}

def reference(x, src, dst, edge_attr_16, edge_attr_4, L0_gnn_W_n, L0_gnn_attn_l, L0_gnn_attn_r, L0_gnn_attn_m, L1_gnn_pW0, L1_gnn_pb0, L1_gnn_lW0, L1_gnn_lb0, L1_gnn_rW0, L1_gnn_pW1, L1_gnn_pb1, L1_gnn_lW1, L1_gnn_lb1, L1_gnn_rW1, L1_gnn_pW2, L1_gnn_pb2, L1_gnn_lW2, L1_gnn_lb2, L1_gnn_rW2, L1_gnn_ln_w, L1_gnn_ln_b):
    import jax
    import jax.numpy as jnp

    def _L0_gnn_ref(feat, e_pro, mask, W_n, attn_l, attn_r, attn_m, src, dst):
        import jax, jax.numpy as jnp
        import numpy as np
        N = 6250
        E = 100000
        IN_DIM = 256
        H = 8
        D = 32
        T = 4
        F = 16
        NEG_SLOPE = 0.2
        feat_src = (feat @ W_n).reshape(N, H, D)
        el = jnp.einsum('nhd,hdt->nht', feat_src, attn_l)
        er = jnp.einsum('nhd,hdt->nht', feat_src, attn_r)
        em = jnp.einsum('ef,hft->eht', e_pro, attn_m)
        left = jnp.einsum('eht,et->eh', el[src], mask)
        right = jnp.einsum('eht,et->eh', er[dst], mask)
        em_e = jnp.einsum('eht,et->eh', em, mask)
        e = (left + right + em_e) / 3.0
        e = jnp.where(e > 0, e, NEG_SLOPE * e)
        e_max = jax.ops.segment_max(e, dst, num_segments=N)
        e_exp = jnp.exp(e - e_max[dst])
        e_sum = jax.ops.segment_sum(e_exp, dst, num_segments=N)
        a = e_exp / e_sum[dst]
        msg = feat_src[src] * a[:, :, None]
        rst = jax.ops.segment_sum(msg, dst, num_segments=N)
        return rst.reshape(N, H * D)

    def _L1_gnn_ref(x, edge_index, pW0, pb0, lW0, lb0, rW0, pW1, pb1, lW1, lb1, rW1, pW2, pb2, lW2, lb2, rW2, ln_w, ln_b):
        import jax, jax.numpy as jnp
        import numpy as np
        N = 6250
        E = 37500
        D = 256
        EPS_NORM = 1e-12
        EPS_LN = 1e-05

        def sage_conv(x, src, dst, pW, pb, lW, lb, rW):
            msg = jax.nn.relu(x @ pW + pb)[src]
            agg = jax.ops.segment_sum(msg, dst, num_segments=N)
            deg = jax.ops.segment_sum(jnp.ones((src.shape[0],), msg.dtype), dst, num_segments=N)
            mean = agg / jnp.maximum(deg, 1.0)[:, None]
            out = mean @ lW + lb + x @ rW
            nrm = jnp.maximum(jnp.linalg.norm(out, axis=-1, keepdims=True), EPS_NORM)
            return out / nrm
        src, dst = (edge_index[0], edge_index[1])
        h = jax.nn.silu(sage_conv(x, src, dst, pW0, pb0, lW0, lb0, rW0))
        h = jax.nn.silu(sage_conv(h, src, dst, pW1, pb1, lW1, lb1, rW1))
        h = sage_conv(h, src, dst, pW2, pb2, lW2, lb2, rW2)
        mu = jnp.mean(h, axis=-1, keepdims=True)
        var = jnp.mean(jnp.square(h - mu), axis=-1, keepdims=True)
        return (h - mu) * jax.lax.rsqrt(var + EPS_LN) * ln_w + ln_b
    edge_index = jnp.stack([src, dst])
    h = jnp.maximum(_layernorm(x, axis=-1), 0.0)
    x = x + _L0_gnn_ref(h, edge_attr_16, edge_attr_4, L0_gnn_W_n, L0_gnn_attn_l, L0_gnn_attn_r, L0_gnn_attn_m, src, dst)
    h = jnp.maximum(_layernorm(x, axis=-1), 0.0)
    x = x + _L1_gnn_ref(h, edge_index, L1_gnn_pW0, L1_gnn_pb0, L1_gnn_lW0, L1_gnn_lb0, L1_gnn_rW0, L1_gnn_pW1, L1_gnn_pb1, L1_gnn_lW1, L1_gnn_lb1, L1_gnn_rW1, L1_gnn_pW2, L1_gnn_pb2, L1_gnn_lW2, L1_gnn_lb2, L1_gnn_rW2, L1_gnn_ln_w, L1_gnn_ln_b)
    return x

_drawn_inputs = setup_inputs


def setup_inputs(seed=0):
    import zlib

    import numpy as np

    out = dict(_drawn_inputs(seed))
    spreads = {'L1_gnn_ln_w': (1.0, 0.2), 'L1_gnn_ln_b': (0.0, 0.1)}
    factors = {'edge_attr_16': 4.733,
     'edge_attr_4': 5.395,
     'L0_gnn_attn_l': 5.309,
     'L0_gnn_attn_r': 7.568,
     'L0_gnn_attn_m': 4.495,
     'L1_gnn_pb0': 8.0,
     'L1_gnn_lb0': 4.752}
    for name, (base, spread) in spreads.items():
        noise = np.random.default_rng([zlib.crc32(name.encode()), seed]).standard_normal(out[name].shape)
        drawn = base * np.exp(spread * noise) if base else spread * noise
        out[name] = jnp.asarray(drawn.astype(out[name].dtype))
    for name, factor in factors.items():
        out[name] = (out[name] * factor).astype(out[name].dtype)
    return out
```

```python
import numpy as np
import concourse.bass as bass
from concourse import mybir
from contextlib import ExitStack
from itertools import count

fp32 = mybir.dt.float32
int32 = mybir.dt.int32
ALU = mybir.AluOpType
ACT = mybir.ActivationFunctionType
AX = mybir.AxisListType

P = 128
N, E, D = 6250, 100000, 256
HEADS, HD, KINDS, FEATS = 8, 32, 4, 16
LAYERS = 3
BLOCKS = -(-N // P)
TILES = 7
CHUNK = TILES * P
CHUNKS = -(-E // CHUNK)
SLOTS = 4
ROUNDS = CHUNKS // SLOTS
assert CHUNKS == ROUNDS * SLOTS
TABLE = BLOCKS * P + P
GROUP = 7
GROUPS = BLOCKS // GROUP
assert BLOCKS == GROUP * GROUPS
HW = HD + 1
WIDE = HEADS * HW
ROW = WIDE + HEADS * KINDS
SUMC = WIDE + 1
FAR = 1.0e30
LN_EPS = 1e-5
NORM_EPS = 1e-12
SLOPE = 0.2


PHASE_NUMBERS = count()


class Mem:
    pass


class Count:

    def __init__(self, sem, buffers):
        self.sem, self.buffers = sem, buffers

    def done(self, n):
        return self.buffers + n + 1

    def free(self, n):
        return n + 1


def phase(nc, name, **sems):
    stack = ExitStack()
    made = Mem()
    made.of = {}
    name = f"{name}{next(PHASE_NUMBERS)}"
    for key, buffers in sems.items():
        sem = nc.alloc_semaphore(f"{name}_{key}")
        made.of[key] = sem if buffers is None else Count(sem, buffers)
        if buffers:
            nc.gpsimd.sem_inc(sem, buffers)
    handles = [c.sem if isinstance(c, Count) else c for c in made.of.values()]

    def clear():
        nc.clear_and_free_semaphores(handles)
        nc.all_engine_barrier()

    stack.callback(clear)
    nc.all_engine_barrier()
    return stack, stack.enter_context(nc.Block()), made.of


def hold(eng, sem, value):
    eng.wait_ge(sem, value)
    eng.nop(nofuse=True)


def group_rows(ap):
    return ap.rearrange("(g j p) d -> g p j d", p=P, j=GROUP)


def rounds(eng, body):
    with eng.Fori(0, ROUNDS - 1) as i:
        for k in range(SLOTS):
            body(i, k, False)
    for k in range(SLOTS):
        body(ROUNDS - 1, k, k == SLOTS - 1)


def setup(nc, m, a):
    stack, block, s = phase(nc, "setup", zeroed=0, iota=0, loaded=None, tr_w=0, wt_done=0, fold=0, done_v=0, dv=0, conv=0,
                            zrows=0, zstored=None, flag=0, flag_far=0, fstored=None,
                            odd=0, odd_sum=0, odd_max=0)
    with stack:
        @block.gpsimd
        def _(pool):
            nc.gpsimd.iota(m.iota_row[:], [[1, P]], base=0, channel_multiplier=0,
                           allow_small_or_imprecise_dtypes=True)
            nc.gpsimd.iota(m.iota_p[:], [[0, 1]], base=0, channel_multiplier=1,
                           allow_small_or_imprecise_dtypes=True)
            nc.gpsimd.iota(m.step[:], [[-1, P]], base=0, channel_multiplier=1,
                           allow_small_or_imprecise_dtypes=True).then_inc(s["iota"].sem, 1)

        @block.sync
        def _(sp):
            def load(out, in_):
                sp.dma_start(out, in_).then_inc(s["loaded"], 16)

            load(m.w_node[:, :, 0:D], a["L0_gnn_W_n"].rearrange("(k p) n -> p k n", p=P))
            load(m.attn_edge[:], a["L0_gnn_attn_m"].rearrange("h f t -> f h t"))
            for l in range(LAYERS):
                for half, w in ((0, f"L1_gnn_pW{l}"), (1, f"L1_gnn_rW{l}")):
                    load(m.w_pr[:, l, :, half * D:(half + 1) * D], a[w].rearrange("(k p) n -> p k n", p=P))
                for half, w in ((0, f"L1_gnn_pb{l}"), (1, f"L1_gnn_lb{l}")):
                    load(m.bias[:, l, half * D:(half + 1) * D], a[w][None, :].to_broadcast([P, D]))
                load(m.w_l[:, l], a[f"L1_gnn_lW{l}"].rearrange("(k p) n -> p k n", p=P))
            load(m.ln_w[:], a["L1_gnn_ln_w"][None, :].to_broadcast([P, D]))
            load(m.ln_b[:], a["L1_gnn_ln_b"][None, :].to_broadcast([P, D]))
            sp.wait_ge(s["zrows"].sem, 1)
            for table, row in ((m.sums, SUMC), (m.agg_dram, D)):
                for b in range(0, BLOCKS + 1, GROUP):
                    n = min(GROUP, BLOCKS + 1 - b)
                    sp.dma_start(table[b * P:(b + n) * P].rearrange("(j p) d -> p j d", p=P),
                                 m.zeros[:, 0:n * row].rearrange("p (j d) -> p j d", d=row)).then_inc(s["zstored"], 16)
            sp.dma_start(m.right_dram[BLOCKS * P:TABLE], m.zeros[:, 0:HEADS * KINDS]).then_inc(s["zstored"], 16)
            sp.wait_ge(s["flag_far"].sem, 1)
            sp.dma_start(m.flag_dram.rearrange("(p n) -> p n", p=P), m.lin_f).then_inc(s["fstored"], 16)
            sp.wait_ge(s["fstored"], 16)
            sp.wait_ge(s["zstored"], 16 * (2 * -(-(BLOCKS + 1) // GROUP) + 1))

        @block.scalar
        def _(act):
            def load(out, in_):
                act.dma_start(out, in_).then_inc(s["loaded"], 16)

            load(m.src[:], a["src"])
            load(m.dst, a["dst"])
            load(m.lin_a, a["dst_line"])
            load(m.lin_b, a["dst_line_before"])
            load(m.first[:], a["chunk_first"])
            load(m.last_all, a["chunk_last"].to_broadcast([P, CHUNKS]))
            load(m.first_all, a["chunk_first"].to_broadcast([P, CHUNKS]))
            act.wait_ge(s["zeroed"].sem, 1)
            for side, w in ((0, "L0_gnn_attn_l"), (1, "L0_gnn_attn_r")):
                for h in range(HEADS):
                    at = (h % 4) * HD
                    col = side * HEADS * KINDS + h * KINDS
                    load(m.attn_diag[at:at + HD, h // 4, col:col + KINDS], a[w][h])

        loads = 16 * (2 + 5 * LAYERS + 2 + 7 + 2 * HEADS)

        @block.vector
        def _(dve):
            nc.vector.memset(m.attn_diag[:], 0.0).then_inc(s["zeroed"].sem, 1)
            nc.vector.memset(m.zeros, 0.0).then_inc(s["zrows"].sem, 1)
            nc.vector.memset(m.eps_ln[:], LN_EPS)
            nc.vector.memset(m.ones[:], 1.0)
            nc.vector.memset(m.flags, -FAR)
            nc.vector.memset(m.run_max, 0.0)
            nc.vector.memset(m.carry[:], 0.0)
            nc.vector.memset(m.sums_out, 0.0).then_inc(s["dv"].sem, 1)
            dve.wait_ge(s["iota"].sem, 1)
            nc.vector.tensor_scalar(m.ident[:], m.step[:], 0.0, None, ALU.is_equal).then_inc(s["dv"].sem, 1)
            dve.wait_ge(s["loaded"], loads)
            nc.vector.tensor_copy(m.first_f, m.first_all).then_inc(s["conv"].sem, 1)
            dve.wait_ge(s["conv"].sem, 1)
            nc.vector.tensor_scalar(m.window_p[:], m.first_f, m.iota_p[:, 0:1], None, ALU.add)
            nc.vector.memset(m.shift_by[:], 0.0).then_inc(s["conv"].sem, 1)
            dve.wait_ge(s["conv"].sem, 2)
            nc.vector.tensor_tensor(m.shift_by[:, 1:CHUNKS], m.first_f[:, 1:CHUNKS], m.first_f[:, 0:CHUNKS - 1], ALU.subtract)
            nc.vector.tensor_tensor(m.dst_rel[:].rearrange("p (c t) -> p c t", t=TILES),
                                    m.dst.rearrange("p (c t) -> p c t", t=TILES),
                                    m.first_f[:, :, None].to_broadcast([P, CHUNKS, TILES]), ALU.subtract)
            nc.vector.tensor_tensor(m.lin_f, m.lin_a, m.lin_b, ALU.not_equal).then_inc(s["flag"].sem, 1)
            dve.wait_ge(s["flag"].sem, 1)
            nc.vector.tensor_scalar(m.lin_f, m.lin_f, -FAR, None, ALU.mult).then_inc(s["flag_far"].sem, 1)
            nc.vector.tensor_tensor(m.odd_line, m.lin_a, m.lin_b, ALU.is_lt)
            nc.vector.tensor_scalar(m.odd_span, m.first_all, float(P), None, ALU.add).then_inc(s["odd"].sem, 1)
            dve.wait_ge(s["odd"].sem, 1)
            nc.vector.tensor_tensor(m.odd_span, m.last_all, m.odd_span, ALU.is_ge).then_inc(s["odd"].sem, 1)
            dve.wait_ge(s["odd"].sem, 2)
            nc.vector.tensor_reduce(m.odd[:], m.odd_all, AX.X, ALU.add).then_inc(s["odd"].sem, 1)
            dve.wait_ge(s["tr_w"].sem, 1)
            for j in range(2):
                last = nc.vector.tensor_copy(m.w_nodeT[:, j, :], m.ps[:, j, 0:D])
            last.then_inc(s["wt_done"].sem, 1)
            dve.wait_ge(s["fold"].sem, 1)
            nc.vector.tensor_copy(m.w_node[:, :, D:D + 2 * HEADS * KINDS],
                                  m.ps[:, 2:4, 0:2 * HEADS * KINDS]).then_inc(s["done_v"].sem, 1)
            dve.wait_ge(s["odd_sum"].sem, 1)
            nc.vector.tensor_copy(m.irregular[:], m.ps[0:1, 4, 0:1]).then_inc(s["done_v"].sem, 1)
            dve.wait_ge(s["done_v"].sem, 2)

        @block.tensor
        def _(pe):
            pe.wait_ge(s["odd"].sem, 3)
            nc.tensor.matmul(m.ps[0:1, 4, 0:1], m.odd[:], m.ones[:], start=True, stop=True).then_inc(s["odd_sum"].sem, 1)
            pe.wait_ge(s["loaded"], loads)
            pe.wait_ge(s["dv"].sem, 2)
            for k in range(2):
                for j in range(2):
                    last = nc.tensor.transpose(m.ps[:, j, k * P:(k + 1) * P],
                                               m.w_node[:, k, j * P:(j + 1) * P], m.ident[:])
            last.then_inc(s["tr_w"].sem, 1)
            pe.wait_ge(s["wt_done"].sem, 1)
            for k in range(2):
                for j in range(2):
                    last = nc.tensor.matmul(m.ps[:, 2 + k, 0:2 * HEADS * KINDS], m.w_nodeT[:, j, k * P:(k + 1) * P],
                                            m.attn_diag[:, j, :], start=(j == 0), stop=(j == 1))
            last.then_inc(s["fold"].sem, 1)


def ln_vector(nc, dve, m, s, x, g):
    for j in range(GROUP):
        last = nc.vector.bn_stats(m.bn[:, j, :], x[:, j, :])
    last.then_inc(s["ln_stats"].sem, 1)
    hold(dve, s["ln_stats"].sem, s["ln_stats"].done(g))
    for j in range(GROUP):
        last = nc.vector.bn_aggr(m.mv[:, j, :], m.bn[:, j, :])
    last.then_inc(s["ln_mv"].sem, 1)
    dve.wait_ge(s["ln_sqrt"].sem, s["ln_sqrt"].done(g))
    nc.vector.reciprocal(m.rstd[:], m.std[:]).then_inc(s["ln_rstd"].sem, 1)
    dve.wait_ge(s["ln_rstd"].sem, s["ln_rstd"].done(g))
    nc.vector.scalar_tensor_tensor(m.shift[:], m.mv[:, :, 0], -1.0, m.rstd[:], ALU.mult, ALU.mult).then_inc(s["ln_shift"].sem, 1)


def ln_scalar_sqrt(nc, act, m, s, g):
    act.wait_ge(s["ln_mv"].sem, s["ln_mv"].done(g))
    nc.scalar.activation(m.std[:], m.mv[:, :, 1], ACT.Sqrt, bias=m.eps_ln[:, 0:1]).then_inc(s["ln_sqrt"].sem, 1)


def ln_scalar_apply(nc, act, m, s, x, out, func, g):
    act.wait_ge(s["ln_shift"].sem, s["ln_shift"].done(g))
    for j in range(GROUP):
        last = nc.scalar.activation(out[:, j, :], x[:, j, :], func, bias=m.shift[:, j:j + 1], scale=m.rstd[:, j:j + 1])
    last.then_inc(s["h"].sem, 1)


def transpose_group(nc, m, rows):
    for j in range(GROUP):
        for k in range(2):
            at = j * 2 + k
            last = nc.tensor.transpose(m.ps[:, at // 4, (at % 4) * P:(at % 4 + 1) * P],
                                       rows[:, j, k * P:(k + 1) * P], m.ident[:])
    return last


def copy_transposed(nc, m):
    return nc.scalar.activation(m.hT.rearrange("p j k n -> p (j k n)"),
                                m.ps[:, 0:4, :].rearrange("p b n -> p (b n)")[:, 0:GROUP * D], ACT.Copy)


def group_dma(eng, ap, g, tile, store=False):
    rows = ap[bass.ds(g, 1)].rearrange("o p j d -> (o p) j d")
    return eng.dma_start(rows, tile) if store else eng.dma_start(tile, rows)


def node_features(nc, m, a):
    stack, block, s = phase(nc, "nodes", x=None, ln_stats=0, ln_mv=0, ln_sqrt=0, ln_rstd=0, ln_shift=0, h=1, trans=1, ht=1,
                            mm=GROUP, evac=4, stored=None, out_free=1, zero=0)
    x_g, table, right = group_rows(a["x"]), group_rows(m.table0), group_rows(m.right_dram[0:BLOCKS * P])
    with stack:
        @block.sync
        def _(sp):
            with sp.Fori(0, GROUPS) as g:
                sp.wait_ge(s["h"].sem, s["h"].free(g))
                group_dma(sp, x_g, g, m.x_in[:]).then_inc(s["x"], 16)

        @block.gpsimd
        def _(pool):
            with pool.Fori(0, GROUPS) as g:
                pool.wait_ge(s["evac"].sem, s["evac"].done((g + 1) * GROUP - 1))
                group_dma(pool, table, g, m.table_rows, store=True).then_inc(s["stored"], 16)
                group_dma(pool, right, g, m.right_rows, store=True).then_inc(s["stored"], 16)
                pool.wait_ge(s["stored"], 32 * (g + 1))
                pool.sem_inc(s["out_free"].sem, 1)

        @block.vector
        def _(dve):
            nc.vector.memset(m.table_rows, 0.0).then_inc(s["zero"].sem, 1)
            dve.wait_ge(s["zero"].sem, 1)
            with dve.Fori(0, GROUPS) as g:
                dve.wait_ge(s["x"], 16 * g + 16)
                ln_vector(nc, dve, m, s, m.x_in, g)
                dve.wait_ge(s["out_free"].sem, s["out_free"].free(g))
                for j in range(GROUP):
                    dve.wait_ge(s["mm"].sem, s["mm"].done(g * GROUP + j))
                    out = m.ps[:, 4 + j % 4, :]
                    nc.vector.tensor_copy(m.table_rows[:, j, 0:WIDE].rearrange("p (h c) -> p h c", c=HW)[:, :, 0:HD],
                                          out[:, 0:D].rearrange("p (h c) -> p h c", c=HD))
                    nc.vector.tensor_copy(m.table_rows[:, j, WIDE:ROW], out[:, D:D + 32])
                    nc.vector.tensor_copy(m.right_rows[:, j, :], out[:, D + 32:D + 64]).then_inc(s["evac"].sem, 1)

        @block.scalar
        def _(act):
            with act.Fori(0, GROUPS) as g:
                ln_scalar_sqrt(nc, act, m, s, g)
                act.wait_ge(s["trans"].sem, s["trans"].free(g))
                ln_scalar_apply(nc, act, m, s, m.x_in, m.h, ACT.Relu, g)
                act.wait_ge(s["trans"].sem, s["trans"].done(g))
                act.wait_ge(s["mm"].sem, s["mm"].free((g + 1) * GROUP - 1))
                copy_transposed(nc, m).then_inc(s["ht"].sem, 1)

        @block.tensor
        def _(pe):
            with pe.Fori(0, GROUPS) as g:
                pe.wait_ge(s["h"].sem, s["h"].done(g))
                pe.wait_ge(s["ht"].sem, s["ht"].free(g))
                transpose_group(nc, m, m.h).then_inc(s["trans"].sem, 1)
                pe.wait_ge(s["ht"].sem, s["ht"].done(g))
                for j in range(GROUP):
                    pe.wait_ge(s["evac"].sem, s["evac"].free(g * GROUP + j) if j >= 4 else s["evac"].done(g * GROUP - 1))
                    for k in range(2):
                        last = nc.tensor.matmul(m.ps[:, 4 + j % 4, 0:D + 64], m.hT[:, j, k, :], m.w_node[:, k, :],
                                                start=(k == 0), stop=(k == 1))
                    last.then_inc(s["mm"].sem, 1)


def gather_chunks(nc, pool, m, s, cols, table):
    pair = 2 * TILES

    def body(i, k, last):
        half = k // 2
        if k % 2 == 0:
            pool.wait_ge(s["rows_used"].sem, s["rows_used"].free(i * SLOTS + k + 1))
            nc.gpsimd.tensor_copy(m.index[:, half, :], m.src[:, bass.ds(i * SLOTS * TILES + half * pair, pair)]).then_inc(s["index"].sem, 1)
            hold(pool, s["index"].sem, s["index"].done(i * 2 + half))
        for t in range(TILES):
            at = (k % 2) * TILES + t
            pool.indirect_dma_start(m.ring[:, k, t, 0:cols], None, table,
                                    bass.IndirectOffsetOnAxis(ap=m.index[:, half, at:at + 1], axis=0)).then_inc(s[f"rows{k}"], 16)

    rounds(pool, body)


def window(eng, m, c):
    return eng.value_load(m.first[0:1, bass.ds(c, 1)], min_val=0, max_val=BLOCKS * P - 1)


def store_window(sp, m, s, c, slot, table, cols):
    first = window(sp, m, c)
    sp.wait_ge(s["kept"].sem, s["kept"].done(c))
    sp.dma_start(table[bass.ds(first, P), 0:cols], m.sums_out[:, slot, 0:cols]).then_inc(s["stored"], 16)
    hold(sp, s["stored"], 16 * c + 16)
    sp.sem_inc(s["store"].sem, 1)


def one_hot_of(nc, dve, m, s, c, k, wait):
    dve.wait_ge(s["summed"].sem, s["summed"].free(c))
    nc.vector.tensor_scalar(m.shift_mat[:, k % 2, :], m.step[:], m.shift_by[:, bass.ds(c, 1)], None, ALU.is_equal)
    nc.vector.tensor_tensor(m.one_hot[:, k % 2], m.iota_row[:, None, :].to_broadcast([P, TILES, P]),
                            m.dst_rel[:, bass.ds(c * TILES, TILES)][:, :, None].to_broadcast([P, TILES, P]),
                            ALU.is_equal).then_inc(s["onehot"].sem, 1)


def sum_tiles(nc, m, k, cols, tiles):
    for t in tiles:
        last = nc.tensor.matmul(m.ps[:, 6 + k % 2, 0:cols], m.one_hot[:, k % 2, t, :], m.ring[:, k, t, 0:cols],
                                start=(t == 0), stop=False)
    return last


def attention_edges(nc, m, a):
    stack, block, s = phase(nc, "attend", rows0=None, rows1=None, rows2=None, rows3=None, index=0, rows_used=SLOTS,
                            edges0=None, edges1=None, edge_mm=0, oht=0, right=2, kinds=1, masked=0, red=0, leaky=1,
                            xt=1, fwd=2, bwd=2, mt=1, drop=1, diff=1, expd=0, fb=1, fallen=2, weighed=0,
                            onehot=0, summed=2, scaled=2, kept=2, stored=None, store=2)
    featT = a["edge_attr_16"]
    mask = a["edge_attr_4"]
    ring_heads = [m.ring[:, k, :, 0:WIDE].rearrange("p t (h c) -> p t h c", c=HW) for k in range(SLOTS)]
    loads = 5

    def edge_loads(i, k):
        return 16 * loads * (i * 2 + k // 2 + 1)

    def next_chunk(i, k):
        return (i, k + 1) if k + 1 < SLOTS else (i + 1, 0)

    with stack:
        @block.gpsimd
        def _(pool):
            gather_chunks(nc, pool, m, s, ROW, m.table0)

        @block.sync
        def _(sp):
            def load(i, k):
                c = i * SLOTS + k
                slot = k % 2
                first = window(sp, m, c)
                sp.wait_ge(s["right"].sem, s["right"].free(c))
                sp.wait_ge(s["bwd"].sem, s["bwd"].free(c))
                sem = s[f"edges{slot}"]
                sp.dma_start(m.right[:, slot, :], m.right_dram[bass.ds(first, P)]).then_inc(sem, 16)
                sp.dma_start(m.e_featT[:, slot, :], featT[bass.ds(c, 1)].rearrange("o f e -> (o f) e")).then_inc(sem, 16)
                sp.dma_start(m.e_mask[:, slot, :], mask[bass.ds(c, 1)].rearrange("o p n -> (o p) n")).then_inc(sem, 16)
                sp.dma_start(m.dst_bc[:, slot, :], a["dst_edges"][bass.ds(c, 1)].to_broadcast([P, CHUNK])).then_inc(sem, 16)
                sp.dma_start(m.flags[:, slot, 0:CHUNK], m.flag_rows[bass.ds(c, 1)].to_broadcast([HEADS, CHUNK])).then_inc(sem, 16)

            def body(i, k, last):
                if not last:
                    load(*next_chunk(i, k))
                store_window(sp, m, s, i * SLOTS + k, k % 2, m.sums, SUMC)

            load(0, 0)
            rounds(sp, body)

        @block.tensor
        def _(pe):
            def scores(i, k):
                c = i * SLOTS + k
                slot = k % 2
                pe.wait_ge(s[f"edges{slot}"], edge_loads(i, k))
                pe.wait_ge(s["kinds"].sem, s["kinds"].free(c))
                for t in range(TILES):
                    nc.tensor.matmul(m.ps[:, 0, t * 32:(t + 1) * 32], m.e_featT[:, slot, t * P:(t + 1) * P],
                                     m.attn_edge[:].rearrange("f h t -> f (h t)"), start=(t == 0), stop=False)
                pe.wait_ge(s["oht"].sem, s["oht"].done(c))
                for t in range(TILES):
                    last = nc.tensor.matmul(m.ps[:, 0, t * 32:(t + 1) * 32], m.one_hotT[:, t * P:(t + 1) * P],
                                            m.right[:, slot, :], start=False, stop=(t == TILES - 1))
                last.then_inc(s["right"].sem, 1)

            def to_heads(i, k):
                c = i * SLOTS + k
                pe.wait_ge(s["leaky"].sem, s["leaky"].done(c))
                pe.wait_ge(s["fwd"].sem, s["fwd"].done(c - 1))
                for t in range(TILES):
                    last = nc.tensor.transpose(m.ps[0:HEADS, 1 + t // 4, (t % 4) * P:(t % 4 + 1) * P],
                                               m.score[:, t, :], m.ident[:])
                last.then_inc(s["xt"].sem, 1)

            def to_edges(i, k):
                c = i * SLOTS + k
                pe.wait_ge(s["diff"].sem, s["diff"].free(c))
                pe.wait_ge(s["fallen"].sem, s["fallen"].done(c - 1))
                hold(pe, s["drop"].sem, s["drop"].done(c))
                for t in range(TILES):
                    last = nc.tensor.transpose(m.ps[:, 3, t * HEADS:(t + 1) * HEADS],
                                               m.seg_max[:, t * P:(t + 1) * P], m.ident[0:HEADS, 0:HEADS])
                last.then_inc(s["mt"].sem, 1)
                nc.tensor.matmul(m.ps[:, 4, 0:HEADS], m.drop[:, 0:1].to_broadcast([HEADS, P]),
                                 m.ident[0:HEADS, 0:HEADS], start=True, stop=True).then_inc(s["fb"].sem, 1)

            def body(i, k, last):
                c = i * SLOTS + k
                if not last:
                    scores(*next_chunk(i, k))
                pe.wait_ge(s["weighed"].sem, s["weighed"].done(c))
                pe.wait_ge(s["onehot"].sem, s["onehot"].done(c))
                pe.wait_ge(s["kept"].sem, s["kept"].free(c))
                sum_tiles(nc, m, k, SUMC, range(0, 2))
                if not last:
                    to_heads(*next_chunk(i, k))
                sum_tiles(nc, m, k, SUMC, range(2, TILES)).then_inc(s["rows_used"].sem, 1)
                pe.wait_ge(s["scaled"].sem, s["scaled"].done(c - 1))
                nc.tensor.matmul(m.ps[:, 6 + k % 2, 0:SUMC], m.shift_mat[:, k % 2, :], m.carry[:],
                                 start=False, stop=True).then_inc(s["summed"].sem, 1)
                if not last:
                    to_edges(*next_chunk(i, k))

            scores(0, 0)
            to_heads(0, 0)
            to_edges(0, 0)
            rounds(pe, body)

        @block.vector
        def _(dve):
            def prepare(i, k):
                c = i * SLOTS + k
                slot = k % 2
                hold(dve, s[f"edges{slot}"], edge_loads(i, k))
                dve.wait_ge(s["right"].sem, s["right"].done(c - 1))
                nc.vector.tensor_scalar(m.one_hotT, m.dst_bc[:, slot, :], m.window_p[:, bass.ds(c, 1)], None,
                                        ALU.is_equal).then_inc(s["oht"].sem, 1)
                one_hot_of(nc, dve, m, s, c, k, None)
                dve.wait_ge(s["right"].sem, s["right"].done(c))
                dve.wait_ge(s[f"rows{k}"], 16 * TILES * (i + 1))
                nc.vector.tensor_tensor(m.kinds, m.ps[:, 0, 0:TILES * 32].rearrange("p (t c) -> p t c", c=32),
                                        m.ring[:, k, :, WIDE:ROW], ALU.add).then_inc(s["kinds"].sem, 1)
                dve.wait_ge(s["kinds"].sem, s["kinds"].done(c))
                kinds4 = m.kinds.rearrange("p t (h n) -> p t h n", n=KINDS)
                mask4 = m.e_mask[:, slot, :].rearrange("p (t n) -> p t n", n=KINDS)[:, :, None, :].to_broadcast([P, TILES, HEADS, KINDS])
                nc.vector.tensor_tensor(kinds4, kinds4, mask4, ALU.mult).then_inc(s["masked"].sem, 1)
                dve.wait_ge(s["masked"].sem, s["masked"].done(c))
                nc.vector.tensor_reduce(m.score0, kinds4, AX.X, ALU.add).then_inc(s["red"].sem, 1)
                dve.wait_ge(s["red"].sem, s["red"].done(c))
                nc.vector.scalar_tensor_tensor(m.score, m.score0, SLOPE, m.score0, ALU.mult, ALU.max).then_inc(s["leaky"].sem, 1)
                dve.wait_ge(s["xt"].sem, s["xt"].done(c))
                nc.vector.tensor_tensor_scan(m.run_max[:, slot, :], m.flags[:, slot, 0:CHUNK],
                                             m.ps[0:HEADS, 1:3, :].rearrange("p b n -> p (b n)")[:, 0:CHUNK],
                                             m.run_max[:, 1 - slot, CHUNK - 1:CHUNK], ALU.add, ALU.max).then_inc(s["fwd"].sem, 1)
                dve.wait_ge(s["fwd"].sem, s["fwd"].done(c))
                dve.wait_ge(s["mt"].sem, s["mt"].free(c))
                nc.vector.tensor_tensor_scan(m.seg_max[:, ::-1], m.flags[:, slot, 1:CHUNK + 1][:, ::-1], m.run_max[:, slot, ::-1],
                                             0.0, ALU.add, ALU.max).then_inc(s["bwd"].sem, 1)
                dve.wait_ge(s["bwd"].sem, s["bwd"].done(c))
                dve.wait_ge(s["fb"].sem, s["fb"].free(c))
                nc.vector.tensor_scalar(m.drop[:], m.run_max[:, 1 - slot, CHUNK - 1:CHUNK], m.seg_max[:, 0:1], 0.0,
                                        ALU.subtract, ALU.min).then_inc(s["drop"].sem, 1)

            def weigh(i, k):
                c = i * SLOTS + k
                dve.wait_ge(s["mt"].sem, s["mt"].done(c))
                nc.vector.tensor_tensor(m.diff, m.score, m.ps[:, 3, 0:TILES * HEADS].rearrange("p (t h) -> p t h", h=HEADS),
                                        ALU.subtract).then_inc(s["diff"].sem, 1)
                nc.vector.memset(m.ring[:, k, :, WIDE:SUMC], 1.0)
                dve.wait_ge(s["expd"].sem, s["expd"].done(c))
                nc.vector.tensor_tensor(ring_heads[k][:, :, :, 0:HD], ring_heads[k][:, :, :, 0:HD],
                                        ring_heads[k][:, :, :, HD:HW].to_broadcast([P, TILES, HEADS, HD]),
                                        ALU.mult).then_inc(s["weighed"].sem, 1)

            def rescale(i, k):
                c = i * SLOTS + k
                slot = k % 2
                dve.wait_ge(s["kept"].sem, s["kept"].done(c))
                dve.wait_ge(s["fallen"].sem, s["fallen"].done(c + 1))
                nc.vector.tensor_copy(m.carry[:, WIDE:SUMC], m.sums_out[:, slot, WIDE:SUMC])
                nc.vector.tensor_tensor(m.carry[:, 0:WIDE].rearrange("p (h c) -> p h c", c=HW),
                                        m.sums_out[:, slot, 0:WIDE].rearrange("p (h c) -> p h c", c=HW),
                                        m.fall[:, 1 - slot, :, None].to_broadcast([P, HEADS, HW]), ALU.mult).then_inc(s["scaled"].sem, 1)

            def body(i, k, last):
                if not last:
                    prepare(*next_chunk(i, k))
                    weigh(*next_chunk(i, k))
                    rescale(i, k)

            prepare(0, 0)
            weigh(0, 0)
            rounds(dve, body)

        @block.scalar
        def _(act):
            def weights(i, k):
                c = i * SLOTS + k
                act.wait_ge(s["diff"].sem, s["diff"].done(c))
                nc.scalar.activation(ring_heads[k][:, :, :, HD], m.diff, ACT.Exp, scale=1.0 / 3.0).then_inc(s["expd"].sem, 1)
                act.wait_ge(s["fb"].sem, s["fb"].done(c))
                act.wait_ge(s["scaled"].sem, s["scaled"].free(c))
                nc.scalar.activation(m.fall[:, k % 2, :], m.ps[:, 4, 0:HEADS], ACT.Exp, scale=1.0 / 3.0).then_inc(s["fallen"].sem, 1)

            def body(i, k, last):
                c = i * SLOTS + k
                act.wait_ge(s["summed"].sem, s["summed"].done(c))
                act.wait_ge(s["store"].sem, s["store"].free(c))
                act.wait_ge(s["scaled"].sem, s["scaled"].free(c))
                nc.scalar.activation(m.sums_out[:, k % 2, 0:SUMC], m.ps[:, 6 + k % 2, 0:SUMC], ACT.Copy).then_inc(s["kept"].sem, 1)
                if not last:
                    weights(*next_chunk(i, k))

            weights(0, 0)
            rounds(act, body)


def project_scalar(nc, act, m, s, g):
    act.wait_ge(s["trans"].sem, s["trans"].done(g))
    act.wait_ge(s["mm"].sem, s["mm"].free((g + 1) * GROUP - 1))
    copy_transposed(nc, m).then_inc(s["ht"].sem, 1)
    act.wait_ge(s["evac"].sem, s["evac"].done((g + 1) * GROUP - 1))
    nc.scalar.activation(m.msg, m.msg, ACT.Relu).then_inc(s["relu"].sem, 1)


def project_store(sp, m, s, g, table):
    sp.wait_ge(s["relu"].sem, s["relu"].done(g))
    group_dma(sp, table, g, m.msg, store=True).then_inc(s["stored"], 16)
    hold(sp, s["stored"], 16 * g + 16)
    sp.sem_inc(s["out_free"].sem, 1)


def project_tensor(nc, pe, m, s, l, g):
    pe.wait_ge(s["h"].sem, s["h"].done(g))
    transpose_group(nc, m, m.h).then_inc(s["trans"].sem, 1)
    pe.wait_ge(s["ht"].sem, s["ht"].done(g))
    for j in range(GROUP):
        pe.wait_ge(s["evac"].sem, s["evac"].free(g * GROUP + j) if j >= 4 else s["evac"].done(g * GROUP - 1))
        for k in range(2):
            last = nc.tensor.matmul(m.ps[:, 4 + j % 4, :], m.hT[:, j, k, :], m.w_pr[:, l, k, :], start=(k == 0), stop=(k == 1))
        last.then_inc(s["mm"].sem, 1)


def project_vector(nc, dve, m, s, l, g):
    dve.wait_ge(s["out_free"].sem, s["out_free"].free(g))
    for j in range(GROUP):
        dve.wait_ge(s["mm"].sem, s["mm"].done(g * GROUP + j))
        nc.vector.tensor_tensor(m.msg[:, j, :], m.ps[:, 4 + j % 4, 0:D], m.bias[:, l, 0:D], ALU.add)
        nc.vector.tensor_tensor(m.root[:, bass.ds(g * GROUP + j, 1), :].rearrange("p o c -> p (o c)"),
                                m.ps[:, 4 + j % 4, D:2 * D], m.bias[:, l, D:2 * D], ALU.add).then_inc(s["evac"].sem, 1)


def attention_nodes(nc, m, a):
    stack, block, s = phase(nc, "resid", x=None, x_free=1, kept=None, sum=0, recip=0, norm=1, deg=0, x1=0, ln_stats=0, ln_mv=0,
                            ln_sqrt=0, ln_rstd=0, ln_shift=0, h=1, trans=1, ht=1, mm=GROUP, evac=4, relu=0, stored=None, out_free=1)
    x_g, x1_g, sums_g = group_rows(a["x"]), group_rows(m.x1), group_rows(m.sums[0:BLOCKS * P])
    with stack:
        @block.sync
        def _(sp):
            with sp.Fori(0, GROUPS) as g:
                sp.wait_ge(s["x_free"].sem, s["x_free"].free(g))
                sp.wait_ge(s["h"].sem, s["h"].free(g))
                group_dma(sp, x_g, g, m.x_in[:]).then_inc(s["x"], 16)
                sp.wait_ge(s["norm"].sem, s["norm"].free(g))
                group_dma(sp, sums_g, g, m.sums_in).then_inc(s["x"], 16)
                sp.wait_ge(s["x1"].sem, s["x1"].done(g))
                group_dma(sp, x1_g, g, m.x_in[:], store=True).then_inc(s["kept"], 16)
                hold(sp, s["kept"], 16 * g + 16)
                sp.sem_inc(s["x_free"].sem, 1)
                project_store(sp, m, s, g, group_rows(m.tables[0]))

        @block.vector
        def _(dve):
            with dve.Fori(0, GROUPS) as g:
                dve.wait_ge(s["x"], 32 * g + 32)
                heads = m.sums_in[:, :, 0:WIDE].rearrange("p j (h c) -> p j h c", c=HW)
                nc.vector.tensor_scalar(m.degree[:], m.sums_in[:, :, WIDE], 1.0, None, ALU.max)
                nc.vector.tensor_scalar(m.weight[:], heads[:, :, :, HD], 1.0e-30, None, ALU.max).then_inc(s["sum"].sem, 1)
                dve.wait_ge(s["sum"].sem, s["sum"].done(g))
                nc.vector.reciprocal(m.inv_deg[:, bass.ds(g * GROUP, GROUP)], m.degree[:])
                nc.vector.reciprocal(m.weight[:], m.weight[:]).then_inc(s["recip"].sem, 1)
                dve.wait_ge(s["recip"].sem, s["recip"].done(g))
                nc.vector.tensor_tensor(m.o[:].rearrange("p j (h c) -> p j h c", c=HD), heads[:, :, :, 0:HD],
                                        m.weight[:, :, :, None].to_broadcast([P, GROUP, HEADS, HD]), ALU.mult).then_inc(s["norm"].sem, 1)
                dve.wait_ge(s["norm"].sem, s["norm"].done(g))
                nc.vector.tensor_tensor(m.x_in[:], m.x_in[:], m.o[:], ALU.add).then_inc(s["x1"].sem, 1)
                hold(dve, s["x1"].sem, s["x1"].done(g))
                ln_vector(nc, dve, m, s, m.x_in, g)
                project_vector(nc, dve, m, s, 0, g)

        @block.scalar
        def _(act):
            with act.Fori(0, GROUPS) as g:
                ln_scalar_sqrt(nc, act, m, s, g)
                ln_scalar_apply(nc, act, m, s, m.x_in, m.h, ACT.Relu, g)
                project_scalar(nc, act, m, s, g)

        @block.tensor
        def _(pe):
            with pe.Fori(0, GROUPS) as g:
                project_tensor(nc, pe, m, s, 0, g)


def sum_edges(nc, m, l):
    stack, block, s = phase(nc, f"edges{l}", rows0=None, rows1=None, rows2=None, rows3=None, index=0, rows_used=SLOTS,
                            onehot=0, summed=2, kept=2, stored=None, store=2)
    with stack:
        @block.gpsimd
        def _(pool):
            gather_chunks(nc, pool, m, s, D, m.tables[l])

        @block.sync
        def _(sp):
            rounds(sp, lambda i, k, last: store_window(sp, m, s, i * SLOTS + k, k % 2, m.agg_dram, D))

        @block.tensor
        def _(pe):
            def body(i, k, last):
                c = i * SLOTS + k
                pe.wait_ge(s[f"rows{k}"], 16 * TILES * (i + 1))
                pe.wait_ge(s["onehot"].sem, s["onehot"].done(c))
                pe.wait_ge(s["kept"].sem, s["kept"].free(c))
                sum_tiles(nc, m, k, D, range(TILES)).then_inc(s["rows_used"].sem, 1)
                pe.wait_ge(s["kept"].sem, s["kept"].done(c - 1))
                nc.tensor.matmul(m.ps[:, 6 + k % 2, 0:D], m.shift_mat[:, k % 2, :], m.sums_out[:, 1 - k % 2, 0:D],
                                 start=False, stop=True).then_inc(s["summed"].sem, 1)

            rounds(pe, body)

        @block.vector
        def _(dve):
            nc.vector.memset(m.sums_out[:, 1, :], 0.0)
            rounds(dve, lambda i, k, last: one_hot_of(nc, dve, m, s, i * SLOTS + k, k, None))

        @block.scalar
        def _(act):
            def body(i, k, last):
                c = i * SLOTS + k
                act.wait_ge(s["summed"].sem, s["summed"].done(c))
                act.wait_ge(s["store"].sem, s["store"].free(c))
                nc.scalar.activation(m.sums_out[:, k % 2, 0:D], m.ps[:, 6 + k % 2, 0:D], ACT.Copy).then_inc(s["kept"].sem, 1)

            rounds(act, body)


def layer_nodes(nc, m, a, l):
    final = l == LAYERS - 1
    own = (dict(x1=None, out=0, ln_stats=0, ln_mv=0, ln_sqrt=0, ln_rstd=0, ln_shift=0, aff=0, affb=0) if final
           else dict(ey=0, e1=0, er=1, trans=1, ht=1, mm=GROUP, evac=4, relu=0))
    stack, block, s = phase(nc, f"nodes{l}", agg=None, scaled=1, mtrans=1, mht=1, lmm=0, o=4, sq=0, ss=0, nsqrt=0, floor=0,
                            nrecip=0, y=0, h=1, stored=None, out_free=1, **own)
    x1_g, out_g, agg_g = group_rows(m.x1), group_rows(a["out"]), group_rows(m.agg_dram[0:BLOCKS * P])
    with stack:
        @block.sync
        def _(sp):
            with sp.Fori(0, GROUPS) as g:
                sp.wait_ge(s["scaled"].sem, s["scaled"].free(g))
                group_dma(sp, agg_g, g, m.sums_in[:, :, 0:D]).then_inc(s["agg"], 16)
                if final:
                    sp.wait_ge(s["out_free"].sem, s["out_free"].free(g))
                    group_dma(sp, x1_g, g, m.x_in[:]).then_inc(s["x1"], 16)
                    sp.wait_ge(s["out"].sem, s["out"].done(g))
                    group_dma(sp, out_g, g, m.x_in[:], store=True).then_inc(s["stored"], 16)
                    hold(sp, s["stored"], 16 * g + 16)
                    sp.sem_inc(s["out_free"].sem, 1)
                else:
                    project_store(sp, m, s, g, group_rows(m.tables[l + 1]))

        @block.vector
        def _(dve):
            with dve.Fori(0, GROUPS) as g:
                dve.wait_ge(s["agg"], 16 * g + 16)
                nc.vector.tensor_tensor(m.mean, m.sums_in[:, :, 0:D], m.inv_deg[:, bass.ds(g * GROUP, GROUP)][:, :, None].to_broadcast([P, GROUP, D]),
                                        ALU.mult).then_inc(s["scaled"].sem, 1)
                for j in range(GROUP):
                    dve.wait_ge(s["lmm"].sem, s["lmm"].done(g * GROUP + j))
                    nc.vector.tensor_tensor(m.o[:, j, :], m.ps[:, 4 + j % 4, 0:D],
                                            m.root[:, bass.ds(g * GROUP + j, 1), :].rearrange("p o c -> p (o c)"), ALU.add).then_inc(s["o"].sem, 1)
                dve.wait_ge(s["o"].sem, s["o"].done((g + 1) * GROUP - 1))
                nc.vector.tensor_tensor(m.h[:], m.o[:], m.o[:], ALU.mult).then_inc(s["sq"].sem, 1)
                dve.wait_ge(s["sq"].sem, s["sq"].done(g))
                nc.vector.tensor_reduce(m.norm2[:], m.h[:], AX.X, ALU.add).then_inc(s["ss"].sem, 1)
                dve.wait_ge(s["nsqrt"].sem, s["nsqrt"].done(g))
                nc.vector.tensor_scalar(m.norm[:], m.norm[:], NORM_EPS, None, ALU.max).then_inc(s["floor"].sem, 1)
                dve.wait_ge(s["floor"].sem, s["floor"].done(g))
                nc.vector.reciprocal(m.inv_norm[:], m.norm[:]).then_inc(s["nrecip"].sem, 1)
                dve.wait_ge(s["nrecip"].sem, s["nrecip"].done(g))
                nc.vector.tensor_tensor(m.o[:], m.o[:], m.inv_norm[:, :, None].to_broadcast([P, GROUP, D]), ALU.mult).then_inc(s["y"].sem, 1)
                if not final:
                    dve.wait_ge(s["ey"].sem, s["ey"].done(g))
                    nc.vector.tensor_scalar(m.ey, m.ey, 1.0, None, ALU.add).then_inc(s["e1"].sem, 1)
                    dve.wait_ge(s["e1"].sem, s["e1"].done(g))
                    nc.vector.reciprocal(m.ey, m.ey).then_inc(s["er"].sem, 1)
                    dve.wait_ge(s["er"].sem, s["er"].done(g))
                    nc.vector.tensor_tensor(m.h[:], m.o[:], m.ey, ALU.mult).then_inc(s["h"].sem, 1)
                    project_vector(nc, dve, m, s, l + 1, g)
                else:
                    hold(dve, s["y"].sem, s["y"].done(g))
                    ln_vector(nc, dve, m, s, m.o, g)
                    dve.wait_ge(s["h"].sem, s["h"].done(g))
                    nc.vector.tensor_tensor(m.h[:], m.h[:], m.ln_w[:, None, :].to_broadcast([P, GROUP, D]), ALU.mult).then_inc(s["aff"].sem, 1)
                    dve.wait_ge(s["aff"].sem, s["aff"].done(g))
                    nc.vector.tensor_tensor(m.h[:], m.h[:], m.ln_b[:, None, :].to_broadcast([P, GROUP, D]), ALU.add).then_inc(s["affb"].sem, 1)
                    dve.wait_ge(s["affb"].sem, s["affb"].done(g))
                    dve.wait_ge(s["x1"], 16 * g + 16)
                    nc.vector.tensor_tensor(m.x_in[:], m.x_in[:], m.h[:], ALU.add).then_inc(s["out"].sem, 1)

        @block.scalar
        def _(act):
            with act.Fori(0, GROUPS) as g:
                act.wait_ge(s["mtrans"].sem, s["mtrans"].done(g))
                copy_transposed(nc, m).then_inc(s["mht"].sem, 1)
                act.wait_ge(s["ss"].sem, s["ss"].done(g))
                nc.scalar.activation(m.norm[:], m.norm2[:], ACT.Sqrt).then_inc(s["nsqrt"].sem, 1)
                if not final:
                    act.wait_ge(s["y"].sem, s["y"].done(g))
                    nc.scalar.activation(m.ey, m.o[:], ACT.Exp, scale=-1.0).then_inc(s["ey"].sem, 1)
                    project_scalar(nc, act, m, s, g)
                else:
                    ln_scalar_sqrt(nc, act, m, s, g)
                    ln_scalar_apply(nc, act, m, s, m.o, m.h, ACT.Identity, g)

        @block.tensor
        def _(pe):
            with pe.Fori(0, GROUPS) as g:
                pe.wait_ge(s["scaled"].sem, s["scaled"].done(g))
                if final:
                    pe.wait_ge(s["mht"].sem, s["mht"].free(g))
                else:
                    pe.wait_ge(s["ht"].sem, s["ht"].free(g))
                transpose_group(nc, m, m.mean).then_inc(s["mtrans"].sem, 1)
                pe.wait_ge(s["mht"].sem, s["mht"].done(g))
                if not final:
                    pe.wait_ge(s["evac"].sem, s["evac"].done(g * GROUP - 1))
                for j in range(GROUP):
                    pe.wait_ge(s["o"].sem, s["o"].free(g * GROUP + j) if j >= 4 else s["o"].done(g * GROUP - 1))
                    for k in range(2):
                        last = nc.tensor.matmul(m.ps[:, 4 + j % 4, 0:D], m.hT[:, j, k, :], m.w_l[:, l, k, :], start=(k == 0), stop=(k == 1))
                    last.then_inc(s["lmm"].sem, 1)
                if not final:
                    pe.wait_ge(s["o"].sem, s["o"].done((g + 1) * GROUP - 1))
                    project_tensor(nc, pe, m, s, l + 1, g)


def any_tile(nc, m, a, name, cols, table, into, attend):
    stack, block, s = phase(nc, name, edges=None, edges_free=1, index=0, got=None, scores=0, sT=0, sTc=0, rowmax=0,
                            same=0, first=0, uniq=0, work=0, ready=0, put=None, summed=0, merged=0, expd=0)
    weigh = attend == "sum"
    tiles = CHUNKS * TILES
    steps = {"max": 9, "sum": 5, None: 1}[attend]
    with stack:
        @block.sync
        def _(sp):
            with sp.Fori(0, tiles) as t:
                sp.wait_ge(s["edges_free"].sem, s["edges_free"].free(t))
                sp.dma_start(m.g_dst_bc, m.dst_tiles[bass.ds(t, 1)].to_broadcast([P, P])).then_inc(s["edges"], 16)
                sp.dma_start(m.g_featT, a["feat_tiles"][bass.ds(t, 1)].rearrange("o f e -> (o f) e")).then_inc(s["edges"], 16)
                sp.dma_start(m.g_mask, a["mask_tiles"][bass.ds(t, 1)].rearrange("o p n -> (o p) n")).then_inc(s["edges"], 16)

        @block.gpsimd
        def _(pool):
            with pool.Fori(0, tiles) as t:
                hold(pool, s["uniq"].sem, s["uniq"].done(t))
                pool.indirect_dma_start(m.g_rows[:, 0:cols], None, table,
                                        bass.IndirectOffsetOnAxis(ap=m.g_src, axis=0)).then_inc(s["got"], 16)
                if attend == "max":
                    pool.indirect_dma_start(m.g_right, None, m.right_dram,
                                            bass.IndirectOffsetOnAxis(ap=m.g_dst, axis=0)).then_inc(s["got"], 16)
                if attend == "sum":
                    pool.indirect_dma_start(m.g_max, None, m.max_dram,
                                            bass.IndirectOffsetOnAxis(ap=m.g_dst, axis=0)).then_inc(s["got"], 16)
                width = HEADS if attend == "max" else SUMC if weigh else D
                pool.indirect_dma_start(m.g_old[:, 0:width], None, into,
                                        bass.IndirectOffsetOnAxis(ap=m.g_dst, axis=0)).then_inc(s["got"], 16)
                hold(pool, s["merged"].sem, s["merged"].done(t))
                pool.indirect_dma_start(into, bass.IndirectOffsetOnAxis(ap=m.g_once, axis=0), m.g_old[:, 0:width], None,
                                        bounds_check=TABLE - 1, oob_is_err=False).then_inc(s["put"], 16)
                hold(pool, s["put"], 16 * t + 16)
                pool.sem_inc(s["edges_free"].sem, 1)

        @block.tensor
        def _(pe):
            with pe.Fori(0, tiles) as t:
                if attend == "max":
                    pe.wait_ge(s["edges"], 48 * t + 48)
                    nc.tensor.matmul(m.ps[:, 0, 0:32], m.g_featT, m.attn_edge[:].rearrange("f h t -> f (h t)"),
                                     start=True, stop=True).then_inc(s["scores"].sem, 1)
                    pe.wait_ge(s["ready"].sem, s["ready"].done(t))
                    nc.tensor.transpose(m.ps[0:HEADS, 1, 0:P], m.g_score, m.ident[:]).then_inc(s["sT"].sem, 1)
                    pe.wait_ge(s["sTc"].sem, s["sTc"].done(t))
                    for h in range(HEADS):
                        last = nc.tensor.matmul(m.ps[:, 2 + h // 4, (h % 4) * P:(h % 4 + 1) * P],
                                                m.ident[0:HEADS, h:h + 1].to_broadcast([HEADS, P]), m.g_scoreT,
                                                start=True, stop=True)
                    last.then_inc(s["rowmax"].sem, 1)
                else:
                    pe.wait_ge(s["ready"].sem, s["ready"].done(t))
                    width = SUMC if weigh else D
                    nc.tensor.matmul(m.ps[:, 0, 0:width], m.g_same, m.g_rows[:, 0:width],
                                     start=True, stop=True).then_inc(s["summed"].sem, 1)

        @block.vector
        def _(dve):
            with dve.Fori(0, tiles) as t:
                n = [0]

                def link(ins):
                    n[0] += 1
                    ins.then_inc(s["work"].sem, 1)
                    dve.wait_ge(s["work"].sem, total * t + n[0])

                total = {"max": 13, "sum": 10, None: 7}[attend]
                dve.wait_ge(s["edges"], 48 * t + 48)
                nc.vector.tensor_copy(m.g_src, m.src[:, bass.ds(t, 1)])
                link(nc.vector.tensor_copy(m.g_dst, m.dst_all[:, bass.ds(t, 1)]))
                link(nc.vector.tensor_copy(m.g_dstf, m.g_dst))
                link(nc.vector.tensor_scalar(m.g_same, m.g_dst_bc, m.g_dstf, None, ALU.is_equal))
                link(nc.vector.scalar_tensor_tensor(m.g_masked, m.step[:], 0.0, m.g_same, ALU.is_gt, ALU.mult))
                link(nc.vector.tensor_reduce(m.g_dups, m.g_masked, AX.X, ALU.add))
                link(nc.vector.tensor_scalar(m.g_dups, m.g_dups, float(TABLE), None, ALU.mult))
                link(nc.vector.tensor_tensor(m.g_dups, m.g_dups, m.g_dstf, ALU.add))
                nc.vector.tensor_copy(m.g_once, m.g_dups).then_inc(s["uniq"].sem, 1)
                gets = 32 if attend is None else 48
                dve.wait_ge(s["got"], gets * t + gets)
                if attend == "max":
                    dve.wait_ge(s["scores"].sem, s["scores"].done(t))
                    kinds = m.g_kinds
                    link(nc.vector.tensor_tensor(kinds, m.ps[:, 0, 0:32], m.g_rows[:, WIDE:ROW], ALU.add))
                    link(nc.vector.tensor_tensor(kinds, kinds, m.g_right, ALU.add))
                    kinds3 = kinds.rearrange("p (h n) -> p h n", n=KINDS)
                    link(nc.vector.tensor_tensor(kinds3, kinds3, m.g_mask[:, None, :].to_broadcast([P, HEADS, KINDS]), ALU.mult))
                    link(nc.vector.tensor_reduce(m.g_score0, kinds3, AX.X, ALU.add))
                    nc.vector.scalar_tensor_tensor(m.g_score, m.g_score0, SLOPE, m.g_score0, ALU.mult, ALU.max).then_inc(s["ready"].sem, 1)
                    dve.wait_ge(s["ready"].sem, s["ready"].done(t))
                    nc.vector.tensor_copy(m.g_scores[:, bass.ds(t, 1), :].rearrange("p o h -> p (o h)"), m.g_score)
                    dve.wait_ge(s["sT"].sem, s["sT"].done(t))
                    nc.vector.tensor_copy(m.g_scoreT, m.ps[0:HEADS, 1, 0:P]).then_inc(s["sTc"].sem, 1)
                    link(nc.vector.tensor_scalar(m.g_masked, m.g_same, FAR, -FAR, ALU.mult, ALU.add))
                    dve.wait_ge(s["rowmax"].sem, s["rowmax"].done(t))
                    wide = m.ps[:, 2:4, :].rearrange("p b n -> p (b n)").rearrange("p (h e) -> p h e", h=HEADS)
                    nc.vector.tensor_tensor(m.g_wide, wide, m.g_masked[:, None, :].to_broadcast([P, HEADS, P]), ALU.add).then_inc(s["same"].sem, 1)
                    dve.wait_ge(s["same"].sem, s["same"].done(t))
                    link(nc.vector.tensor_reduce(m.g_score0, m.g_wide, AX.X, ALU.max))
                    nc.vector.tensor_tensor(m.g_old[:, 0:HEADS], m.g_old[:, 0:HEADS], m.g_score0, ALU.max).then_inc(s["merged"].sem, 1)
                else:
                    if weigh:
                        link(nc.vector.tensor_tensor(m.g_score0, m.g_scores[:, bass.ds(t, 1), :].rearrange("p o h -> p (o h)"),
                                                     m.g_max, ALU.subtract))
                        nc.vector.memset(m.g_rows[:, WIDE:SUMC], 1.0)
                        link(nc.vector.tensor_copy(m.g_score, m.g_score0))
                        nc.vector.memset(m.g_kinds, 0.0).then_inc(s["first"].sem, 1)
                        dve.wait_ge(s["expd"].sem, s["expd"].done(t))
                        heads = m.g_rows[:, 0:WIDE].rearrange("p (h c) -> p h c", c=HW)
                        link(nc.vector.tensor_tensor(heads[:, :, 0:HD], heads[:, :, 0:HD],
                                                     heads[:, :, HD:HW].to_broadcast([P, HEADS, HD]), ALU.mult))
                    nc.vector.memset(m.g_kinds, 0.0).then_inc(s["ready"].sem, 1)
                    dve.wait_ge(s["summed"].sem, s["summed"].done(t))
                    width = SUMC if weigh else D
                    nc.vector.tensor_tensor(m.g_old[:, 0:width], m.g_old[:, 0:width], m.ps[:, 0, 0:width], ALU.add).then_inc(s["merged"].sem, 1)
                hold(dve, s["edges_free"].sem, s["edges_free"].done(t))

        if weigh:
            @block.scalar
            def _(act):
                with act.Fori(0, tiles) as t:
                    act.wait_ge(s["first"].sem, s["first"].done(t))
                    nc.scalar.activation(m.g_rows[:, 0:WIDE].rearrange("p (h c) -> p h c", c=HW)[:, :, HD],
                                         m.g_score, ACT.Exp, scale=1.0 / 3.0).then_inc(s["expd"].sem, 1)


def load_destinations(nc, m, a):
    stack, block, s = phase(nc, "dests", loaded=None)
    with stack:
        @block.sync
        def _(sp):
            sp.dma_start(m.dst_all, a["dst"]).then_inc(s["loaded"], 16)
            sp.wait_ge(s["loaded"], 16)


def any_start(nc, m, a, table, cols, value):
    stack, block, s = phase(nc, "fill", filled=0, stored=None)
    with stack:
        @block.vector
        def _(dve):
            nc.vector.memset(m.g_old[:, 0:cols], value).then_inc(s["filled"].sem, 1)

        @block.sync
        def _(sp):
            sp.wait_ge(s["filled"].sem, 1)
            for b in range(BLOCKS + 1):
                sp.dma_start(table[b * P:(b + 1) * P], m.g_old[:, 0:cols]).then_inc(s["stored"], 16)
            sp.wait_ge(s["stored"], 16 * (BLOCKS + 1))


def build(nc, a):
    m = Mem()

    def dram(name, *shape):
        return nc.dram_tensor(name, shape, fp32, kind="Internal").ap()

    m.table0 = dram("attention_table", BLOCKS * P, ROW)
    m.right_dram = dram("right_scores", TABLE, HEADS * KINDS)
    m.sums = dram("attention_sums", TABLE, SUMC)
    m.agg_dram = dram("message_sums", TABLE, D)
    m.tables = [dram(f"message_table{l}", BLOCKS * P, D) for l in range(LAYERS)]
    m.x1 = dram("x_after_attention", BLOCKS * P, D)
    m.max_dram = dram("score_maxima", TABLE, HEADS)
    m.flag_dram = dram("run_flags", CHUNKS * CHUNK)
    m.dst_tiles = a["dst_edges"].rearrange("c (t e) -> (c t) e", e=P)
    m.flag_rows = m.flag_dram.rearrange("(c n) -> c n", n=CHUNK)
    with ExitStack() as ctx:
        def sb(name, shape, dt=fp32):
            return ctx.enter_context(nc.sbuf_tensor(name, shape, dt))

        m.iota_row = sb("iota_row", [P, P])
        m.iota_p = sb("iota_p", [P, 1])
        m.step = sb("step", [P, P])
        m.ident = sb("ident", [P, P])
        m.eps_ln = sb("eps_ln", [P, 1])
        m.ones = sb("ones", [P, 1])
        m.odd = sb("odd", [P, 1])
        m.irregular = sb("irregular", [1, 1], int32)
        m.w_node = sb("w_node", [P, 2, D + 64])
        m.attn_diag = sb("attn_diag", [P, 2, 64])
        m.attn_edge = sb("attn_edge", [FEATS, HEADS, KINDS])
        m.w_pr = sb("w_pr", [P, LAYERS, 2, 2 * D])
        m.w_l = sb("w_l", [P, LAYERS, 2, D])
        m.bias = sb("bias", [P, LAYERS, 2 * D])
        m.ln_w = sb("ln_w", [P, D])
        m.ln_b = sb("ln_b", [P, D])
        m.src = sb("src_index", [P, CHUNKS * TILES], int32)
        m.dst_rel = sb("dst_rel", [P, CHUNKS * TILES])
        m.first = sb("chunk_first", [1, CHUNKS], int32)
        m.window_p = sb("window_p", [P, CHUNKS])
        m.shift_by = sb("shift_by", [P, CHUNKS])
        m.inv_deg = sb("inv_deg", [P, BLOCKS])
        m.root = sb("root", [P, BLOCKS, D])
        m.index = sb("index", [P, 2, 2 * TILES], int32)
        m.one_hot = sb("one_hot", [P, 2, TILES, P])
        m.shift_mat = sb("shift_mat", [P, 2, P])
        m.sums_out_t = sb("sums_out", [P, 2, SUMC])
        m.sums_out = m.sums_out_t[:]
        m.carry = sb("carry", [P, SUMC])
        m.fall = sb("fall", [P, 2, HEADS])
        m.drop = sb("drop", [HEADS, 1])
        m.x_in = sb("x_in", [P, GROUP, D])
        m.h = sb("h", [P, GROUP, D])
        m.o = sb("o", [P, GROUP, D])
        m.bn = sb("bn", [P, GROUP, 6])
        m.mv = sb("mv", [P, GROUP, 2])
        m.std = sb("std", [P, GROUP])
        m.rstd = sb("rstd", [P, GROUP])
        m.shift = sb("shift", [P, GROUP])
        m.norm2 = sb("norm2", [P, GROUP])
        m.norm = sb("norm", [P, GROUP])
        m.inv_norm = sb("inv_norm", [P, GROUP])
        m.degree = sb("degree", [P, GROUP])
        m.weight = sb("weight", [P, GROUP, HEADS])
        ring_cols = SLOTS * TILES * ROW
        ring = sb("ring", [P, ring_cols])
        m.ring = ring[:].rearrange("p (k t c) -> p k t c", k=SLOTS, t=TILES)
        size = GROUP * D
        assert ring_cols >= 3 * size + GROUP * ROW
        m.msg = ring[:, 0:size].rearrange("p (j c) -> p j c", c=D)
        m.mean = ring[:, size:2 * size].rearrange("p (j c) -> p j c", c=D)
        m.ey = m.mean
        m.hT = ring[:, 2 * size:3 * size].rearrange("p (j k n) -> p j k n", j=GROUP, k=2)
        m.sums_in = ring[:, 3 * size:3 * size + GROUP * SUMC].rearrange("p (j c) -> p j c", c=SUMC)
        m.table_rows = ring[:, 3 * size:3 * size + GROUP * ROW].rearrange("p (j c) -> p j c", c=ROW)
        m.right_rows = ring[:, 0:GROUP * 32].rearrange("p (j c) -> p j c", c=32)
        at = [0]

        def part(space, cols, dt=fp32):
            view = space[:, at[0]:at[0] + cols]
            at[0] += cols
            return view if dt is fp32 else view.bitcast(dt)

        m.w_nodeT = part(ring, 2 * D).rearrange("p (j n) -> p j n", j=2)
        m.dst = part(ring, CHUNKS * TILES, int32)
        m.lin_a = part(ring, CHUNKS * TILES, int32)
        m.lin_b = part(ring, CHUNKS * TILES, int32)
        m.lin_f = part(ring, CHUNKS * TILES)
        m.first_all = part(ring, CHUNKS, int32)
        m.first_f = part(ring, CHUNKS)
        m.zeros = part(ring, GROUP * SUMC)
        m.last_all = part(ring, CHUNKS, int32)
        m.odd_all = part(ring, CHUNKS * TILES + CHUNKS)
        m.odd_line, m.odd_span = m.odd_all[:, 0:CHUNKS * TILES], m.odd_all[:, CHUNKS * TILES:]
        work = sb("attention_work", [P, CHUNK * 10 + 2 + TILES * 32 * 2 + 64 + TILES * 3 * HEADS])
        at[0] = 0
        m.one_hotT = part(work, CHUNK)
        m.dst_bc = part(work, 2 * CHUNK, int32).rearrange("p (k e) -> p k e", k=2)
        m.e_featT = part(work, 2 * CHUNK)[0:FEATS].rearrange("p (k e) -> p k e", k=2)
        m.run_max = part(work, 2 * CHUNK)[0:HEADS].rearrange("p (k e) -> p k e", k=2)
        m.seg_max = part(work, CHUNK)[0:HEADS]
        m.flags = part(work, 2 * (CHUNK + 1))[0:HEADS].rearrange("p (k e) -> p k e", k=2)
        m.e_mask = part(work, 2 * TILES * KINDS).rearrange("p (k e) -> p k e", k=2)
        m.right = part(work, 2 * HEADS * KINDS).rearrange("p (k e) -> p k e", k=2)
        m.kinds = part(work, TILES * 32).rearrange("p (t c) -> p t c", t=TILES)
        m.score0 = part(work, TILES * HEADS).rearrange("p (t c) -> p t c", t=TILES)
        m.score = part(work, TILES * HEADS).rearrange("p (t c) -> p t c", t=TILES)
        m.diff = part(work, TILES * HEADS).rearrange("p (t c) -> p t c", t=TILES)
        at[0] = 0
        m.g_scores = m.root[:].rearrange("p b c -> p (b c)")[:, 0:CHUNKS * TILES * HEADS].rearrange("p (t h) -> p t h", h=HEADS)
        m.g_rows, m.g_old = part(work, ROW), part(work, SUMC)
        m.g_same, m.g_masked = part(work, P), part(work, P)
        m.g_dst_bc = part(work, P, int32)
        m.g_featT = part(work, P)[0:FEATS]
        m.g_scoreT = part(work, P)[0:HEADS]
        m.g_wide = part(work, HEADS * P).rearrange("p (h e) -> p h e", h=HEADS)
        m.g_mask, m.g_right, m.g_kinds = part(work, KINDS), part(work, 32), part(work, 32)
        m.g_score0, m.g_score, m.g_max = part(work, HEADS), part(work, HEADS), part(work, HEADS)
        m.g_src, m.g_dst, m.g_once = part(work, 1, int32), part(work, 1, int32), part(work, 1, int32)
        m.g_dstf, m.g_dups = part(work, 1), part(work, 1)
        m.dst_all = part(work, CHUNKS * TILES, int32)
        m.ps = ctx.enter_context(nc.psum_tensor("ps", [P, 8, 512], fp32))

        setup(nc, m, a)
        node_features(nc, m, a)
        irregular = nc.values_load(m.irregular[0:1, 0:1], min_val=0, max_val=CHUNKS * (CHUNK + P))
        with nc.If(irregular < 1):
            attention_edges(nc, m, a)
            attention_nodes(nc, m, a)
            for l in range(LAYERS):
                sum_edges(nc, m, l)
                layer_nodes(nc, m, a, l)
        with nc.Else():
            load_destinations(nc, m, a)
            any_start(nc, m, a, m.max_dram, HEADS, -FAR)
            any_tile(nc, m, a, "anymax", ROW, m.table0, m.max_dram, "max")
            any_tile(nc, m, a, "anysum", ROW, m.table0, m.sums, "sum")
            attention_nodes(nc, m, a)
            for l in range(LAYERS):
                any_start(nc, m, a, m.agg_dram, D, 0.0)
                load_destinations(nc, m, a)
                any_tile(nc, m, a, f"any{l}", D, m.tables[l], m.agg_dram, None)
                layer_nodes(nc, m, a, l)


def kernel(**inputs):
    import concourse.bacc as _bacc
    from concourse import mybir as _mybir
    from concourse.bass_utils import run_bass_kernel_spmd as _run

    rows = CHUNKS * CHUNK

    def padded(x, n, fill):
        x = np.asarray(x)
        out = np.full((n,) + x.shape[1:], fill, x.dtype)
        out[:x.shape[0]] = x
        return out

    arrays = {}
    for name, value in inputs.items():
        value = np.asarray(value)
        if name == "x":
            arrays[name] = padded(value, BLOCKS * P, 0)
        elif name == "src":
            arrays[name] = padded(value, rows, 0).reshape(-1, P).T
        elif name == "dst":
            line = padded(value, rows, BLOCKS * P - 1)
            before = np.concatenate([np.full(1, -1, line.dtype), line[:-1]])
            arrays["dst_line"] = line.reshape(P, -1)
            arrays["dst_line_before"] = before.reshape(P, -1)
            arrays["dst_edges"] = line.reshape(CHUNKS, CHUNK)
            arrays["chunk_first"] = line[0::CHUNK].reshape(1, CHUNKS)
            arrays["chunk_last"] = line[CHUNK - 1::CHUNK].reshape(1, CHUNKS)
            arrays["dst"] = line.reshape(-1, P).T
        elif name == "edge_attr_16":
            arrays[name] = padded(value, rows, 0).reshape(CHUNKS, CHUNK, FEATS).transpose(0, 2, 1)
            arrays["feat_tiles"] = padded(value, rows, 0).reshape(-1, P, FEATS).transpose(0, 2, 1)
        elif name == "edge_attr_4":
            arrays[name] = padded(value, rows, 0).reshape(CHUNKS, TILES, P, KINDS).transpose(0, 2, 1, 3).reshape(CHUNKS, P, TILES * KINDS)
            arrays["mask_tiles"] = padded(value, rows, 0).reshape(-1, P, KINDS)
        else:
            arrays[name] = value
    arrays = {f"in_{k}": np.ascontiguousarray(v) for k, v in arrays.items()}

    nc = _bacc.Bacc("TRN2", target_bir_lowering=False, num_devices=1)
    a = {k[3:]: nc.dram_tensor(k, v.shape, _mybir.dt.from_np(v.dtype), kind="ExternalInput").ap() for k, v in arrays.items()}
    a["out"] = nc.dram_tensor("out", (BLOCKS * P, D), _mybir.dt.float32, kind="ExternalOutput").ap()
    build(nc, a)
    r = _run(nc, [arrays], core_ids=[0])
    return r.results[0]["out"][:N]
```

```python
import numpy as np
import concourse.bass as bass
from concourse import mybir
from contextlib import ExitStack
from itertools import count

fp32 = mybir.dt.float32
int32 = mybir.dt.int32
ALU = mybir.AluOpType
ACT = mybir.ActivationFunctionType
AX = mybir.AxisListType

P = 128
N, E, D = 6250, 100000, 256
HEADS, HD, KINDS, FEATS = 8, 32, 4, 16
LAYERS = 3
BLOCKS = -(-N // P)
TILES = 7
CHUNK = TILES * P
CHUNKS = -(-E // CHUNK)
SLOTS = 4
ROUNDS = CHUNKS // SLOTS
assert CHUNKS == ROUNDS * SLOTS and ROUNDS % 2 == 0
TABLE = BLOCKS * P + P
FALL = 128
BEFORE = 2
SUPER = 16
SUPERS = CHUNKS // SUPER
GROUP = 7
DELAY = 2
STARTS = [SUPER * q // GROUP for q in range(GROUP)]
GROUPS = BLOCKS // GROUP
assert BLOCKS == GROUP * GROUPS and CHUNKS == SUPER * SUPERS and SUPERS == GROUPS
HW = HD + 1
WIDE = HEADS * HW
ROW = WIDE + HEADS * KINDS
SUMC = WIDE + 1
FAR = 1.0e30
LN_EPS = 1e-5
NORM_EPS = 1e-12
SLOPE = 0.2


PHASE_NUMBERS = count()


class Mem:
    pass


class Count:

    def __init__(self, sem, buffers):
        self.sem, self.buffers = sem, buffers

    def done(self, n):
        return self.buffers + n + 1

    def free(self, n):
        return n + 1


def phase(nc, name, **sems):
    stack = ExitStack()
    made = Mem()
    made.of = {}
    name = f"{name}{next(PHASE_NUMBERS)}"
    for key, buffers in sems.items():
        sem = nc.alloc_semaphore(f"{name}_{key}")
        made.of[key] = sem if buffers is None else Count(sem, buffers)
        if buffers:
            nc.gpsimd.sem_inc(sem, buffers)
    handles = [c.sem if isinstance(c, Count) else c for c in made.of.values()]

    def clear():
        nc.clear_and_free_semaphores(handles)
        nc.all_engine_barrier()

    stack.callback(clear)
    nc.all_engine_barrier()
    return stack, stack.enter_context(nc.Block()), made.of


def hold(eng, sem, value):
    eng.wait_ge(sem, value)
    eng.nop(nofuse=True)


def group_rows(ap):
    return ap.rearrange("(g j p) d -> g p j d", p=P, j=GROUP)


def rounds(eng, body):
    with eng.Fori(0, ROUNDS - 1) as i:
        for k in range(SLOTS):
            body(i, k, SLOTS)
    for k in range(SLOTS):
        body(ROUNDS - 1, k, SLOTS - 1 - k)


def setup(nc, m, a):
    stack, block, s = phase(nc, "setup", zeroed=0, iota=0, loaded=None, tr_w=0, wt_done=0, fold=0, done_v=0, dv=0, conv=0,
                            zrows=0, zstored=None, flag=0, flag_far=0, fstored=None,
                            odd=0, odd_sum=0, odd_max=0)
    with stack:
        @block.gpsimd
        def _(pool):
            nc.gpsimd.iota(m.iota_row[:], [[1, P]], base=0, channel_multiplier=0,
                           allow_small_or_imprecise_dtypes=True)
            nc.gpsimd.iota(m.iota_p[:], [[0, 1]], base=0, channel_multiplier=1,
                           allow_small_or_imprecise_dtypes=True)
            nc.gpsimd.iota(m.step[:], [[-1, P]], base=0, channel_multiplier=1,
                           allow_small_or_imprecise_dtypes=True).then_inc(s["iota"].sem, 1)

        @block.sync
        def _(sp):
            def load(out, in_):
                sp.dma_start(out, in_).then_inc(s["loaded"], 16)

            load(m.w_node[:, :, 0:D], a["L0_gnn_W_n"].rearrange("(k p) n -> p k n", p=P))
            sp.wait_ge(s["zeroed"].sem, 1)
            for t in range(TILES):
                load(m.attn_edge[t * FEATS:(t + 1) * FEATS, t, :].rearrange("f (h n) -> f h n", n=KINDS),
                     a["L0_gnn_attn_m"].rearrange("h f t -> f h t"))
            for l in range(LAYERS):
                for half, w in ((0, f"L1_gnn_pW{l}"), (1, f"L1_gnn_rW{l}")):
                    load(m.w_pr[:, l, :, half * D:(half + 1) * D], a[w].rearrange("(k p) n -> p k n", p=P))
                for half, w in ((0, f"L1_gnn_pb{l}"), (1, f"L1_gnn_lb{l}")):
                    load(m.bias[:, l, half * D:(half + 1) * D], a[w][None, :].to_broadcast([P, D]))
                load(m.w_l[:, l], a[f"L1_gnn_lW{l}"].rearrange("(k p) n -> p k n", p=P))
            load(m.ln_w[:], a["L1_gnn_ln_w"][None, :].to_broadcast([P, D]))
            load(m.ln_b[:], a["L1_gnn_ln_b"][None, :].to_broadcast([P, D]))
            sp.wait_ge(s["zrows"].sem, 1)
            for table, row in ((m.sums, SUMC), (m.agg_dram, D)):
                for b in range(0, BLOCKS + 1, GROUP):
                    n = min(GROUP, BLOCKS + 1 - b)
                    sp.dma_start(table[b * P:(b + n) * P].rearrange("(j p) d -> p j d", p=P),
                                 m.zeros[:, 0:n * row].rearrange("p (j d) -> p j d", d=row)).then_inc(s["zstored"], 16)
            sp.dma_start(m.right_dram[BLOCKS * P:TABLE], m.zeros[:, 0:HEADS * KINDS]).then_inc(s["zstored"], 16)
            sp.wait_ge(s["flag_far"].sem, 1)
            sp.dma_start(m.flag_dram.rearrange("(p n) -> p n", p=P), m.lin_f).then_inc(s["fstored"], 16)
            sp.wait_ge(s["fstored"], 16)
            sp.wait_ge(s["zstored"], 16 * (2 * -(-(BLOCKS + 1) // GROUP) + 1))

        @block.scalar
        def _(act):
            def load(out, in_):
                act.dma_start(out, in_).then_inc(s["loaded"], 16)

            load(m.src[:], a["src"])
            load(m.dst, a["dst"])
            load(m.lin_a, a["dst_line"])
            load(m.lin_b, a["dst_line_before"])
            load(m.first[:], a["chunk_first"])
            load(m.last_all, a["chunk_last"].to_broadcast([P, CHUNKS]))
            load(m.first_all, a["chunk_first"].to_broadcast([P, CHUNKS]))
            load(m.floor_all, a["chunk_floor"].to_broadcast([P, CHUNKS]))
            act.wait_ge(s["zeroed"].sem, 1)
            for side, w in ((0, "L0_gnn_attn_l"), (1, "L0_gnn_attn_r")):
                for h in range(HEADS):
                    at = (h % 4) * HD
                    col = side * HEADS * KINDS + h * KINDS
                    load(m.attn_diag[at:at + HD, h // 4, col:col + KINDS], a[w][h])

        loads = 16 * (1 + TILES + 5 * LAYERS + 2 + 8 + 2 * HEADS)

        @block.vector
        def _(dve):
            nc.vector.memset(m.attn_edge[:], 0.0)
            nc.vector.memset(m.attn_diag[:], 0.0).then_inc(s["zeroed"].sem, 1)
            nc.vector.memset(m.zeros, 0.0).then_inc(s["zrows"].sem, 1)
            nc.vector.memset(m.eps_ln[:], LN_EPS)
            nc.vector.memset(m.ones[:], 1.0)
            nc.vector.memset(m.flags, -FAR)
            nc.vector.memset(m.run_max, 0.0)
            nc.vector.memset(m.carry[:], 0.0)
            nc.vector.memset(m.sums_out, 0.0).then_inc(s["dv"].sem, 1)
            dve.wait_ge(s["iota"].sem, 1)
            nc.vector.tensor_scalar(m.ident[:], m.step[:], 0.0, None, ALU.is_equal).then_inc(s["dv"].sem, 1)
            dve.wait_ge(s["loaded"], loads)
            nc.vector.tensor_copy(m.first_f, m.first_all).then_inc(s["conv"].sem, 1)
            dve.wait_ge(s["conv"].sem, 1)
            nc.vector.tensor_scalar(m.window_p[:], m.first_f, m.iota_p[:, 0:1], None, ALU.add)
            nc.vector.memset(m.shift_by[:], 0.0).then_inc(s["conv"].sem, 1)
            dve.wait_ge(s["conv"].sem, 2)
            nc.vector.tensor_tensor(m.shift_by[:, 1:CHUNKS], m.first_f[:, 1:CHUNKS], m.first_f[:, 0:CHUNKS - 1], ALU.subtract)
            nc.vector.tensor_tensor(m.dst_rel[:].rearrange("p (c t) -> p c t", t=TILES),
                                    m.dst.rearrange("p (c t) -> p c t", t=TILES),
                                    m.first_f[:, :, None].to_broadcast([P, CHUNKS, TILES]), ALU.subtract)
            nc.vector.tensor_tensor(m.lin_f, m.lin_a, m.lin_b, ALU.not_equal).then_inc(s["flag"].sem, 1)
            dve.wait_ge(s["flag"].sem, 1)
            nc.vector.tensor_scalar(m.lin_f, m.lin_f, -FAR, None, ALU.mult).then_inc(s["flag_far"].sem, 1)
            nc.vector.tensor_tensor(m.odd_line, m.lin_a, m.lin_b, ALU.is_lt)
            nc.vector.tensor_tensor(m.odd_floor, m.first_all, m.floor_all, ALU.is_lt)
            nc.vector.tensor_scalar(m.odd_span, m.first_all, float(P), None, ALU.add).then_inc(s["odd"].sem, 1)
            dve.wait_ge(s["odd"].sem, 1)
            nc.vector.tensor_tensor(m.odd_span, m.last_all, m.odd_span, ALU.is_ge).then_inc(s["odd"].sem, 1)
            dve.wait_ge(s["odd"].sem, 2)
            nc.vector.tensor_reduce(m.odd[:], m.odd_all, AX.X, ALU.add).then_inc(s["odd"].sem, 1)
            dve.wait_ge(s["tr_w"].sem, 1)
            for j in range(2):
                last = nc.vector.tensor_copy(m.w_nodeT[:, j, :], m.ps[:, j, 0:D])
            last.then_inc(s["wt_done"].sem, 1)
            dve.wait_ge(s["fold"].sem, 1)
            nc.vector.tensor_copy(m.w_node[:, :, D:D + 2 * HEADS * KINDS],
                                  m.ps[:, 2:4, 0:2 * HEADS * KINDS]).then_inc(s["done_v"].sem, 1)
            dve.wait_ge(s["odd_sum"].sem, 1)
            nc.vector.tensor_copy(m.irregular[:], m.ps[0:1, 4, 0:1]).then_inc(s["done_v"].sem, 1)
            dve.wait_ge(s["done_v"].sem, 2)

        @block.tensor
        def _(pe):
            pe.wait_ge(s["odd"].sem, 3)
            nc.tensor.matmul(m.ps[0:1, 4, 0:1], m.odd[:], m.ones[:], start=True, stop=True).then_inc(s["odd_sum"].sem, 1)
            pe.wait_ge(s["loaded"], loads)
            pe.wait_ge(s["dv"].sem, 2)
            for k in range(2):
                for j in range(2):
                    last = nc.tensor.transpose(m.ps[:, j, k * P:(k + 1) * P],
                                               m.w_node[:, k, j * P:(j + 1) * P], m.ident[:])
            last.then_inc(s["tr_w"].sem, 1)
            pe.wait_ge(s["wt_done"].sem, 1)
            for k in range(2):
                for j in range(2):
                    last = nc.tensor.matmul(m.ps[:, 2 + k, 0:2 * HEADS * KINDS], m.w_nodeT[:, j, k * P:(k + 1) * P],
                                            m.attn_diag[:, j, :], start=(j == 0), stop=(j == 1))
            last.then_inc(s["fold"].sem, 1)


def ln_vector(nc, dve, m, s, x, g):
    for j in range(GROUP):
        last = nc.vector.bn_stats(m.bn[:, j, :], x[:, j, :])
    last.then_inc(s["ln_stats"].sem, 1)
    hold(dve, s["ln_stats"].sem, s["ln_stats"].done(g))
    for j in range(GROUP):
        last = nc.vector.bn_aggr(m.mv[:, j, :], m.bn[:, j, :])
    last.then_inc(s["ln_mv"].sem, 1)
    dve.wait_ge(s["ln_sqrt"].sem, s["ln_sqrt"].done(g))
    nc.vector.reciprocal(m.rstd[:], m.std[:]).then_inc(s["ln_rstd"].sem, 1)
    dve.wait_ge(s["ln_rstd"].sem, s["ln_rstd"].done(g))
    nc.vector.scalar_tensor_tensor(m.shift[:], m.mv[:, :, 0], -1.0, m.rstd[:], ALU.mult, ALU.mult).then_inc(s["ln_shift"].sem, 1)


def ln_scalar_sqrt(nc, act, m, s, g):
    act.wait_ge(s["ln_mv"].sem, s["ln_mv"].done(g))
    nc.scalar.activation(m.std[:], m.mv[:, :, 1], ACT.Sqrt, bias=m.eps_ln[:, 0:1]).then_inc(s["ln_sqrt"].sem, 1)


def ln_scalar_apply(nc, act, m, s, x, out, func, g):
    act.wait_ge(s["ln_shift"].sem, s["ln_shift"].done(g))
    for j in range(GROUP):
        last = nc.scalar.activation(out[:, j, :], x[:, j, :], func, bias=m.shift[:, j:j + 1], scale=m.rstd[:, j:j + 1])
    last.then_inc(s["h"].sem, 1)


def transpose_group(nc, m, rows):
    for j in range(GROUP):
        for k in range(2):
            at = j * 2 + k
            last = nc.tensor.transpose(m.ps[:, at // 4, (at % 4) * P:(at % 4 + 1) * P],
                                       rows[:, j, k * P:(k + 1) * P], m.ident[:])
    return last


def copy_transposed(nc, m):
    return nc.scalar.activation(m.hT.rearrange("p j k n -> p (j k n)"),
                                m.ps[:, 0:4, :].rearrange("p b n -> p (b n)")[:, 0:GROUP * D], ACT.Copy)


def group_dma(eng, ap, g, tile, store=False):
    rows = ap[bass.ds(g, 1)].rearrange("o p j d -> (o p) j d")
    return eng.dma_start(rows, tile) if store else eng.dma_start(tile, rows)


def node_features(nc, m, a):
    stack, block, s = phase(nc, "nodes", x=None, ln_stats=0, ln_mv=0, ln_sqrt=0, ln_rstd=0, ln_shift=0, h=1, trans=1, ht=1,
                            mm=GROUP, evac=4, stored=None, out_free=1, zero=0)
    x_g, table, right = group_rows(a["x"]), group_rows(m.table0), group_rows(m.right_dram[0:BLOCKS * P])
    with stack:
        @block.sync
        def _(sp):
            with sp.Fori(0, GROUPS) as g:
                sp.wait_ge(s["h"].sem, s["h"].free(g))
                group_dma(sp, x_g, g, m.x_in[:]).then_inc(s["x"], 16)

        @block.gpsimd
        def _(pool):
            with pool.Fori(0, GROUPS) as g:
                pool.wait_ge(s["evac"].sem, s["evac"].done((g + 1) * GROUP - 1))
                group_dma(pool, table, g, m.table_rows, store=True).then_inc(s["stored"], 16)
                group_dma(pool, right, g, m.right_rows, store=True).then_inc(s["stored"], 16)
                pool.wait_ge(s["stored"], 32 * (g + 1))
                pool.sem_inc(s["out_free"].sem, 1)

        @block.vector
        def _(dve):
            nc.vector.memset(m.table_rows, 0.0).then_inc(s["zero"].sem, 1)
            dve.wait_ge(s["zero"].sem, 1)
            with dve.Fori(0, GROUPS) as g:
                dve.wait_ge(s["x"], 16 * g + 16)
                ln_vector(nc, dve, m, s, m.x_in, g)
                dve.wait_ge(s["out_free"].sem, s["out_free"].free(g))
                for j in range(GROUP):
                    dve.wait_ge(s["mm"].sem, s["mm"].done(g * GROUP + j))
                    out = m.ps[:, 4 + j % 4, :]
                    nc.vector.tensor_copy(m.table_rows[:, j, 0:WIDE].rearrange("p (h c) -> p h c", c=HW)[:, :, 0:HD],
                                          out[:, 0:D].rearrange("p (h c) -> p h c", c=HD))
                    nc.vector.tensor_copy(m.table_rows[:, j, WIDE:ROW], out[:, D:D + 32])
                    nc.vector.tensor_copy(m.right_rows[:, j, :], out[:, D + 32:D + 64]).then_inc(s["evac"].sem, 1)

        @block.scalar
        def _(act):
            with act.Fori(0, GROUPS) as g:
                ln_scalar_sqrt(nc, act, m, s, g)
                act.wait_ge(s["trans"].sem, s["trans"].free(g))
                ln_scalar_apply(nc, act, m, s, m.x_in, m.h, ACT.Relu, g)
                act.wait_ge(s["trans"].sem, s["trans"].done(g))
                act.wait_ge(s["mm"].sem, s["mm"].free((g + 1) * GROUP - 1))
                copy_transposed(nc, m).then_inc(s["ht"].sem, 1)

        @block.tensor
        def _(pe):
            with pe.Fori(0, GROUPS) as g:
                pe.wait_ge(s["h"].sem, s["h"].done(g))
                pe.wait_ge(s["ht"].sem, s["ht"].free(g))
                transpose_group(nc, m, m.h).then_inc(s["trans"].sem, 1)
                pe.wait_ge(s["ht"].sem, s["ht"].done(g))
                for j in range(GROUP):
                    pe.wait_ge(s["evac"].sem, s["evac"].free(g * GROUP + j) if j >= 4 else s["evac"].done(g * GROUP - 1))
                    for k in range(2):
                        last = nc.tensor.matmul(m.ps[:, 4 + j % 4, 0:D + 64], m.hT[:, j, k, :], m.w_node[:, k, :],
                                                start=(k == 0), stop=(k == 1))
                    last.then_inc(s["mm"].sem, 1)


def gather_chunks(nc, pool, m, s, cols, table):
    batch = SLOTS * TILES
    with pool.Fori(0, ROUNDS // 2) as r:
        for half in range(2):
            for k in range(SLOTS):
                c = (r * 2 + half) * SLOTS + k
                hold(pool, s["rows_used"].sem, s["rows_used"].free(c))
                if k == 0:
                    nc.gpsimd.tensor_copy(m.index[:, half, :], m.src[:, bass.ds((r * 2 + half) * batch, batch)]).then_inc(s["index"].sem, 1)
                    hold(pool, s["index"].sem, s["index"].done(r * 2 + half))
                for t in range(TILES):
                    at = k * TILES + t
                    pool.indirect_dma_start(m.ring[:, k, t, 0:cols], None, table,
                                            bass.IndirectOffsetOnAxis(ap=m.index[:, half, at:at + 1], axis=0)).then_inc(s[f"rows{k}"], 16)


def window(eng, m, c):
    return eng.value_load(m.first[0:1, bass.ds(c, 1)], min_val=0, max_val=BLOCKS * P - 1)


def store_window(sp, m, s, c, slot, table, cols):
    first = window(sp, m, c)
    sp.wait_ge(s["kept"].sem, s["kept"].done(c))
    sp.dma_start(table[bass.ds(first, P), 0:cols], m.sums_out[:, slot, 0:cols]).then_inc(s["stored"], 16)
    hold(sp, s["stored"], 16 * c + 16)
    sp.sem_inc(s["store"].sem, 1)


def one_hot_of(nc, dve, m, s, c, k, wait):
    dve.wait_ge(s["summed"].sem, s["summed"].free(c))
    nc.vector.tensor_scalar(m.shift_mat[:, k % 2, :], m.step[:], m.shift_by[:, bass.ds(c, 1)], None, ALU.is_equal)
    nc.vector.tensor_tensor(m.one_hot[:, k % 2], m.iota_row[:, None, :].to_broadcast([P, TILES, P]),
                            m.dst_rel[:, bass.ds(c * TILES, TILES)][:, :, None].to_broadcast([P, TILES, P]),
                            ALU.is_equal).then_inc(s["onehot"].sem, 1)


def sum_tiles(nc, m, k, cols, tiles):
    for t in tiles:
        last = nc.tensor.matmul(m.ps[:, 6 + k % 2, 0:cols], m.one_hot[:, k % 2, t, :], m.ring[:, k, t, 0:cols],
                                start=(t == 0), stop=False)
    return last


NODE_SEMS = dict(htrans=1, ht=1, proj=1, evac=1, relu=0, put=None, put_free=1)


def there(n):
    return not isinstance(n, int) or 0 <= n < BLOCKS


def supersteps(eng, chunk, first, second):
    def superstep(g, left):
        for j in range(SUPER):
            chunk(g * (SUPER // SLOTS) + j // SLOTS, j % SLOTS, left + SUPER - 1 - j)
            for q, start in enumerate(STARTS):
                if j == start:
                    first(g * GROUP + q - DELAY)
                if j == start + 1:
                    second(g * GROUP + q - DELAY)

    superstep(0, SUPER)
    with eng.Fori(1, SUPERS - 1) as g:
        superstep(g, SUPER)
    superstep(SUPERS - 1, 0)
    for n in range(BLOCKS - DELAY, BLOCKS + 2):
        first(n)
        second(n)


def blocks_alone(eng, first, second):
    for n in range(-1, 2):
        first(n)
        second(n)
    with eng.Fori(2, BLOCKS - 1) as n:
        first(n)
        second(n)
    for n in range(BLOCKS - 1, BLOCKS + 2):
        first(n)
        second(n)


def block_rows(ap, n):
    return ap[bass.ds(n * P, P)]


def of_block(tile, n):
    return tile[:, bass.ds(n, 1), :].rearrange("p o c -> p (o c)")


def transpose_block(nc, m, bank, rows):
    for k in range(2):
        last = nc.tensor.transpose(m.ps[:, bank, k * P:(k + 1) * P], rows[:, k * P:(k + 1) * P], m.ident[:])
    return last


def project_transposed(nc, act, m, s, n):
    act.wait_ge(s["htrans"].sem, s["htrans"].done(n))
    act.wait_ge(s["proj"].sem, s["proj"].free(n))
    nc.scalar.activation(m.b_hT[:], m.ps[:, 4, 0:D], ACT.Copy).then_inc(s["ht"].sem, 1)


def project_relu(nc, act, m, s, n):
    act.wait_ge(s["evac"].sem, s["evac"].done(n))
    nc.scalar.activation(m.b_msg[:], m.b_msg[:], ACT.Relu).then_inc(s["relu"].sem, 1)


def project_transpose(nc, pe, m, s, n):
    pe.wait_ge(s["h"].sem, s["h"].done(n))
    pe.wait_ge(s["ht"].sem, s["ht"].free(n))
    transpose_block(nc, m, 4, m.b_h).then_inc(s["htrans"].sem, 1)


def project_multiply(nc, pe, m, s, l, n):
    pe.wait_ge(s["ht"].sem, s["ht"].done(n))
    pe.wait_ge(s["evac"].sem, s["evac"].free(n))
    for k in range(2):
        last = nc.tensor.matmul(m.ps[:, 5, :], m.b_hT[:, k * P:(k + 1) * P], m.w_pr[:, l, k, :], start=(k == 0), stop=(k == 1))
    last.then_inc(s["proj"].sem, 1)


def project_bias(nc, dve, m, s, l, n):
    dve.wait_ge(s["proj"].sem, s["proj"].done(n))
    dve.wait_ge(s["put_free"].sem, s["put_free"].free(n))
    nc.vector.tensor_tensor(m.b_msg[:], m.ps[:, 5, 0:D], m.bias[:, l, 0:D], ALU.add)
    nc.vector.tensor_tensor(of_block(m.root, n), m.ps[:, 5, D:2 * D], m.bias[:, l, D:2 * D], ALU.add).then_inc(s["evac"].sem, 1)


def project_store(sp, m, s, table, n):
    sp.wait_ge(s["relu"].sem, s["relu"].done(n))
    sp.dma_start(block_rows(table, n), m.b_msg[:]).then_inc(s["put"], 16)
    hold(sp, s["put"], 16 * n + 16)
    sp.sem_inc(s["put_free"].sem, 1)


def norm_statistics(nc, dve, m, s, rows, n):
    nc.vector.bn_stats(m.b_bn[:], rows).then_inc(s["stats"].sem, 1)
    hold(dve, s["stats"].sem, s["stats"].done(n))
    nc.vector.bn_aggr(m.b_mv[:], m.b_bn[:]).then_inc(s["mv"].sem, 1)


def norm_scale(nc, dve, m, s, n):
    dve.wait_ge(s["std"].sem, s["std"].done(n))
    nc.vector.reciprocal(m.b_rstd[:], m.b_std[:]).then_inc(s["rstd"].sem, 1)
    dve.wait_ge(s["rstd"].sem, s["rstd"].done(n))
    nc.vector.scalar_tensor_tensor(m.b_shift[:], m.b_mv[:, 0:1], -1.0, m.b_rstd[:], ALU.mult, ALU.mult).then_inc(s["shift"].sem, 1)


def norm_scalar(nc, act, m, s, rows, func, n):
    act.wait_ge(s["mv"].sem, s["mv"].done(n))
    nc.scalar.activation(m.b_std[:], m.b_mv[:, 1:2], ACT.Sqrt, bias=m.eps_ln[:, 0:1]).then_inc(s["std"].sem, 1)
    act.wait_ge(s["shift"].sem, s["shift"].done(n))
    act.wait_ge(s["h_free"].sem, s["h_free"].free(n))
    nc.scalar.activation(m.b_h[:], rows, func, bias=m.b_shift[:, 0:1], scale=m.b_rstd[:, 0:1]).then_inc(s["h"].sem, 1)


NORM_SEMS = dict(stats=0, mv=0, std=0, rstd=0, shift=0)


class AttentionNodes:

    sems = dict(NODE_SEMS, **NORM_SEMS, sums=None, floors=0, recips=0, norm=1, x1=1, x1_put=None, x1_free=1, h=1)

    @staticmethod
    def sync(nc, sp, m, a, s):
        def first(n):
            if there(n - 2):
                project_store(sp, m, s, m.tables[0], n - 2)

        def second(n):
            if there(n):
                sp.wait_ge(s["x1"].sem, s["x1"].done(n))
                sp.dma_start(block_rows(m.x1, n), m.b_o[:]).then_inc(s["x1_put"], 16)
                hold(sp, s["x1_put"], 16 * n + 16)
                sp.sem_inc(s["x1_free"].sem, 1)
            if there(n + 1):
                sp.wait_ge(s["x1"].sem, s["x1"].free(n + 1))
                sp.dma_start(m.b_sums[:, 0:SUMC], block_rows(m.sums, n + 1)).then_inc(s["sums"], 16)
                sp.dma_start(m.b_x[:], block_rows(a["x"], n + 1)).then_inc(s["sums"], 16)

        return first, second

    @staticmethod
    def tensor(nc, pe, m, s):
        def first(n):
            if there(n - 1):
                project_transpose(nc, pe, m, s, n - 1)

        def second(n):
            if there(n - 1):
                project_multiply(nc, pe, m, s, 0, n - 1)

        return first, second

    @staticmethod
    def vector(nc, dve, m, s):
        def first(n):
            if not there(n):
                return
            dve.wait_ge(s["sums"], 32 * n + 32)
            heads = m.b_sums[:, 0:WIDE].rearrange("p (h c) -> p h c", c=HW)
            nc.vector.tensor_scalar(m.b_degree[:], m.b_sums[:, WIDE:SUMC], 1.0, None, ALU.max)
            nc.vector.tensor_scalar(m.b_weight[:], heads[:, :, HD], 1.0e-30, None, ALU.max).then_inc(s["floors"].sem, 1)
            dve.wait_ge(s["floors"].sem, s["floors"].done(n))
            nc.vector.reciprocal(m.inv_deg[:, bass.ds(n, 1)], m.b_degree[:])
            nc.vector.reciprocal(m.b_weight[:], m.b_weight[:]).then_inc(s["recips"].sem, 1)
            dve.wait_ge(s["recips"].sem, s["recips"].done(n))
            dve.wait_ge(s["x1_free"].sem, s["x1_free"].free(n))
            dve.wait_ge(s["h"].sem, s["h"].free(n))
            nc.vector.tensor_tensor(m.b_o[:].rearrange("p (h c) -> p h c", c=HD), heads[:, :, 0:HD],
                                    m.b_weight[:, :, None].to_broadcast([P, HEADS, HD]), ALU.mult).then_inc(s["norm"].sem, 1)
            dve.wait_ge(s["norm"].sem, s["norm"].done(n))
            nc.vector.tensor_tensor(m.b_o[:], m.b_o[:], m.b_x[:], ALU.add).then_inc(s["x1"].sem, 1)

        def second(n):
            if there(n):
                hold(dve, s["x1"].sem, s["x1"].done(n))
                norm_statistics(nc, dve, m, s, m.b_o[:], n)
            if there(n - 1):
                project_bias(nc, dve, m, s, 0, n - 1)
            if there(n):
                norm_scale(nc, dve, m, s, n)

        return first, second

    @staticmethod
    def scalar(nc, act, m, s):
        def first(n):
            if there(n - 1):
                project_transposed(nc, act, m, s, n - 1)

        def second(n):
            if there(n):
                norm_scalar(nc, act, m, dict(s, h_free=s["htrans"]), m.b_o[:], ACT.Relu, n)
            if there(n - 1):
                project_relu(nc, act, m, s, n - 1)

        return first, second


class LayerNodes:

    def __init__(self, l):
        self.l, self.final = l, l == LAYERS - 1
        self.sems = dict(agg=None, atrans=1, at=1, lmm=1, o=1, norm2=0, root2=0, floor=0, recip=0, h=1)
        if self.final:
            self.sems.update(NORM_SEMS, x1=None, y=0, aff=0, affb=0, out=1, put=None, put_free=1)
        else:
            self.sems.update(NODE_SEMS, ey=0, e1=0, er=0)

    def sync(self, nc, sp, m, a, s):
        def first(n):
            if self.final:
                if there(n - 1):
                    sp.wait_ge(s["out"].sem, s["out"].done(n - 1))
                    sp.dma_start(block_rows(a["out"], n - 1), m.b_h[:]).then_inc(s["put"], 16)
                    hold(sp, s["put"], 16 * (n - 1) + 16)
                    sp.sem_inc(s["put_free"].sem, 1)
                if there(n):
                    sp.dma_start(m.b_x[:], block_rows(m.x1, n)).then_inc(s["x1"], 16)
            elif there(n - 2):
                project_store(sp, m, s, m.tables[self.l + 1], n - 2)

        def second(n):
            if there(n + 1):
                sp.wait_ge(s["atrans"].sem, s["atrans"].free(n + 1))
                sp.dma_start(m.b_sums[:, 0:D], block_rows(m.agg_dram, n + 1)).then_inc(s["agg"], 16)

        return first, second

    def tensor(self, nc, pe, m, s):
        def first(n):
            if not self.final and there(n - 1):
                project_transpose(nc, pe, m, s, n - 1)
            if there(n):
                pe.wait_ge(s["agg"], 16 * n + 16)
                pe.wait_ge(s["at"].sem, s["at"].free(n))
                transpose_block(nc, m, 0, m.b_sums).then_inc(s["atrans"].sem, 1)

        def second(n):
            if there(n):
                pe.wait_ge(s["at"].sem, s["at"].done(n))
                pe.wait_ge(s["o"].sem, s["o"].free(n))
                for k in range(2):
                    last = nc.tensor.matmul(m.ps[:, 2, 0:D], m.b_aT[:, k * P:(k + 1) * P], m.w_l[:, self.l, k, :],
                                            start=(k == 0), stop=(k == 1))
                last.then_inc(s["lmm"].sem, 1)
            if not self.final and there(n - 1):
                project_multiply(nc, pe, m, s, self.l + 1, n - 1)

        return first, second

    def vector(self, nc, dve, m, s):
        def first(n):
            pass

        def second(n):
            if there(n):
                dve.wait_ge(s["lmm"].sem, s["lmm"].done(n))
                nc.vector.scalar_tensor_tensor(m.b_o[:], m.ps[:, 2, 0:D], m.inv_deg[:, bass.ds(n, 1)], of_block(m.root, n),
                                               ALU.mult, ALU.add).then_inc(s["o"].sem, 1)
            if not self.final and there(n - 1):
                project_bias(nc, dve, m, s, self.l + 1, n - 1)
            if not there(n):
                return
            dve.wait_ge(s["root2"].sem, s["root2"].done(n))
            nc.vector.tensor_scalar(m.b_norm[:], m.b_norm[:], NORM_EPS, -1.0, ALU.max, ALU.mult).then_inc(s["floor"].sem, 1)
            dve.wait_ge(s["floor"].sem, s["floor"].done(n))
            nc.vector.reciprocal(m.b_inv_norm[:], m.b_norm[:]).then_inc(s["recip"].sem, 1)
            if not self.final:
                dve.wait_ge(s["ey"].sem, s["ey"].done(n))
                nc.vector.tensor_scalar(m.b_ey[:], m.b_ey[:], 1.0, -1.0, ALU.add, ALU.mult).then_inc(s["e1"].sem, 1)
                dve.wait_ge(s["e1"].sem, s["e1"].done(n))
                nc.vector.reciprocal(m.b_ey[:], m.b_ey[:]).then_inc(s["er"].sem, 1)
                dve.wait_ge(s["er"].sem, s["er"].done(n))
                dve.wait_ge(s["htrans"].sem, s["htrans"].free(n))
                nc.vector.scalar_tensor_tensor(m.b_h[:], m.b_o[:], m.b_inv_norm[:, 0:1], m.b_ey[:], ALU.mult, ALU.mult).then_inc(s["h"].sem, 1)
            else:
                dve.wait_ge(s["recip"].sem, s["recip"].done(n))
                nc.vector.tensor_scalar(m.b_ey[:], m.b_o[:], m.b_inv_norm[:, 0:1], -1.0, ALU.mult, ALU.mult).then_inc(s["y"].sem, 1)
                hold(dve, s["y"].sem, s["y"].done(n))
                norm_statistics(nc, dve, m, s, m.b_ey[:], n)
                norm_scale(nc, dve, m, s, n)
                dve.wait_ge(s["h"].sem, s["h"].done(n))
                nc.vector.tensor_tensor(m.b_h[:], m.b_h[:], m.ln_w[:], ALU.mult).then_inc(s["aff"].sem, 1)
                dve.wait_ge(s["aff"].sem, s["aff"].done(n))
                nc.vector.tensor_tensor(m.b_h[:], m.b_h[:], m.ln_b[:], ALU.add).then_inc(s["affb"].sem, 1)
                dve.wait_ge(s["affb"].sem, s["affb"].done(n))
                dve.wait_ge(s["x1"], 16 * n + 16)
                nc.vector.tensor_tensor(m.b_h[:], m.b_h[:], m.b_x[:], ALU.add).then_inc(s["out"].sem, 1)

        return first, second

    def scalar(self, nc, act, m, s):
        def first(n):
            if not self.final and there(n - 1):
                project_transposed(nc, act, m, s, n - 1)
            if there(n):
                act.wait_ge(s["atrans"].sem, s["atrans"].done(n))
                act.wait_ge(s["lmm"].sem, s["lmm"].free(n))
                nc.scalar.activation(m.b_aT[:], m.ps[:, 0, 0:D], ACT.Copy).then_inc(s["at"].sem, 1)

        def second(n):
            if there(n):
                act.wait_ge(s["o"].sem, s["o"].done(n))
                nc.scalar.activation(m.b_ey[:], m.b_o[:], ACT.Square, accum_out=m.b_norm2[:, 0:1]).then_inc(s["norm2"].sem, 1)
                act.wait_ge(s["norm2"].sem, s["norm2"].done(n))
                nc.scalar.activation(m.b_norm[:], m.b_norm2[:], ACT.Sqrt).then_inc(s["root2"].sem, 1)
                if not self.final:
                    act.wait_ge(s["recip"].sem, s["recip"].done(n))
                    nc.scalar.activation(m.b_ey[:], m.b_o[:], ACT.Exp, scale=m.b_inv_norm[:, 0:1]).then_inc(s["ey"].sem, 1)
            if not self.final and there(n - 1):
                project_relu(nc, act, m, s, n - 1)
            if self.final and there(n):
                norm_scalar(nc, act, m, dict(s, h_free=s["put_free"]), m.b_ey[:], ACT.Identity, n)

        return first, second


def nodes_alone(nc, m, a, name, nodes):
    stack, block, s = phase(nc, name, **nodes.sems)
    with stack:
        @block.sync
        def _(sp):
            blocks_alone(sp, *nodes.sync(nc, sp, m, a, s))

        @block.tensor
        def _(pe):
            blocks_alone(pe, *nodes.tensor(nc, pe, m, s))

        @block.vector
        def _(dve):
            blocks_alone(dve, *nodes.vector(nc, dve, m, s))

        @block.scalar
        def _(act):
            blocks_alone(act, *nodes.scalar(nc, act, m, s))


def layer(nc, m, a, l):
    nodes = LayerNodes(l)
    stack, block, s = phase(nc, f"layer{l}", rows0=None, rows1=None, rows2=None, rows3=None, index=0, rows_used=SLOTS,
                            onehot=0, summed=2, kept=2, stored=None, store=2, **nodes.sems)
    with stack:
        @block.gpsimd
        def _(pool):
            gather_chunks(nc, pool, m, s, D, m.tables[l])

        @block.sync
        def _(sp):
            def chunk(i, k, left):
                store_window(sp, m, s, i * SLOTS + k, k % 2, m.agg_dram, D)

            supersteps(sp, chunk, *nodes.sync(nc, sp, m, a, s))

        @block.tensor
        def _(pe):
            def chunk(i, k, left):
                c = i * SLOTS + k
                pe.wait_ge(s[f"rows{k}"], 16 * TILES * (i + 1))
                pe.wait_ge(s["onehot"].sem, s["onehot"].done(c))
                pe.wait_ge(s["kept"].sem, s["kept"].free(c))
                sum_tiles(nc, m, k, D, range(TILES)).then_inc(s["rows_used"].sem, 1)
                pe.wait_ge(s["kept"].sem, s["kept"].done(c - 1))
                nc.tensor.matmul(m.ps[:, 6 + k % 2, 0:D], m.shift_mat[:, k % 2, :], m.sums_out[:, 1 - k % 2, 0:D],
                                 start=False, stop=True).then_inc(s["summed"].sem, 1)

            supersteps(pe, chunk, *nodes.tensor(nc, pe, m, s))

        @block.vector
        def _(dve):
            def chunk(i, k, left):
                if left:
                    one_hot_of(nc, dve, m, s, i * SLOTS + k + 1, k + 1, None)

            nc.vector.memset(m.sums_out[:, 1, :], 0.0)
            one_hot_of(nc, dve, m, s, 0, 0, None)
            supersteps(dve, chunk, *nodes.vector(nc, dve, m, s))

        @block.scalar
        def _(act):
            def chunk(i, k, left):
                c = i * SLOTS + k
                act.wait_ge(s["summed"].sem, s["summed"].done(c))
                act.wait_ge(s["store"].sem, s["store"].free(c))
                nc.scalar.activation(m.sums_out[:, k % 2, 0:D], m.ps[:, 6 + k % 2, 0:D], ACT.Copy).then_inc(s["kept"].sem, 1)

            supersteps(act, chunk, *nodes.scalar(nc, act, m, s))


def attention(nc, m, a):
    nodes = AttentionNodes
    stack, block, s = phase(nc, "attend", rows0=None, rows1=None, rows2=None, rows3=None, index=0, rows_used=SLOTS,
                            edges0=None, edges1=None, oht=0, right=2, kinds=1, masked=0, red=0, leaky=2,
                            xt=1, fwd=2, bwd=SLOTS, mt=1, drop=1, diff=1, expd=0, fallen=2, weighed=0,
                            onehot=0, summed=2, scaled=2, kept=2, stored=None, store=2, **nodes.sems)
    featT = a["edge_attr_16"]
    mask = a["edge_attr_4"]
    ring_heads = [m.ring[:, k, :, 0:WIDE].rearrange("p t (h c) -> p t h c", c=HW) for k in range(SLOTS)]
    loads = 5

    def edge_loads(i, k):
        return 16 * loads * (i * 2 + k // 2 + 1)

    def ahead(i, k, n):
        return i + (k + n) // SLOTS, (k + n) % SLOTS

    def pipeline(eng, step, slots):
        step((0, 0), None, None)
        step((0, 1), (0, 0), None)

        def body(i, k, left):
            step(ahead(i, k, 2) if left >= 2 else None, ahead(i, k, 1) if left >= 1 else None, (i, k))

        supersteps(eng, body, *slots)

    with stack:
        @block.gpsimd
        def _(pool):
            gather_chunks(nc, pool, m, s, ROW, m.table0)

        @block.sync
        def _(sp):
            def load(i, k):
                c = i * SLOTS + k
                slot = k % 2
                first = window(sp, m, c)
                sp.wait_ge(s["right"].sem, s["right"].free(c))
                sp.wait_ge(s["leaky"].sem, s["leaky"].free(c))
                sp.wait_ge(s["bwd"].sem, s["bwd"].free(c))
                sem = s[f"edges{slot}"]
                sp.dma_start(m.dst_bc[:, slot, :], a["dst_edges"][bass.ds(c, 1)].to_broadcast([P, CHUNK])).then_inc(sem, 16)
                sp.dma_start(m.right[:, slot, :], m.right_dram[bass.ds(first, P)]).then_inc(sem, 16)
                sp.dma_start(m.e_featT[:, slot, :], featT[bass.ds(c, 1)].rearrange("o f e -> (o f) e")).then_inc(sem, 16)
                sp.dma_start(m.e_mask[:, slot, :], mask[bass.ds(c, 1)].rearrange("o p n -> (o p) n")).then_inc(sem, 16)
                sp.dma_start(m.flags[:, k, 0:CHUNK], m.flag_rows[bass.ds(c, 1)].to_broadcast([HEADS, CHUNK])).then_inc(sem, 16)

            def body(i, k, left):
                if left >= 3:
                    load(*ahead(i, k, 3))
                store_window(sp, m, s, i * SLOTS + k, k % 2, m.sums, SUMC)

            for k in range(3):
                load(0, k)
            supersteps(sp, body, *nodes.sync(nc, sp, m, a, s))

        @block.tensor
        def _(pe):
            def to_heads(i, k):
                c = i * SLOTS + k
                pe.wait_ge(s["leaky"].sem, s["leaky"].done(c))
                pe.wait_ge(s["fwd"].sem, s["fwd"].done(c - 1))
                for t in range(TILES):
                    last = nc.tensor.transpose(m.ps[0:HEADS, 1 + t // 4, (t % 4) * P:(t % 4 + 1) * P],
                                               m.score[:, k % 2, t, :], m.ident[:])
                last.then_inc(s["xt"].sem, 1)

            def scores(i, k):
                c = i * SLOTS + k
                slot = k % 2
                pe.wait_ge(s[f"edges{slot}"], edge_loads(i, k))
                pe.wait_ge(s["kinds"].sem, s["kinds"].free(c))
                nc.tensor.matmul(m.ps[:, 0, 0:TILES * 32], m.e_featT[:, slot, :], m.attn_edge[:].rearrange("f t c -> f (t c)"),
                                 start=True, stop=False)
                pe.wait_ge(s["oht"].sem, s["oht"].done(c))
                for t in range(TILES):
                    last = nc.tensor.matmul(m.ps[:, 0, t * 32:(t + 1) * 32], m.one_hotT[:, t * P:(t + 1) * P],
                                            m.right[:, slot, :], start=False, stop=(t == TILES - 1))
                last.then_inc(s["right"].sem, 1)

            def to_edges(i, k):
                c = i * SLOTS + k
                pe.wait_ge(s["diff"].sem, s["diff"].free(c))
                pe.wait_ge(s["fallen"].sem, s["fallen"].done(c - 1))
                hold(pe, s["drop"].sem, s["drop"].done(c))
                nc.tensor.matmul(m.ps[:, 3, FALL:FALL + HEADS], m.drop[:, 0:1].to_broadcast([HEADS, P]),
                                 m.ident[0:HEADS, 0:HEADS], start=True, stop=True)
                for t in range(TILES):
                    last = nc.tensor.transpose(m.ps[:, 3, t * HEADS:(t + 1) * HEADS],
                                               m.seg_max[:, t * P:(t + 1) * P], m.ident[0:HEADS, 0:HEADS])
                last.then_inc(s["mt"].sem, 1)

            def step(score, weigh, total):
                if score:
                    scores(*score)
                if total:
                    i, k = total
                    c = i * SLOTS + k
                    pe.wait_ge(s["weighed"].sem, s["weighed"].done(c))
                    pe.wait_ge(s["onehot"].sem, s["onehot"].done(c))
                    pe.wait_ge(s["kept"].sem, s["kept"].free(c))
                    sum_tiles(nc, m, k, SUMC, range(0, BEFORE))
                if weigh:
                    to_edges(*weigh)
                if total:
                    sum_tiles(nc, m, k, SUMC, range(BEFORE, TILES - 1))
                if score:
                    to_heads(*score)
                if total:
                    sum_tiles(nc, m, k, SUMC, range(TILES - 1, TILES)).then_inc(s["rows_used"].sem, 1)
                    pe.wait_ge(s["scaled"].sem, s["scaled"].done(c))
                    nc.tensor.matmul(m.ps[:, 6 + k % 2, 0:SUMC], m.shift_mat[:, k % 2, :], m.carry[:],
                                     start=False, stop=True).then_inc(s["summed"].sem, 1)

            pipeline(pe, step, nodes.tensor(nc, pe, m, s))

        @block.vector
        def _(dve):
            def step(score, weigh, total):
                if score:
                    ai, ak = score
                    ac, aslot = ai * SLOTS + ak, ak % 2
                    hold(dve, s[f"edges{aslot}"], edge_loads(ai, ak))
                    dve.wait_ge(s["right"].sem, s["right"].done(ac - 1))
                    nc.vector.tensor_scalar(m.one_hotT, m.dst_bc[:, aslot, :], m.window_p[:, bass.ds(ac, 1)], None,
                                            ALU.is_equal).then_inc(s["oht"].sem, 1)
                if total:
                    i, k = total
                    c = i * SLOTS + k
                    dve.wait_ge(s["expd"].sem, s["expd"].done(c))
                    nc.vector.tensor_tensor(ring_heads[k][:, :, :, 0:HD], ring_heads[k][:, :, :, 0:HD],
                                            ring_heads[k][:, :, :, HD:HW].to_broadcast([P, TILES, HEADS, HD]),
                                            ALU.mult).then_inc(s["weighed"].sem, 1)
                if weigh:
                    bi, bk = weigh
                    bc, bslot = bi * SLOTS + bk, bk % 2
                    dve.wait_ge(s["xt"].sem, s["xt"].done(bc))
                    nc.vector.tensor_tensor_scan(m.run_max[:, bslot, :], m.flags[:, bk, 0:CHUNK],
                                                 m.ps[0:HEADS, 1:3, :].rearrange("p b n -> p (b n)")[:, 0:CHUNK],
                                                 m.run_max[:, 1 - bslot, CHUNK - 1:CHUNK], ALU.add, ALU.max).then_inc(s["fwd"].sem, 1)
                if weigh:
                    dve.wait_ge(s["fwd"].sem, s["fwd"].done(bc))
                    dve.wait_ge(s["mt"].sem, s["mt"].free(bc))
                    nc.vector.tensor_tensor_scan(m.seg_max[:, ::-1], m.flags[:, bk, 1:CHUNK + 1][:, ::-1], m.run_max[:, bslot, ::-1],
                                                 0.0, ALU.add, ALU.max).then_inc(s["bwd"].sem, 1)
                if score:
                    dve.wait_ge(s["right"].sem, s["right"].done(ac))
                    dve.wait_ge(s[f"rows{ak}"], 16 * TILES * (ai + 1))
                    nc.vector.tensor_tensor(m.kinds, m.ps[:, 0, 0:TILES * 32].rearrange("p (t c) -> p t c", c=32),
                                            m.ring[:, ak, :, WIDE:ROW], ALU.add).then_inc(s["kinds"].sem, 1)
                if weigh:
                    dve.wait_ge(s["bwd"].sem, s["bwd"].done(bc))
                    nc.vector.tensor_scalar(m.drop[:], m.run_max[:, 1 - bslot, CHUNK - 1:CHUNK], m.seg_max[:, 0:1], 0.0,
                                            ALU.subtract, ALU.min).then_inc(s["drop"].sem, 1)
                if score:
                    dve.wait_ge(s["kinds"].sem, s["kinds"].done(ac))
                    kinds4 = m.kinds.rearrange("p t (h n) -> p t h n", n=KINDS)
                    mask4 = m.e_mask[:, aslot, :].rearrange("p (t n) -> p t n", n=KINDS)[:, :, None, :].to_broadcast([P, TILES, HEADS, KINDS])
                    nc.vector.tensor_tensor(kinds4, kinds4, mask4, ALU.mult).then_inc(s["masked"].sem, 1)
                if total:
                    rescale(i, k)
                if weigh:
                    one_hot_of(nc, dve, m, s, bc, bk, None)
                if score:
                    dve.wait_ge(s["masked"].sem, s["masked"].done(ac))
                    nc.vector.tensor_reduce(m.score0, kinds4, AX.X, ALU.add).then_inc(s["red"].sem, 1)
                if weigh:
                    dve.wait_ge(s["mt"].sem, s["mt"].done(bc))
                    nc.vector.tensor_tensor(m.diff, m.score[:, bslot], m.ps[:, 3, 0:TILES * HEADS].rearrange("p (t h) -> p t h", h=HEADS),
                                            ALU.subtract).then_inc(s["diff"].sem, 1)
                if score:
                    dve.wait_ge(s["red"].sem, s["red"].done(ac))
                    nc.vector.scalar_tensor_tensor(m.score[:, aslot], m.score0, SLOPE, m.score0, ALU.mult, ALU.max).then_inc(s["leaky"].sem, 1)
                if weigh:
                    nc.vector.memset(m.ring[:, bk, :, WIDE:SUMC], 1.0)

            def rescale(i, k):
                c = i * SLOTS + k
                slot = (k + 1) % 2
                dve.wait_ge(s["kept"].sem, s["kept"].done(c - 1))
                dve.wait_ge(s["fallen"].sem, s["fallen"].done(c))
                nc.vector.tensor_copy(m.carry[:, WIDE:SUMC], m.sums_out[:, slot, WIDE:SUMC])
                nc.vector.tensor_tensor(m.carry[:, 0:WIDE].rearrange("p (h c) -> p h c", c=HW),
                                        m.sums_out[:, slot, 0:WIDE].rearrange("p (h c) -> p h c", c=HW),
                                        m.fall[:, k % 2, :, None].to_broadcast([P, HEADS, HW]), ALU.mult).then_inc(s["scaled"].sem, 1)

            pipeline(dve, step, nodes.vector(nc, dve, m, s))

        @block.scalar
        def _(act):
            def step(score, weigh, total):
                if weigh:
                    i, k = weigh
                    c = i * SLOTS + k
                    act.wait_ge(s["diff"].sem, s["diff"].done(c))
                    nc.scalar.activation(ring_heads[k][:, :, :, HD], m.diff, ACT.Exp, scale=1.0 / 3.0).then_inc(s["expd"].sem, 1)
                    act.wait_ge(s["scaled"].sem, s["scaled"].free(c))
                    nc.scalar.activation(m.fall[:, k % 2, :], m.ps[:, 3, FALL:FALL + HEADS], ACT.Exp, scale=1.0 / 3.0).then_inc(s["fallen"].sem, 1)
                if total:
                    i, k = total
                    c = i * SLOTS + k
                    act.wait_ge(s["summed"].sem, s["summed"].done(c))
                    act.wait_ge(s["store"].sem, s["store"].free(c))
                    act.wait_ge(s["scaled"].sem, s["scaled"].done(c - 1))
                    nc.scalar.activation(m.sums_out[:, k % 2, 0:SUMC], m.ps[:, 6 + k % 2, 0:SUMC], ACT.Copy).then_inc(s["kept"].sem, 1)

            pipeline(act, step, nodes.scalar(nc, act, m, s))


def any_tile(nc, m, a, name, cols, table, into, attend):
    stack, block, s = phase(nc, name, edges=None, edges_free=1, index=0, got=None, scores=0, sT=0, sTc=0, rowmax=0,
                            same=0, first=0, uniq=0, work=0, ready=0, put=None, summed=0, merged=0, expd=0)
    weigh = attend == "sum"
    tiles = CHUNKS * TILES
    steps = {"max": 9, "sum": 5, None: 1}[attend]
    with stack:
        @block.sync
        def _(sp):
            with sp.Fori(0, tiles) as t:
                sp.wait_ge(s["edges_free"].sem, s["edges_free"].free(t))
                sp.dma_start(m.g_dst_bc, m.dst_tiles[bass.ds(t, 1)].to_broadcast([P, P])).then_inc(s["edges"], 16)
                sp.dma_start(m.g_featT, a["feat_tiles"][bass.ds(t, 1)].rearrange("o f e -> (o f) e")).then_inc(s["edges"], 16)
                sp.dma_start(m.g_mask, a["mask_tiles"][bass.ds(t, 1)].rearrange("o p n -> (o p) n")).then_inc(s["edges"], 16)

        @block.gpsimd
        def _(pool):
            with pool.Fori(0, tiles) as t:
                hold(pool, s["uniq"].sem, s["uniq"].done(t))
                pool.indirect_dma_start(m.g_rows[:, 0:cols], None, table,
                                        bass.IndirectOffsetOnAxis(ap=m.g_src, axis=0)).then_inc(s["got"], 16)
                if attend == "max":
                    pool.indirect_dma_start(m.g_right, None, m.right_dram,
                                            bass.IndirectOffsetOnAxis(ap=m.g_dst, axis=0)).then_inc(s["got"], 16)
                if attend == "sum":
                    pool.indirect_dma_start(m.g_max, None, m.max_dram,
                                            bass.IndirectOffsetOnAxis(ap=m.g_dst, axis=0)).then_inc(s["got"], 16)
                width = HEADS if attend == "max" else SUMC if weigh else D
                pool.indirect_dma_start(m.g_old[:, 0:width], None, into,
                                        bass.IndirectOffsetOnAxis(ap=m.g_dst, axis=0)).then_inc(s["got"], 16)
                hold(pool, s["merged"].sem, s["merged"].done(t))
                pool.indirect_dma_start(into, bass.IndirectOffsetOnAxis(ap=m.g_once, axis=0), m.g_old[:, 0:width], None,
                                        bounds_check=TABLE - 1, oob_is_err=False).then_inc(s["put"], 16)
                hold(pool, s["put"], 16 * t + 16)
                pool.sem_inc(s["edges_free"].sem, 1)

        @block.tensor
        def _(pe):
            with pe.Fori(0, tiles) as t:
                if attend == "max":
                    pe.wait_ge(s["edges"], 48 * t + 48)
                    nc.tensor.matmul(m.ps[:, 0, 0:32], m.g_featT, m.attn_edge[0:FEATS, 0, :],
                                     start=True, stop=True).then_inc(s["scores"].sem, 1)
                    pe.wait_ge(s["ready"].sem, s["ready"].done(t))
                    nc.tensor.transpose(m.ps[0:HEADS, 1, 0:P], m.g_score, m.ident[:]).then_inc(s["sT"].sem, 1)
                    pe.wait_ge(s["sTc"].sem, s["sTc"].done(t))
                    for h in range(HEADS):
                        last = nc.tensor.matmul(m.ps[:, 2 + h // 4, (h % 4) * P:(h % 4 + 1) * P],
                                                m.ident[0:HEADS, h:h + 1].to_broadcast([HEADS, P]), m.g_scoreT,
                                                start=True, stop=True)
                    last.then_inc(s["rowmax"].sem, 1)
                else:
                    pe.wait_ge(s["ready"].sem, s["ready"].done(t))
                    width = SUMC if weigh else D
                    nc.tensor.matmul(m.ps[:, 0, 0:width], m.g_same, m.g_rows[:, 0:width],
                                     start=True, stop=True).then_inc(s["summed"].sem, 1)

        @block.vector
        def _(dve):
            with dve.Fori(0, tiles) as t:
                n = [0]

                def link(ins):
                    n[0] += 1
                    ins.then_inc(s["work"].sem, 1)
                    dve.wait_ge(s["work"].sem, total * t + n[0])

                total = {"max": 13, "sum": 10, None: 7}[attend]
                dve.wait_ge(s["edges"], 48 * t + 48)
                nc.vector.tensor_copy(m.g_src, m.src[:, bass.ds(t, 1)])
                link(nc.vector.tensor_copy(m.g_dst, m.dst_all[:, bass.ds(t, 1)]))
                link(nc.vector.tensor_copy(m.g_dstf, m.g_dst))
                link(nc.vector.tensor_scalar(m.g_same, m.g_dst_bc, m.g_dstf, None, ALU.is_equal))
                link(nc.vector.scalar_tensor_tensor(m.g_masked, m.step[:], 0.0, m.g_same, ALU.is_gt, ALU.mult))
                link(nc.vector.tensor_reduce(m.g_dups, m.g_masked, AX.X, ALU.add))
                link(nc.vector.tensor_scalar(m.g_dups, m.g_dups, float(TABLE), None, ALU.mult))
                link(nc.vector.tensor_tensor(m.g_dups, m.g_dups, m.g_dstf, ALU.add))
                nc.vector.tensor_copy(m.g_once, m.g_dups).then_inc(s["uniq"].sem, 1)
                gets = 32 if attend is None else 48
                dve.wait_ge(s["got"], gets * t + gets)
                if attend == "max":
                    dve.wait_ge(s["scores"].sem, s["scores"].done(t))
                    kinds = m.g_kinds
                    link(nc.vector.tensor_tensor(kinds, m.ps[:, 0, 0:32], m.g_rows[:, WIDE:ROW], ALU.add))
                    link(nc.vector.tensor_tensor(kinds, kinds, m.g_right, ALU.add))
                    kinds3 = kinds.rearrange("p (h n) -> p h n", n=KINDS)
                    link(nc.vector.tensor_tensor(kinds3, kinds3, m.g_mask[:, None, :].to_broadcast([P, HEADS, KINDS]), ALU.mult))
                    link(nc.vector.tensor_reduce(m.g_score0, kinds3, AX.X, ALU.add))
                    nc.vector.scalar_tensor_tensor(m.g_score, m.g_score0, SLOPE, m.g_score0, ALU.mult, ALU.max).then_inc(s["ready"].sem, 1)
                    dve.wait_ge(s["ready"].sem, s["ready"].done(t))
                    nc.vector.tensor_copy(m.g_scores[:, bass.ds(t, 1), :].rearrange("p o h -> p (o h)"), m.g_score)
                    dve.wait_ge(s["sT"].sem, s["sT"].done(t))
                    nc.vector.tensor_copy(m.g_scoreT, m.ps[0:HEADS, 1, 0:P]).then_inc(s["sTc"].sem, 1)
                    link(nc.vector.tensor_scalar(m.g_masked, m.g_same, FAR, -FAR, ALU.mult, ALU.add))
                    dve.wait_ge(s["rowmax"].sem, s["rowmax"].done(t))
                    wide = m.ps[:, 2:4, :].rearrange("p b n -> p (b n)").rearrange("p (h e) -> p h e", h=HEADS)
                    nc.vector.tensor_tensor(m.g_wide, wide, m.g_masked[:, None, :].to_broadcast([P, HEADS, P]), ALU.add).then_inc(s["same"].sem, 1)
                    dve.wait_ge(s["same"].sem, s["same"].done(t))
                    link(nc.vector.tensor_reduce(m.g_score0, m.g_wide, AX.X, ALU.max))
                    nc.vector.tensor_tensor(m.g_old[:, 0:HEADS], m.g_old[:, 0:HEADS], m.g_score0, ALU.max).then_inc(s["merged"].sem, 1)
                else:
                    if weigh:
                        link(nc.vector.tensor_tensor(m.g_score0, m.g_scores[:, bass.ds(t, 1), :].rearrange("p o h -> p (o h)"),
                                                     m.g_max, ALU.subtract))
                        nc.vector.memset(m.g_rows[:, WIDE:SUMC], 1.0)
                        link(nc.vector.tensor_copy(m.g_score, m.g_score0))
                        nc.vector.memset(m.g_kinds, 0.0).then_inc(s["first"].sem, 1)
                        dve.wait_ge(s["expd"].sem, s["expd"].done(t))
                        heads = m.g_rows[:, 0:WIDE].rearrange("p (h c) -> p h c", c=HW)
                        link(nc.vector.tensor_tensor(heads[:, :, 0:HD], heads[:, :, 0:HD],
                                                     heads[:, :, HD:HW].to_broadcast([P, HEADS, HD]), ALU.mult))
                    nc.vector.memset(m.g_kinds, 0.0).then_inc(s["ready"].sem, 1)
                    dve.wait_ge(s["summed"].sem, s["summed"].done(t))
                    width = SUMC if weigh else D
                    nc.vector.tensor_tensor(m.g_old[:, 0:width], m.g_old[:, 0:width], m.ps[:, 0, 0:width], ALU.add).then_inc(s["merged"].sem, 1)
                hold(dve, s["edges_free"].sem, s["edges_free"].done(t))

        if weigh:
            @block.scalar
            def _(act):
                with act.Fori(0, tiles) as t:
                    act.wait_ge(s["first"].sem, s["first"].done(t))
                    nc.scalar.activation(m.g_rows[:, 0:WIDE].rearrange("p (h c) -> p h c", c=HW)[:, :, HD],
                                         m.g_score, ACT.Exp, scale=1.0 / 3.0).then_inc(s["expd"].sem, 1)


def load_destinations(nc, m, a):
    stack, block, s = phase(nc, "dests", loaded=None)
    with stack:
        @block.sync
        def _(sp):
            sp.dma_start(m.dst_all, a["dst"]).then_inc(s["loaded"], 16)
            sp.wait_ge(s["loaded"], 16)


def any_start(nc, m, a, table, cols, value):
    stack, block, s = phase(nc, "fill", filled=0, stored=None)
    with stack:
        @block.vector
        def _(dve):
            nc.vector.memset(m.g_old[:, 0:cols], value).then_inc(s["filled"].sem, 1)

        @block.sync
        def _(sp):
            sp.wait_ge(s["filled"].sem, 1)
            for b in range(BLOCKS + 1):
                sp.dma_start(table[b * P:(b + 1) * P], m.g_old[:, 0:cols]).then_inc(s["stored"], 16)
            sp.wait_ge(s["stored"], 16 * (BLOCKS + 1))


def build(nc, a):
    m = Mem()

    def dram(name, *shape):
        return nc.dram_tensor(name, shape, fp32, kind="Internal").ap()

    m.table0 = dram("attention_table", BLOCKS * P, ROW)
    m.right_dram = dram("right_scores", TABLE, HEADS * KINDS)
    m.sums = dram("attention_sums", TABLE, SUMC)
    m.agg_dram = dram("message_sums", TABLE, D)
    m.tables = [dram(f"message_table{l}", BLOCKS * P, D) for l in range(LAYERS)]
    m.x1 = dram("x_after_attention", BLOCKS * P, D)
    m.max_dram = dram("score_maxima", TABLE, HEADS)
    m.flag_dram = dram("run_flags", CHUNKS * CHUNK)
    m.dst_tiles = a["dst_edges"].rearrange("c (t e) -> (c t) e", e=P)
    m.flag_rows = m.flag_dram.rearrange("(c n) -> c n", n=CHUNK)
    with ExitStack() as ctx:
        def sb(name, shape, dt=fp32):
            return ctx.enter_context(nc.sbuf_tensor(name, shape, dt))

        m.iota_row = sb("iota_row", [P, P])
        m.iota_p = sb("iota_p", [P, 1])
        m.step = sb("step", [P, P])
        m.ident = sb("ident", [P, P])
        m.eps_ln = sb("eps_ln", [P, 1])
        m.ones = sb("ones", [P, 1])
        m.odd = sb("odd", [P, 1])
        m.irregular = sb("irregular", [1, 1], int32)
        m.w_node = sb("w_node", [P, 2, D + 64])
        m.attn_diag = sb("attn_diag", [P, 2, 64])
        m.attn_edge = sb("attn_edge", [TILES * FEATS, TILES, HEADS * KINDS])
        m.w_pr = sb("w_pr", [P, LAYERS, 2, 2 * D])
        m.w_l = sb("w_l", [P, LAYERS, 2, D])
        m.bias = sb("bias", [P, LAYERS, 2 * D])
        m.ln_w = sb("ln_w", [P, D])
        m.ln_b = sb("ln_b", [P, D])
        m.src = sb("src_index", [P, CHUNKS * TILES], int32)
        m.dst_rel = sb("dst_rel", [P, CHUNKS * TILES])
        m.first = sb("chunk_first", [1, CHUNKS], int32)
        m.window_p = sb("window_p", [P, CHUNKS])
        m.shift_by = sb("shift_by", [P, CHUNKS])
        m.inv_deg = sb("inv_deg", [P, BLOCKS])
        m.root = sb("root", [P, BLOCKS, D])
        m.index = sb("index", [P, 2, SLOTS * TILES], int32)
        m.one_hot = sb("one_hot", [P, 2, TILES, P])
        m.shift_mat = sb("shift_mat", [P, 2, P])
        m.sums_out_t = sb("sums_out", [P, 2, SUMC])
        m.sums_out = m.sums_out_t[:]
        m.carry = sb("carry", [P, SUMC])
        m.fall = sb("fall", [P, 2, HEADS])
        m.drop = sb("drop", [HEADS, 1])
        root = m.root[:].rearrange("p b c -> p (b c)")
        m.x_in = root[:, 0:GROUP * D].rearrange("p (j c) -> p j c", c=D)
        m.h = root[:, GROUP * D:2 * GROUP * D].rearrange("p (j c) -> p j c", c=D)
        m.bn = sb("bn", [P, GROUP, 6])
        m.mv = sb("mv", [P, GROUP, 2])
        m.std = sb("std", [P, GROUP])
        m.rstd = sb("rstd", [P, GROUP])
        m.shift = sb("shift", [P, GROUP])
        m.b_sums = sb("block_sums", [P, SUMC])
        m.b_x = sb("block_x", [P, D])
        m.b_o = sb("block_o", [P, D])
        m.b_h = sb("block_h", [P, D])
        m.b_hT = sb("block_hT", [P, D])
        m.b_aT = sb("block_aT", [P, D])
        m.b_ey = sb("block_ey", [P, D])
        m.b_msg = sb("block_msg", [P, D])
        m.b_bn = sb("block_bn", [P, 6])
        m.b_mv = sb("block_mv", [P, 2])
        m.b_weight = sb("block_weight", [P, HEADS])
        m.b_std = sb("block_std", [P, 1])
        m.b_rstd = sb("block_rstd", [P, 1])
        m.b_shift = sb("block_shift", [P, 1])
        m.b_norm2 = sb("block_norm2", [P, 1])
        m.b_norm = sb("block_norm", [P, 1])
        m.b_inv_norm = sb("block_inv_norm", [P, 1])
        m.b_degree = sb("block_degree", [P, 1])
        ring_cols = SLOTS * TILES * ROW
        ring = sb("ring", [P, ring_cols])
        m.ring = ring[:].rearrange("p (k t c) -> p k t c", k=SLOTS, t=TILES)
        size = GROUP * D
        m.hT = ring[:, 0:size].rearrange("p (j k n) -> p j k n", j=GROUP, k=2)
        m.table_rows = ring[:, size:size + GROUP * ROW].rearrange("p (j c) -> p j c", c=ROW)
        m.right_rows = ring[:, size + GROUP * ROW:size + GROUP * (ROW + 32)].rearrange("p (j c) -> p j c", c=32)
        assert ring_cols >= size + GROUP * (ROW + 32)
        at = [0]

        def part(space, cols, dt=fp32):
            view = space[:, at[0]:at[0] + cols]
            at[0] += cols
            return view if dt is fp32 else view.bitcast(dt)

        m.w_nodeT = part(ring, 2 * D).rearrange("p (j n) -> p j n", j=2)
        m.dst = part(ring, CHUNKS * TILES, int32)
        m.lin_a = part(ring, CHUNKS * TILES, int32)
        m.lin_b = part(ring, CHUNKS * TILES, int32)
        m.lin_f = part(ring, CHUNKS * TILES)
        m.first_all = part(ring, CHUNKS, int32)
        m.first_f = part(ring, CHUNKS)
        m.zeros = part(ring, GROUP * SUMC)
        m.last_all = part(ring, CHUNKS, int32)
        m.floor_all = part(ring, CHUNKS, int32)
        m.odd_all = part(ring, CHUNKS * TILES + 2 * CHUNKS)
        m.odd_line = m.odd_all[:, 0:CHUNKS * TILES]
        m.odd_span = m.odd_all[:, CHUNKS * TILES:CHUNKS * TILES + CHUNKS]
        m.odd_floor = m.odd_all[:, CHUNKS * TILES + CHUNKS:]
        work = sb("attention_work", [P, CHUNK * 7 + 2 * P + SLOTS * (CHUNK + 1) + TILES * (2 * KINDS + 32 + 4 * HEADS) + 64])
        at[0] = 0
        m.one_hotT = part(work, CHUNK)
        m.dst_bc = part(work, 2 * CHUNK, int32).rearrange("p (k e) -> p k e", k=2)
        m.e_featT = part(work, 2 * P)[0:TILES * FEATS].rearrange("p (k e) -> p k e", k=2)
        m.run_max = part(work, 2 * CHUNK)[0:HEADS].rearrange("p (k e) -> p k e", k=2)
        m.seg_max = part(work, CHUNK)[0:HEADS]
        m.flags = part(work, SLOTS * (CHUNK + 1))[0:HEADS].rearrange("p (k e) -> p k e", k=SLOTS)
        m.e_mask = part(work, 2 * TILES * KINDS).rearrange("p (k e) -> p k e", k=2)
        m.right = part(work, 2 * HEADS * KINDS).rearrange("p (k e) -> p k e", k=2)
        m.kinds = part(work, TILES * 32).rearrange("p (t c) -> p t c", t=TILES)
        m.score0 = part(work, TILES * HEADS).rearrange("p (t c) -> p t c", t=TILES)
        m.score = part(work, 2 * TILES * HEADS).rearrange("p (k t c) -> p k t c", k=2, t=TILES)
        m.diff = part(work, TILES * HEADS).rearrange("p (t c) -> p t c", t=TILES)
        at[0] = 0
        m.g_scores = root[:, 0:CHUNKS * TILES * HEADS].rearrange("p (t h) -> p t h", h=HEADS)
        m.g_rows, m.g_old = part(work, ROW), part(work, SUMC)
        m.g_same, m.g_masked = part(work, P), part(work, P)
        m.g_dst_bc = part(work, P, int32)
        m.g_featT = part(work, P)[0:FEATS]
        m.g_scoreT = part(work, P)[0:HEADS]
        m.g_wide = part(work, HEADS * P).rearrange("p (h e) -> p h e", h=HEADS)
        m.g_mask, m.g_right, m.g_kinds = part(work, KINDS), part(work, 32), part(work, 32)
        m.g_score0, m.g_score, m.g_max = part(work, HEADS), part(work, HEADS), part(work, HEADS)
        m.g_src, m.g_dst, m.g_once = part(work, 1, int32), part(work, 1, int32), part(work, 1, int32)
        m.g_dstf, m.g_dups = part(work, 1), part(work, 1)
        m.dst_all = part(work, CHUNKS * TILES, int32)
        m.ps = ctx.enter_context(nc.psum_tensor("ps", [P, 8, 512], fp32))

        setup(nc, m, a)
        node_features(nc, m, a)
        irregular = nc.values_load(m.irregular[0:1, 0:1], min_val=0, max_val=CHUNKS * (CHUNK + 2 * P))
        with nc.If(irregular < 1):
            attention(nc, m, a)
            for l in range(LAYERS):
                layer(nc, m, a, l)
        with nc.Else():
            load_destinations(nc, m, a)
            any_start(nc, m, a, m.max_dram, HEADS, -FAR)
            any_tile(nc, m, a, "anymax", ROW, m.table0, m.max_dram, "max")
            any_tile(nc, m, a, "anysum", ROW, m.table0, m.sums, "sum")
            nodes_alone(nc, m, a, "attnodes", AttentionNodes)
            for l in range(LAYERS):
                any_start(nc, m, a, m.agg_dram, D, 0.0)
                load_destinations(nc, m, a)
                any_tile(nc, m, a, f"any{l}", D, m.tables[l], m.agg_dram, None)
                nodes_alone(nc, m, a, f"nodes{l}", LayerNodes(l))


def kernel(**inputs):
    import concourse.bacc as _bacc
    from concourse import mybir as _mybir
    from concourse.bass_utils import run_bass_kernel_spmd as _run

    rows = CHUNKS * CHUNK

    def padded(x, n, fill):
        x = np.asarray(x)
        out = np.full((n,) + x.shape[1:], fill, x.dtype)
        out[:x.shape[0]] = x
        return out

    floor = np.zeros((1, CHUNKS + 1), np.int32)
    for g in range(SUPERS):
        for q, start in enumerate(STARTS):
            floor[0, g * SUPER + start + 2] = (g * GROUP + q - DELAY + 2) * P
    arrays = {"chunk_floor": floor[:, 0:CHUNKS]}
    for name, value in inputs.items():
        value = np.asarray(value)
        if name == "x":
            arrays[name] = padded(value, BLOCKS * P, 0)
        elif name == "src":
            arrays[name] = padded(value, rows, 0).reshape(-1, P).T
        elif name == "dst":
            line = padded(value, rows, BLOCKS * P - 1)
            before = np.concatenate([np.full(1, -1, line.dtype), line[:-1]])
            arrays["dst_line"] = line.reshape(P, -1)
            arrays["dst_line_before"] = before.reshape(P, -1)
            arrays["dst_edges"] = line.reshape(CHUNKS, CHUNK)
            arrays["chunk_first"] = line[0::CHUNK].reshape(1, CHUNKS)
            arrays["chunk_last"] = line[CHUNK - 1::CHUNK].reshape(1, CHUNKS)
            arrays["dst"] = line.reshape(-1, P).T
        elif name == "edge_attr_16":
            arrays[name] = padded(value, rows, 0).reshape(CHUNKS, TILES, P, FEATS).transpose(0, 1, 3, 2).reshape(CHUNKS, TILES * FEATS, P)
            arrays["feat_tiles"] = padded(value, rows, 0).reshape(-1, P, FEATS).transpose(0, 2, 1)
        elif name == "edge_attr_4":
            arrays[name] = padded(value, rows, 0).reshape(CHUNKS, TILES, P, KINDS).transpose(0, 2, 1, 3).reshape(CHUNKS, P, TILES * KINDS)
            arrays["mask_tiles"] = padded(value, rows, 0).reshape(-1, P, KINDS)
        else:
            arrays[name] = value
    arrays = {f"in_{k}": np.ascontiguousarray(v) for k, v in arrays.items()}

    nc = _bacc.Bacc("TRN2", target_bir_lowering=False, num_devices=1)
    a = {k[3:]: nc.dram_tensor(k, v.shape, _mybir.dt.from_np(v.dtype), kind="ExternalInput").ap() for k, v in arrays.items()}
    a["out"] = nc.dram_tensor("out", (BLOCKS * P, D), _mybir.dt.float32, kind="ExternalOutput").ap()
    build(nc, a)
    r = _run(nc, [arrays], core_ids=[0])
    return r.results[0]["out"][:N]
```

```python
import numpy as np
import concourse.bass as bass
from concourse import mybir
from contextlib import ExitStack
from itertools import count

fp32 = mybir.dt.float32
int32 = mybir.dt.int32
ALU = mybir.AluOpType
ACT = mybir.ActivationFunctionType
AX = mybir.AxisListType

P = 128
N, E, D = 6250, 100000, 256
HEADS, HD, KINDS, FEATS = 8, 32, 4, 16
LAYERS = 3
BLOCKS = -(-N // P)
TILES = 7
CHUNK = TILES * P
CHUNKS = -(-E // CHUNK)
SLOTS = 4
ROUNDS = CHUNKS // SLOTS
assert CHUNKS == ROUNDS * SLOTS and ROUNDS % 2 == 0
TABLE = BLOCKS * P + P
FALL = 128
BEFORE = 4
SUPER = 16
SUPERS = CHUNKS // SUPER
GROUP = 7
DELAY = 2
STARTS = [SUPER * q // GROUP for q in range(GROUP)]
GROUPS = BLOCKS // GROUP
assert BLOCKS == GROUP * GROUPS and CHUNKS == SUPER * SUPERS and SUPERS == GROUPS
HW = HD + 1
WIDE = HEADS * HW
ROW = WIDE + HEADS * KINDS
SUMC = WIDE + 1
FAR = 1.0e30
LN_EPS = 1e-5
NORM_EPS = 1e-12
SLOPE = 0.2


PHASE_NUMBERS = count()


class Mem:
    pass


class Count:

    def __init__(self, sem, buffers):
        self.sem, self.buffers = sem, buffers

    def done(self, n):
        return self.buffers + n + 1

    def free(self, n):
        return n + 1


def phase(nc, name, **sems):
    stack = ExitStack()
    made = Mem()
    made.of = {}
    name = f"{name}{next(PHASE_NUMBERS)}"
    for key, buffers in sems.items():
        sem = nc.alloc_semaphore(f"{name}_{key}")
        made.of[key] = sem if buffers is None else Count(sem, buffers)
        if buffers:
            nc.gpsimd.sem_inc(sem, buffers)
    handles = [c.sem if isinstance(c, Count) else c for c in made.of.values()]

    def clear():
        nc.clear_and_free_semaphores(handles)
        nc.all_engine_barrier()

    stack.callback(clear)
    nc.all_engine_barrier()
    return stack, stack.enter_context(nc.Block()), made.of


def hold(eng, sem, value):
    eng.wait_ge(sem, value)
    eng.nop(nofuse=True)


def group_rows(ap):
    return ap.rearrange("(g j p) d -> g p j d", p=P, j=GROUP)


def setup(nc, m, a):
    stack, block, s = phase(nc, "setup", zeroed=0, iota=0, loaded=None, tr_w=0, wt_done=0, fold=0, done_v=0, dv=0, conv=0,
                            zrows=0, zstored=None, flag=0, flag_far=0, fstored=None,
                            odd=0, odd_sum=0, odd_max=0)
    with stack:
        @block.gpsimd
        def _(pool):
            nc.gpsimd.iota(m.iota_row[:], [[1, P]], base=0, channel_multiplier=0,
                           allow_small_or_imprecise_dtypes=True)
            nc.gpsimd.iota(m.iota_p[:], [[0, 1]], base=0, channel_multiplier=1,
                           allow_small_or_imprecise_dtypes=True)
            nc.gpsimd.iota(m.step[:], [[-1, P]], base=0, channel_multiplier=1,
                           allow_small_or_imprecise_dtypes=True).then_inc(s["iota"].sem, 1)

        @block.sync
        def _(sp):
            def load(out, in_):
                sp.dma_start(out, in_).then_inc(s["loaded"], 16)

            load(m.w_node[:, :, 0:D], a["L0_gnn_W_n"].rearrange("(k p) n -> p k n", p=P))
            sp.wait_ge(s["zeroed"].sem, 1)
            for t in range(TILES):
                load(m.attn_edge[t * FEATS:(t + 1) * FEATS, t, :].rearrange("f (h n) -> f h n", n=KINDS),
                     a["L0_gnn_attn_m"].rearrange("h f t -> f h t"))
            for l in range(LAYERS):
                for half, w in ((0, f"L1_gnn_pW{l}"), (1, f"L1_gnn_rW{l}")):
                    load(m.w_pr[:, l, :, half * D:(half + 1) * D], a[w].rearrange("(k p) n -> p k n", p=P))
                for half, w in ((0, f"L1_gnn_pb{l}"), (1, f"L1_gnn_lb{l}")):
                    load(m.bias[:, l, half * D:(half + 1) * D], a[w][None, :].to_broadcast([P, D]))
                load(m.w_l[:, l], a[f"L1_gnn_lW{l}"].rearrange("(k p) n -> p k n", p=P))
            load(m.ln_w[:], a["L1_gnn_ln_w"][None, :].to_broadcast([P, D]))
            load(m.ln_b[:], a["L1_gnn_ln_b"][None, :].to_broadcast([P, D]))
            sp.wait_ge(s["zrows"].sem, 1)
            sp.dma_start(m.right_dram[BLOCKS * P:TABLE], m.zeros).then_inc(s["zstored"], 16)
            sp.wait_ge(s["flag_far"].sem, 1)
            sp.dma_start(m.flag_dram.rearrange("(p n) -> p n", p=P), m.lin_f).then_inc(s["fstored"], 16)
            sp.wait_ge(s["fstored"], 16)
            sp.wait_ge(s["zstored"], 16)

        @block.scalar
        def _(act):
            def load(out, in_):
                act.dma_start(out, in_).then_inc(s["loaded"], 16)

            load(m.src[:], a["src"])
            load(m.dst, a["dst"])
            load(m.lin_a, a["dst_line"])
            load(m.lin_b, a["dst_line_before"])
            load(m.first[:, 1:CHUNKS], a["chunk_first"][:, 1:CHUNKS])
            load(m.last_all, a["chunk_last"].to_broadcast([P, CHUNKS]))
            load(m.first_all[:, 1:CHUNKS], a["chunk_first"][:, 1:CHUNKS].to_broadcast([P, CHUNKS - 1]))
            load(m.floor_all, a["chunk_floor"].to_broadcast([P, CHUNKS]))
            act.wait_ge(s["zeroed"].sem, 1)
            for side, w in ((0, "L0_gnn_attn_l"), (1, "L0_gnn_attn_r")):
                for h in range(HEADS):
                    at = (h % 4) * HD
                    col = side * HEADS * KINDS + h * KINDS
                    load(m.attn_diag[at:at + HD, h // 4, col:col + KINDS], a[w][h])

        loads = 16 * (1 + TILES + 5 * LAYERS + 2 + 8 + 2 * HEADS)

        @block.vector
        def _(dve):
            nc.vector.memset(m.first[:, 0:1], 0)
            nc.vector.memset(m.first_all[:, 0:1], 0)
            nc.vector.memset(m.attn_edge[:], 0.0)
            nc.vector.memset(m.attn_diag[:], 0.0).then_inc(s["zeroed"].sem, 1)
            nc.vector.memset(m.zeros, 0.0).then_inc(s["zrows"].sem, 1)
            nc.vector.memset(m.eps_ln[:], LN_EPS)
            nc.vector.memset(m.ones[:], 1.0)
            nc.vector.memset(m.flags, -FAR)
            nc.vector.memset(m.run_max, 0.0)
            nc.vector.memset(m.carry[:], 0.0)
            nc.vector.memset(m.sums_out, 0.0).then_inc(s["dv"].sem, 1)
            dve.wait_ge(s["iota"].sem, 1)
            nc.vector.tensor_scalar(m.ident[:], m.step[:], 0.0, None, ALU.is_equal).then_inc(s["dv"].sem, 1)
            dve.wait_ge(s["loaded"], loads)
            nc.vector.tensor_copy(m.first_f, m.first_all).then_inc(s["conv"].sem, 1)
            dve.wait_ge(s["conv"].sem, 1)
            nc.vector.tensor_scalar(m.window_p[:], m.first_f, m.iota_p[:, 0:1], None, ALU.add)
            nc.vector.memset(m.shift_by[:], 0.0).then_inc(s["conv"].sem, 1)
            dve.wait_ge(s["conv"].sem, 2)
            nc.vector.tensor_tensor(m.shift_by[:, 1:CHUNKS], m.first_f[:, 1:CHUNKS], m.first_f[:, 0:CHUNKS - 1], ALU.subtract)
            nc.vector.tensor_tensor(m.dst_rel[:].rearrange("p (c t) -> p c t", t=TILES),
                                    m.dst.rearrange("p (c t) -> p c t", t=TILES),
                                    m.first_f[:, :, None].to_broadcast([P, CHUNKS, TILES]), ALU.subtract)
            nc.vector.tensor_tensor(m.lin_f, m.lin_a, m.lin_b, ALU.not_equal).then_inc(s["flag"].sem, 1)
            dve.wait_ge(s["flag"].sem, 1)
            nc.vector.tensor_scalar(m.lin_f, m.lin_f, -FAR, None, ALU.mult).then_inc(s["flag_far"].sem, 1)
            nc.vector.tensor_scalar(m.odd_gap, m.shift_by[:], float(P), None, ALU.is_gt)
            nc.vector.tensor_tensor(m.odd_line, m.lin_a, m.lin_b, ALU.is_lt)
            nc.vector.tensor_tensor(m.odd_floor, m.first_all, m.floor_all, ALU.is_lt)
            nc.vector.tensor_scalar(m.odd_span, m.first_all, float(P), None, ALU.add).then_inc(s["odd"].sem, 1)
            dve.wait_ge(s["odd"].sem, 1)
            nc.vector.tensor_tensor(m.odd_span, m.last_all, m.odd_span, ALU.is_ge).then_inc(s["odd"].sem, 1)
            dve.wait_ge(s["odd"].sem, 2)
            nc.vector.tensor_reduce(m.odd[:], m.odd_all, AX.X, ALU.add).then_inc(s["odd"].sem, 1)
            dve.wait_ge(s["tr_w"].sem, 1)
            for j in range(2):
                last = nc.vector.tensor_copy(m.w_nodeT[:, j, :], m.ps[:, j, 0:D])
            last.then_inc(s["wt_done"].sem, 1)
            dve.wait_ge(s["fold"].sem, 1)
            nc.vector.tensor_copy(m.w_node[:, :, D:D + 2 * HEADS * KINDS],
                                  m.ps[:, 2:4, 0:2 * HEADS * KINDS]).then_inc(s["done_v"].sem, 1)
            dve.wait_ge(s["odd_sum"].sem, 1)
            nc.vector.tensor_copy(m.irregular[:], m.ps[0:1, 4, 0:1]).then_inc(s["done_v"].sem, 1)
            dve.wait_ge(s["done_v"].sem, 2)

        @block.tensor
        def _(pe):
            pe.wait_ge(s["odd"].sem, 3)
            nc.tensor.matmul(m.ps[0:1, 4, 0:1], m.odd[:], m.ones[:], start=True, stop=True).then_inc(s["odd_sum"].sem, 1)
            pe.wait_ge(s["loaded"], loads)
            pe.wait_ge(s["dv"].sem, 2)
            for k in range(2):
                for j in range(2):
                    last = nc.tensor.transpose(m.ps[:, j, k * P:(k + 1) * P],
                                               m.w_node[:, k, j * P:(j + 1) * P], m.ident[:])
            last.then_inc(s["tr_w"].sem, 1)
            pe.wait_ge(s["wt_done"].sem, 1)
            for k in range(2):
                for j in range(2):
                    last = nc.tensor.matmul(m.ps[:, 2 + k, 0:2 * HEADS * KINDS], m.w_nodeT[:, j, k * P:(k + 1) * P],
                                            m.attn_diag[:, j, :], start=(j == 0), stop=(j == 1))
            last.then_inc(s["fold"].sem, 1)


def transpose_group(nc, m, rows):
    for j in range(GROUP):
        for k in range(2):
            at = j * 2 + k
            last = nc.tensor.transpose(m.ps[:, at // 4, (at % 4) * P:(at % 4 + 1) * P],
                                       rows[:, j, k * P:(k + 1) * P], m.ident[:])
    return last


def copy_transposed(nc, m):
    return nc.scalar.activation(m.hT.rearrange("p j k n -> p (j k n)"),
                                m.ps[:, 0:4, :].rearrange("p b n -> p (b n)")[:, 0:GROUP * D], ACT.Copy)


def group_dma(eng, ap, g, tile, store=False):
    rows = ap[bass.ds(g, 1)].rearrange("o p j d -> (o p) j d")
    return eng.dma_start(rows, tile) if store else eng.dma_start(tile, rows)


def groups(eng, norm, project, norm_first=True):
    norm(0, 0, 0)
    with eng.Fori(0, GROUPS // 2) as r:
        for b in range(2):
            if norm_first:
                norm(r * 2 + b + 1, 1 - b, r + b)
            project(r * 2 + b, b)
            if not norm_first:
                norm(r * 2 + b + 1, 1 - b, r + b)
    project(GROUPS - 1, (GROUPS - 1) % 2)


def node_features(nc, m, a):
    stack, block, s = phase(nc, "nodes", x0=None, x1=None, ln_stats=0, ln_mv=0, ln_sqrt=0, ln_rstd=0, ln_shift=0, h=2, trans=2, ht=1,
                            mm=GROUP, evac=4, stored=None, out_free=1, zero=0)
    x_g, table, right = group_rows(a["x"]), group_rows(m.table0), group_rows(m.right_dram[0:BLOCKS * P])
    with stack:
        @block.sync
        def _(sp):
            def load(g, b, turn):
                sp.wait_ge(s["h"].sem, s["h"].free(g))
                group_dma(sp, x_g, g, m.x_in[:, b]).then_inc(s[f"x{b}"], 16)

            groups(sp, load, lambda g, b: None)

        @block.gpsimd
        def _(pool):
            with pool.Fori(0, GROUPS) as g:
                pool.wait_ge(s["evac"].sem, s["evac"].done((g + 1) * GROUP - 1))
                group_dma(pool, table, g, m.table_rows, store=True).then_inc(s["stored"], 16)
                group_dma(pool, right, g, m.right_rows, store=True).then_inc(s["stored"], 16)
                pool.wait_ge(s["stored"], 32 * (g + 1))
                pool.sem_inc(s["out_free"].sem, 1)

        @block.vector
        def _(dve):
            def norm(g, b, turn):
                dve.wait_ge(s[f"x{b}"], 16 * turn + 16)
                for j in range(GROUP):
                    last = nc.vector.bn_stats(m.bn[:, b, j, :], m.x_in[:, b, j, :])
                last.then_inc(s["ln_stats"].sem, 1)
                hold(dve, s["ln_stats"].sem, s["ln_stats"].done(g))
                for j in range(GROUP):
                    last = nc.vector.bn_aggr(m.mv[:, b, j, :], m.bn[:, b, j, :])
                last.then_inc(s["ln_mv"].sem, 1)
                dve.wait_ge(s["ln_sqrt"].sem, s["ln_sqrt"].done(g))
                nc.vector.reciprocal(m.rstd[:, b, :], m.std[:, b, :]).then_inc(s["ln_rstd"].sem, 1)
                dve.wait_ge(s["ln_rstd"].sem, s["ln_rstd"].done(g))
                nc.vector.scalar_tensor_tensor(m.shift[:, b, :], m.mv[:, b, :, 0], -1.0, m.rstd[:, b, :],
                                               ALU.mult, ALU.mult).then_inc(s["ln_shift"].sem, 1)

            def project(g, b):
                dve.wait_ge(s["out_free"].sem, s["out_free"].free(g))
                for j in range(GROUP):
                    dve.wait_ge(s["mm"].sem, s["mm"].done(g * GROUP + j))
                    out = m.ps[:, 4 + j % 4, :]
                    nc.vector.tensor_copy(m.table_rows[:, j, 0:WIDE].rearrange("p (h c) -> p h c", c=HW)[:, :, 0:HD],
                                          out[:, 0:D].rearrange("p (h c) -> p h c", c=HD))
                    nc.vector.tensor_copy(m.table_rows[:, j, WIDE:ROW], out[:, D:D + 32])
                    nc.vector.tensor_copy(m.right_rows[:, j, :], out[:, D + 32:D + 64]).then_inc(s["evac"].sem, 1)

            nc.vector.memset(m.table_rows, 0.0).then_inc(s["zero"].sem, 1)
            dve.wait_ge(s["zero"].sem, 1)
            groups(dve, norm, project)

        @block.scalar
        def _(act):
            def norm(g, b, turn):
                act.wait_ge(s["ln_mv"].sem, s["ln_mv"].done(g))
                nc.scalar.activation(m.std[:, b, :], m.mv[:, b, :, 1], ACT.Sqrt, bias=m.eps_ln[:, 0:1]).then_inc(s["ln_sqrt"].sem, 1)
                act.wait_ge(s["ln_shift"].sem, s["ln_shift"].done(g))
                act.wait_ge(s["trans"].sem, s["trans"].free(g))
                for j in range(GROUP):
                    last = nc.scalar.activation(m.h[:, b, j, :], m.x_in[:, b, j, :], ACT.Relu,
                                                bias=m.shift[:, b, j:j + 1], scale=m.rstd[:, b, j:j + 1])
                last.then_inc(s["h"].sem, 1)

            def project(g, b):
                act.wait_ge(s["trans"].sem, s["trans"].done(g))
                act.wait_ge(s["mm"].sem, s["mm"].free((g + 1) * GROUP - 1))
                copy_transposed(nc, m).then_inc(s["ht"].sem, 1)

            groups(act, norm, project, norm_first=False)

        @block.tensor
        def _(pe):
            def project(g, b):
                pe.wait_ge(s["h"].sem, s["h"].done(g))
                pe.wait_ge(s["ht"].sem, s["ht"].free(g))
                transpose_group(nc, m, m.h[:, b]).then_inc(s["trans"].sem, 1)
                pe.wait_ge(s["ht"].sem, s["ht"].done(g))
                for j in range(GROUP):
                    pe.wait_ge(s["evac"].sem, s["evac"].free(g * GROUP + j) if j >= 4 else s["evac"].done(g * GROUP - 1))
                    for k in range(2):
                        last = nc.tensor.matmul(m.ps[:, 4 + j % 4, 0:D + 64], m.hT[:, j, k, :], m.w_node[:, k, :],
                                                start=(k == 0), stop=(k == 1))
                    last.then_inc(s["mm"].sem, 1)

            groups(pe, lambda g, b, turn: None, project)


def gather_chunks(nc, pool, m, s, cols, table):
    batch = SLOTS * TILES
    with pool.Fori(0, ROUNDS // 2) as r:
        for half in range(2):
            for k in range(SLOTS):
                c = (r * 2 + half) * SLOTS + k
                hold(pool, s["rows_used"].sem, s["rows_used"].free(c))
                if k == 0:
                    nc.gpsimd.tensor_copy(m.index[:, half, :], m.src[:, bass.ds((r * 2 + half) * batch, batch)]).then_inc(s["index"].sem, 1)
                    hold(pool, s["index"].sem, s["index"].done(r * 2 + half))
                for t in range(TILES):
                    at = k * TILES + t
                    pool.indirect_dma_start(m.ring[:, k, t, 0:cols], None, table,
                                            bass.IndirectOffsetOnAxis(ap=m.index[:, half, at:at + 1], axis=0)).then_inc(s[f"rows{k}"], 16)


def window(eng, m, c):
    return eng.value_load(m.first[0:1, bass.ds(c, 1)], min_val=0, max_val=BLOCKS * P - 1)


def store_window(sp, m, s, c, slot, table, cols):
    first = window(sp, m, c)
    sp.wait_ge(s["kept"].sem, s["kept"].done(c))
    sp.dma_start(table[bass.ds(first, P), 0:cols], m.sums_out[:, slot, 0:cols]).then_inc(s["stored"], 16)
    hold(sp, s["stored"], 16 * c + 16)
    sp.sem_inc(s["store"].sem, 1)


def one_hot_of(nc, dve, m, s, c, k):
    dve.wait_ge(s["summed"].sem, s["summed"].free(c))
    nc.vector.tensor_scalar(m.shift_mat[:, k % 2, :], m.step[:], m.shift_by[:, bass.ds(c, 1)], None, ALU.is_equal)
    nc.vector.tensor_tensor(m.one_hot[:, k % 2], m.iota_row[:, None, :].to_broadcast([P, TILES, P]),
                            m.dst_rel[:, bass.ds(c * TILES, TILES)][:, :, None].to_broadcast([P, TILES, P]),
                            ALU.is_equal).then_inc(s["onehot"].sem, 1)


def sum_tiles(nc, m, k, cols, tiles):
    for t in tiles:
        last = nc.tensor.matmul(m.ps[:, 6 + k % 2, 0:cols], m.one_hot[:, k % 2, t, :], m.ring[:, k, t, 0:cols],
                                start=(t == 0), stop=False)
    return last


NODE_SEMS = dict(htrans=1, ht=1, proj=1, evac=1, relu=0, put=None, put_free=1)


def there(n):
    return not isinstance(n, int) or 0 <= n < BLOCKS


def supersteps(eng, chunk, first, second):
    def superstep(g, left):
        for j in range(SUPER):
            chunk(g * (SUPER // SLOTS) + j // SLOTS, j % SLOTS, left + SUPER - 1 - j)
            for q, start in enumerate(STARTS):
                if j == start:
                    first(g * GROUP + q - DELAY)
                if j == start + 1:
                    second(g * GROUP + q - DELAY)

    superstep(0, SUPER)
    with eng.Fori(1, SUPERS - 1) as g:
        superstep(g, SUPER)
    superstep(SUPERS - 1, 0)
    for n in range(BLOCKS - DELAY, BLOCKS + 2):
        first(n)
        second(n)


def blocks_alone(eng, first, second):
    for n in range(-1, 2):
        first(n)
        second(n)
    with eng.Fori(2, BLOCKS - 1) as n:
        first(n)
        second(n)
    for n in range(BLOCKS - 1, BLOCKS + 2):
        first(n)
        second(n)


def block_rows(ap, n):
    return ap[bass.ds(n * P, P)]


def of_block(tile, n):
    return tile[:, bass.ds(n, 1), :].rearrange("p o c -> p (o c)")


def transpose_block(nc, m, bank, rows):
    for k in range(2):
        last = nc.tensor.transpose(m.ps[:, bank, k * P:(k + 1) * P], rows[:, k * P:(k + 1) * P], m.ident[:])
    return last


def project_transposed(nc, act, m, s, n):
    act.wait_ge(s["htrans"].sem, s["htrans"].done(n))
    act.wait_ge(s["proj"].sem, s["proj"].free(n))
    nc.scalar.activation(m.b_hT[:], m.ps[:, 4, 0:D], ACT.Copy).then_inc(s["ht"].sem, 1)


def project_relu(nc, act, m, s, n):
    act.wait_ge(s["evac"].sem, s["evac"].done(n))
    nc.scalar.activation(m.b_msg[:], m.b_msg[:], ACT.Relu).then_inc(s["relu"].sem, 1)


def project_transpose(nc, pe, m, s, n):
    pe.wait_ge(s["h"].sem, s["h"].done(n))
    pe.wait_ge(s["ht"].sem, s["ht"].free(n))
    transpose_block(nc, m, 4, m.b_h).then_inc(s["htrans"].sem, 1)


def project_multiply(nc, pe, m, s, l, n):
    pe.wait_ge(s["ht"].sem, s["ht"].done(n))
    pe.wait_ge(s["evac"].sem, s["evac"].free(n))
    for k in range(2):
        last = nc.tensor.matmul(m.ps[:, 5, :], m.b_hT[:, k * P:(k + 1) * P], m.w_pr[:, l, k, :], start=(k == 0), stop=(k == 1))
    last.then_inc(s["proj"].sem, 1)


def project_bias(nc, dve, m, s, l, n):
    dve.wait_ge(s["proj"].sem, s["proj"].done(n))
    dve.wait_ge(s["put_free"].sem, s["put_free"].free(n))
    nc.vector.tensor_tensor(m.b_msg[:], m.ps[:, 5, 0:D], m.bias[:, l, 0:D], ALU.add)
    nc.vector.tensor_tensor(of_block(m.root, n), m.ps[:, 5, D:2 * D], m.bias[:, l, D:2 * D], ALU.add).then_inc(s["evac"].sem, 1)


def project_store(sp, m, s, table, n):
    sp.wait_ge(s["relu"].sem, s["relu"].done(n))
    sp.dma_start(block_rows(table, n), m.b_msg[:]).then_inc(s["put"], 16)


def project_stored(sp, s, n):
    hold(sp, s["put"], 16 * n + 16)
    sp.sem_inc(s["put_free"].sem, 1)


def norm_statistics(nc, dve, m, s, rows, n):
    nc.vector.bn_stats(m.b_bn[:], rows).then_inc(s["stats"].sem, 1)
    hold(dve, s["stats"].sem, s["stats"].done(n))
    nc.vector.bn_aggr(m.b_mv[:], m.b_bn[:]).then_inc(s["mv"].sem, 1)


def norm_scale(nc, dve, m, s, n):
    dve.wait_ge(s["std"].sem, s["std"].done(n))
    nc.vector.reciprocal(m.b_rstd[:], m.b_std[:]).then_inc(s["rstd"].sem, 1)
    dve.wait_ge(s["rstd"].sem, s["rstd"].done(n))
    nc.vector.scalar_tensor_tensor(m.b_shift[:], m.b_mv[:, 0:1], -1.0, m.b_rstd[:], ALU.mult, ALU.mult).then_inc(s["shift"].sem, 1)


def norm_sqrt(nc, act, m, s, n):
    act.wait_ge(s["mv"].sem, s["mv"].done(n))
    nc.scalar.activation(m.b_std[:], m.b_mv[:, 1:2], ACT.Sqrt, bias=m.eps_ln[:, 0:1]).then_inc(s["std"].sem, 1)


def norm_apply(nc, act, m, s, rows, func, n):
    act.wait_ge(s["shift"].sem, s["shift"].done(n))
    act.wait_ge(s["h_free"].sem, s["h_free"].free(n))
    nc.scalar.activation(m.b_h[:], rows, func, bias=m.b_shift[:, 0:1], scale=m.b_rstd[:, 0:1]).then_inc(s["h"].sem, 1)


NORM_SEMS = dict(stats=0, mv=0, std=0, rstd=0, shift=0)


class AttentionNodes:

    sems = dict(NODE_SEMS, **NORM_SEMS, sums=None, floors=0, recips=0, norm=1, x1=1, x1_put=None, x1_free=1, h=1)

    @staticmethod
    def sync(nc, sp, m, a, s):
        def first(n):
            pass

        def second(n):
            if there(n + 1):
                sp.wait_ge(s["x1"].sem, s["x1"].free(n + 1))
                sp.dma_start(m.b_sums[:, 0:SUMC], block_rows(m.sums, n + 1)).then_inc(s["sums"], 16)
                sp.dma_start(m.b_x[:], block_rows(a["x"], n + 1)).then_inc(s["sums"], 16)
            if there(n):
                sp.wait_ge(s["x1"].sem, s["x1"].done(n))
                sp.dma_start(block_rows(m.x1, n), m.b_o[:]).then_inc(s["x1_put"], 16)
            if there(n - 2):
                project_store(sp, m, s, m.tables[0], n - 2)
            if there(n):
                hold(sp, s["x1_put"], 16 * n + 16)
                sp.sem_inc(s["x1_free"].sem, 1)
            if there(n - 2):
                project_stored(sp, s, n - 2)

        return first, second

    @staticmethod
    def tensor(nc, pe, m, s):
        def first(n):
            if there(n - 2):
                project_multiply(nc, pe, m, s, 0, n - 2)

        def second(n):
            if there(n - 1):
                project_transpose(nc, pe, m, s, n - 1)

        return first, second

    @staticmethod
    def vector(nc, dve, m, s):
        def first(n):
            if there(n - 1):
                norm_scale(nc, dve, m, s, n - 1)

        def second(n):
            if there(n - 2):
                project_bias(nc, dve, m, s, 0, n - 2)
            if not there(n):
                return
            dve.wait_ge(s["sums"], 32 * n + 32)
            heads = m.b_sums[:, 0:WIDE].rearrange("p (h c) -> p h c", c=HW)
            nc.vector.tensor_scalar(m.b_degree[:], m.b_sums[:, WIDE:SUMC], 1.0, None, ALU.max)
            nc.vector.tensor_scalar(m.b_weight[:], heads[:, :, HD], 1.0e-30, None, ALU.max).then_inc(s["floors"].sem, 1)
            dve.wait_ge(s["floors"].sem, s["floors"].done(n))
            nc.vector.reciprocal(m.inv_deg[:, bass.ds(n, 1)], m.b_degree[:])
            nc.vector.reciprocal(m.b_weight[:], m.b_weight[:]).then_inc(s["recips"].sem, 1)
            dve.wait_ge(s["recips"].sem, s["recips"].done(n))
            dve.wait_ge(s["x1_free"].sem, s["x1_free"].free(n))
            dve.wait_ge(s["h"].sem, s["h"].free(n))
            nc.vector.tensor_tensor(m.b_o[:].rearrange("p (h c) -> p h c", c=HD), heads[:, :, 0:HD],
                                    m.b_weight[:, :, None].to_broadcast([P, HEADS, HD]), ALU.mult).then_inc(s["norm"].sem, 1)
            dve.wait_ge(s["norm"].sem, s["norm"].done(n))
            nc.vector.tensor_tensor(m.b_o[:], m.b_o[:], m.b_x[:], ALU.add).then_inc(s["x1"].sem, 1)
            hold(dve, s["x1"].sem, s["x1"].done(n))
            norm_statistics(nc, dve, m, s, m.b_o[:], n)

        return first, second

    @staticmethod
    def scalar(nc, act, m, s):
        def first(n):
            if there(n - 1):
                norm_apply(nc, act, m, dict(s, h_free=s["htrans"]), m.b_o[:], ACT.Relu, n - 1)

        def second(n):
            if there(n):
                norm_sqrt(nc, act, m, s, n)
            if there(n - 2):
                project_relu(nc, act, m, s, n - 2)
            if there(n - 1):
                project_transposed(nc, act, m, s, n - 1)

        return first, second


class LayerNodes:

    def __init__(self, l):
        self.l, self.final = l, l == LAYERS - 1
        self.sems = dict(agg=None, atrans=1, at=1, lmm=1, o=1, norm2=0, root2=0, floor=0, recip=0, h=1)
        if self.final:
            self.sems.update(NORM_SEMS, x1=None, y=0, aff=0, affb=0, out=1, put=None, put_free=1)
        else:
            self.sems.update(NODE_SEMS, ey=0, e1=0, er=0)

    def sync(self, nc, sp, m, a, s):
        def first(n):
            if self.final:
                if there(n - 1):
                    sp.wait_ge(s["out"].sem, s["out"].done(n - 1))
                    sp.dma_start(block_rows(a["out"], n - 1), m.b_h[:]).then_inc(s["put"], 16)
                    hold(sp, s["put"], 16 * (n - 1) + 16)
                    sp.sem_inc(s["put_free"].sem, 1)
                if there(n):
                    sp.dma_start(m.b_x[:], block_rows(m.x1, n)).then_inc(s["x1"], 16)

        def second(n):
            if there(n + 1):
                sp.wait_ge(s["atrans"].sem, s["atrans"].free(n + 1))
                sp.dma_start(m.b_sums[:, 0:D], block_rows(m.agg_dram, n + 1)).then_inc(s["agg"], 16)
            if not self.final and there(n - 2):
                project_store(sp, m, s, m.tables[self.l + 1], n - 2)
                project_stored(sp, s, n - 2)

        return first, second

    def tensor(self, nc, pe, m, s):
        def first(n):
            if not self.final and there(n - 1):
                project_transpose(nc, pe, m, s, n - 1)
            if there(n):
                pe.wait_ge(s["agg"], 16 * n + 16)
                pe.wait_ge(s["at"].sem, s["at"].free(n))
                transpose_block(nc, m, 0, m.b_sums).then_inc(s["atrans"].sem, 1)

        def second(n):
            if there(n):
                pe.wait_ge(s["at"].sem, s["at"].done(n))
                pe.wait_ge(s["o"].sem, s["o"].free(n))
                for k in range(2):
                    last = nc.tensor.matmul(m.ps[:, 2, 0:D], m.b_aT[:, k * P:(k + 1) * P], m.w_l[:, self.l, k, :],
                                            start=(k == 0), stop=(k == 1))
                last.then_inc(s["lmm"].sem, 1)
            if not self.final and there(n - 1):
                project_multiply(nc, pe, m, s, self.l + 1, n - 1)

        return first, second

    def vector(self, nc, dve, m, s):
        def first(n):
            if not self.final and there(n - 2):
                project_bias(nc, dve, m, s, self.l + 1, n - 2)

        def second(n):
            if there(n):
                dve.wait_ge(s["lmm"].sem, s["lmm"].done(n))
                nc.vector.scalar_tensor_tensor(m.b_o[:], m.ps[:, 2, 0:D], m.inv_deg[:, bass.ds(n, 1)], of_block(m.root, n),
                                               ALU.mult, ALU.add).then_inc(s["o"].sem, 1)
            if not there(n):
                return
            dve.wait_ge(s["root2"].sem, s["root2"].done(n))
            nc.vector.tensor_scalar(m.b_norm[:], m.b_norm[:], NORM_EPS, -1.0, ALU.max, ALU.mult).then_inc(s["floor"].sem, 1)
            dve.wait_ge(s["floor"].sem, s["floor"].done(n))
            nc.vector.reciprocal(m.b_inv_norm[:], m.b_norm[:]).then_inc(s["recip"].sem, 1)
            if not self.final:
                dve.wait_ge(s["ey"].sem, s["ey"].done(n))
                nc.vector.tensor_scalar(m.b_ey[:], m.b_ey[:], 1.0, -1.0, ALU.add, ALU.mult).then_inc(s["e1"].sem, 1)
                dve.wait_ge(s["e1"].sem, s["e1"].done(n))
                nc.vector.reciprocal(m.b_ey[:], m.b_ey[:]).then_inc(s["er"].sem, 1)
                dve.wait_ge(s["er"].sem, s["er"].done(n))
                dve.wait_ge(s["htrans"].sem, s["htrans"].free(n))
                nc.vector.scalar_tensor_tensor(m.b_h[:], m.b_o[:], m.b_inv_norm[:, 0:1], m.b_ey[:], ALU.mult, ALU.mult).then_inc(s["h"].sem, 1)
            else:
                dve.wait_ge(s["recip"].sem, s["recip"].done(n))
                nc.vector.tensor_scalar(m.b_ey[:], m.b_o[:], m.b_inv_norm[:, 0:1], -1.0, ALU.mult, ALU.mult).then_inc(s["y"].sem, 1)
                hold(dve, s["y"].sem, s["y"].done(n))
                norm_statistics(nc, dve, m, s, m.b_ey[:], n)
                norm_scale(nc, dve, m, s, n)
                dve.wait_ge(s["h"].sem, s["h"].done(n))
                nc.vector.tensor_tensor(m.b_h[:], m.b_h[:], m.ln_w[:], ALU.mult).then_inc(s["aff"].sem, 1)
                dve.wait_ge(s["aff"].sem, s["aff"].done(n))
                nc.vector.tensor_tensor(m.b_h[:], m.b_h[:], m.ln_b[:], ALU.add).then_inc(s["affb"].sem, 1)
                dve.wait_ge(s["affb"].sem, s["affb"].done(n))
                dve.wait_ge(s["x1"], 16 * n + 16)
                nc.vector.tensor_tensor(m.b_h[:], m.b_h[:], m.b_x[:], ALU.add).then_inc(s["out"].sem, 1)

        return first, second

    def scalar(self, nc, act, m, s):
        def first(n):
            if not self.final and there(n - 1):
                project_transposed(nc, act, m, s, n - 1)
            if not self.final and there(n - 2):
                project_relu(nc, act, m, s, n - 2)
            if there(n):
                act.wait_ge(s["atrans"].sem, s["atrans"].done(n))
                act.wait_ge(s["lmm"].sem, s["lmm"].free(n))
                nc.scalar.activation(m.b_aT[:], m.ps[:, 0, 0:D], ACT.Copy).then_inc(s["at"].sem, 1)

        def second(n):
            if there(n):
                act.wait_ge(s["o"].sem, s["o"].done(n))
                nc.scalar.activation(m.b_ey[:], m.b_o[:], ACT.Square, accum_out=m.b_norm2[:, 0:1]).then_inc(s["norm2"].sem, 1)
                act.wait_ge(s["norm2"].sem, s["norm2"].done(n))
                nc.scalar.activation(m.b_norm[:], m.b_norm2[:], ACT.Sqrt).then_inc(s["root2"].sem, 1)
                if not self.final:
                    act.wait_ge(s["recip"].sem, s["recip"].done(n))
                    nc.scalar.activation(m.b_ey[:], m.b_o[:], ACT.Exp, scale=m.b_inv_norm[:, 0:1]).then_inc(s["ey"].sem, 1)
            if self.final and there(n):
                norm_sqrt(nc, act, m, s, n)
                norm_apply(nc, act, m, dict(s, h_free=s["put_free"]), m.b_ey[:], ACT.Identity, n)

        return first, second


def nodes_alone(nc, m, a, name, nodes):
    stack, block, s = phase(nc, name, **nodes.sems)
    with stack:
        @block.sync
        def _(sp):
            blocks_alone(sp, *nodes.sync(nc, sp, m, a, s))

        @block.tensor
        def _(pe):
            blocks_alone(pe, *nodes.tensor(nc, pe, m, s))

        @block.vector
        def _(dve):
            blocks_alone(dve, *nodes.vector(nc, dve, m, s))

        @block.scalar
        def _(act):
            blocks_alone(act, *nodes.scalar(nc, act, m, s))


def layer(nc, m, a, l):
    nodes = LayerNodes(l)
    stack, block, s = phase(nc, f"layer{l}", rows0=None, rows1=None, rows2=None, rows3=None, index=0, rows_used=SLOTS,
                            onehot=0, summed=2, kept=2, stored=None, store=2, **nodes.sems)
    with stack:
        @block.gpsimd
        def _(pool):
            gather_chunks(nc, pool, m, s, D, m.tables[l])

        @block.sync
        def _(sp):
            def chunk(i, k, left):
                store_window(sp, m, s, i * SLOTS + k, k % 2, m.agg_dram, D)

            supersteps(sp, chunk, *nodes.sync(nc, sp, m, a, s))

        @block.tensor
        def _(pe):
            def chunk(i, k, left):
                c = i * SLOTS + k
                pe.wait_ge(s[f"rows{k}"], 16 * TILES * (i + 1))
                pe.wait_ge(s["onehot"].sem, s["onehot"].done(c))
                pe.wait_ge(s["kept"].sem, s["kept"].free(c))
                sum_tiles(nc, m, k, D, range(TILES)).then_inc(s["rows_used"].sem, 1)
                pe.wait_ge(s["kept"].sem, s["kept"].done(c - 1))
                nc.tensor.matmul(m.ps[:, 6 + k % 2, 0:D], m.shift_mat[:, k % 2, :], m.sums_out[:, 1 - k % 2, 0:D],
                                 start=False, stop=True).then_inc(s["summed"].sem, 1)

            supersteps(pe, chunk, *nodes.tensor(nc, pe, m, s))

        @block.vector
        def _(dve):
            def chunk(i, k, left):
                if left:
                    one_hot_of(nc, dve, m, s, i * SLOTS + k + 1, k + 1)

            nc.vector.memset(m.sums_out[:, 1, :], 0.0)
            one_hot_of(nc, dve, m, s, 0, 0)
            supersteps(dve, chunk, *nodes.vector(nc, dve, m, s))

        @block.scalar
        def _(act):
            def chunk(i, k, left):
                c = i * SLOTS + k
                act.wait_ge(s["summed"].sem, s["summed"].done(c))
                act.wait_ge(s["store"].sem, s["store"].free(c))
                nc.scalar.activation(m.sums_out[:, k % 2, 0:D], m.ps[:, 6 + k % 2, 0:D], ACT.Copy).then_inc(s["kept"].sem, 1)

            supersteps(act, chunk, *nodes.scalar(nc, act, m, s))


def attention(nc, m, a):
    nodes = AttentionNodes
    stack, block, s = phase(nc, "attend", rows0=None, rows1=None, rows2=None, rows3=None, index=0, rows_used=SLOTS,
                            edges0=None, edges1=None, edges2=None, edges3=None, oht=0, right=SLOTS, kinds=1, masked=0, red=0, leaky=SLOTS,
                            xt=1, fwd=2, bwd=SLOTS, mt=1, drop=1, diff=1, expd=0, fallen=2, weighed=0,
                            onehot=0, apart=0, shifted=0, summed=2, scaled=2, kept=2, stored=None, store=2, **nodes.sems)
    featT = a["edge_attr_16"]
    mask = a["edge_attr_4"]
    ring_heads = [m.ring[:, k, :, 0:WIDE].rearrange("p t (h c) -> p t h c", c=HW) for k in range(SLOTS)]
    loads = 5

    def edge_loads(i, k):
        return 16 * loads * (i + 1)

    def ahead(i, k, n):
        return i + (k + n) // SLOTS, (k + n) % SLOTS

    def pipeline(eng, step, slots):
        step((0, 0), None, None)
        step((0, 1), (0, 0), None)

        def body(i, k, left):
            step(ahead(i, k, 2) if left >= 2 else None, ahead(i, k, 1) if left >= 1 else None, (i, k))

        supersteps(eng, body, *slots)

    with stack:
        @block.gpsimd
        def _(pool):
            gather_chunks(nc, pool, m, s, ROW, m.table0)

        @block.sync
        def _(sp):
            def load(i, k):
                c = i * SLOTS + k
                first = window(sp, m, c)
                sp.wait_ge(s["right"].sem, s["right"].free(c))
                sp.wait_ge(s["leaky"].sem, s["leaky"].free(c))
                sp.wait_ge(s["bwd"].sem, s["bwd"].free(c))
                sem = s[f"edges{k}"]
                sp.dma_start(m.dst_bc[:, k, :], a["dst_edges"][bass.ds(c, 1)].to_broadcast([P, CHUNK])).then_inc(sem, 16)
                sp.dma_start(m.right[:, k, :], m.right_dram[bass.ds(first, P)]).then_inc(sem, 16)
                sp.dma_start(m.e_featT[:, k, :], featT[bass.ds(c, 1)].rearrange("o f e -> (o f) e")).then_inc(sem, 16)
                sp.dma_start(m.e_mask[:, k, :], mask[bass.ds(c, 1)].rearrange("o p n -> (o p) n")).then_inc(sem, 16)
                sp.dma_start(m.flags[:, k, 0:CHUNK], m.flag_rows[bass.ds(c, 1)].to_broadcast([HEADS, CHUNK])).then_inc(sem, 16)

            def body(i, k, left):
                if left >= SLOTS:
                    load(*ahead(i, k, SLOTS))
                store_window(sp, m, s, i * SLOTS + k, k % 2, m.sums, SUMC)

            for k in range(SLOTS):
                load(0, k)
            supersteps(sp, body, *nodes.sync(nc, sp, m, a, s))

        @block.tensor
        def _(pe):
            def to_heads(i, k):
                c = i * SLOTS + k
                pe.wait_ge(s["leaky"].sem, s["leaky"].done(c))
                pe.wait_ge(s["fwd"].sem, s["fwd"].done(c - 1))
                for t in range(TILES):
                    last = nc.tensor.transpose(m.ps[0:HEADS, 1 + t // 4, (t % 4) * P:(t % 4 + 1) * P],
                                               m.score[:, k % 2, t, :], m.ident[:])
                last.then_inc(s["xt"].sem, 1)

            def scores(i, k):
                c = i * SLOTS + k
                pe.wait_ge(s[f"edges{k}"], edge_loads(i, k))
                pe.wait_ge(s["kinds"].sem, s["kinds"].free(c))
                nc.tensor.matmul(m.ps[:, 0, 0:TILES * 32], m.e_featT[:, k, :], m.attn_edge[:].rearrange("f t c -> f (t c)"),
                                 start=True, stop=False)
                pe.wait_ge(s["oht"].sem, s["oht"].done(c))
                for t in range(TILES):
                    last = nc.tensor.matmul(m.ps[:, 0, t * 32:(t + 1) * 32], m.one_hotT[:, t * P:(t + 1) * P],
                                            m.right[:, k, :], start=False, stop=(t == TILES - 1))
                last.then_inc(s["right"].sem, 1)

            def to_edges(i, k):
                c = i * SLOTS + k
                pe.wait_ge(s["diff"].sem, s["diff"].free(c))
                pe.wait_ge(s["fallen"].sem, s["fallen"].done(c - 1))
                hold(pe, s["drop"].sem, s["drop"].done(c))
                nc.tensor.matmul(m.ps[:, 3, FALL:FALL + HEADS], m.drop[:, 0:1].to_broadcast([HEADS, P]),
                                 m.ident[0:HEADS, 0:HEADS], start=True, stop=True)
                for t in range(TILES):
                    last = nc.tensor.transpose(m.ps[:, 3, t * HEADS:(t + 1) * HEADS],
                                               m.seg_max[:, t * P:(t + 1) * P], m.ident[0:HEADS, 0:HEADS])
                last.then_inc(s["mt"].sem, 1)

            def chunk(i, k, left):
                c = i * SLOTS + k
                pe.wait_ge(s["weighed"].sem, s["weighed"].done(c))
                pe.wait_ge(s["onehot"].sem, s["onehot"].done(c))
                pe.wait_ge(s["shifted"].sem, s["shifted"].done(c))
                pe.wait_ge(s["kept"].sem, s["kept"].free(c))
                sum_tiles(nc, m, k, SUMC, range(0, BEFORE))
                if left >= 1:
                    to_edges(*ahead(i, k, 1))
                sum_tiles(nc, m, k, SUMC, range(BEFORE, TILES - 1))
                if left >= 2:
                    to_heads(*ahead(i, k, 2))
                sum_tiles(nc, m, k, SUMC, range(TILES - 1, TILES)).then_inc(s["rows_used"].sem, 1)
                pe.wait_ge(s["scaled"].sem, s["scaled"].done(c))
                nc.tensor.matmul(m.ps[:, 6 + k % 2, 0:SUMC], m.shift_mat[:, k % 2, :], m.carry[:],
                                 start=False, stop=True).then_inc(s["summed"].sem, 1)
                if left >= 3:
                    scores(*ahead(i, k, 3))

            scores(0, 0)
            to_heads(0, 0)
            scores(0, 1)
            to_edges(0, 0)
            to_heads(0, 1)
            scores(0, 2)
            supersteps(pe, chunk, *nodes.tensor(nc, pe, m, s))

        @block.vector
        def _(dve):
            def step(score, weigh, total):
                if score:
                    ai, ak = score
                    ac, aslot = ai * SLOTS + ak, ak % 2
                    hold(dve, s[f"edges{ak}"], edge_loads(ai, ak))
                    dve.wait_ge(s["right"].sem, s["right"].done(ac - 1))
                    nc.vector.tensor_scalar(m.one_hotT, m.dst_bc[:, ak, :], m.window_p[:, bass.ds(ac, 1)], None,
                                            ALU.is_equal).then_inc(s["oht"].sem, 1)
                if total:
                    i, k = total
                    c = i * SLOTS + k
                    dve.wait_ge(s["expd"].sem, s["expd"].done(c))
                    nc.vector.tensor_tensor(ring_heads[k][:, :, :, 0:HD], ring_heads[k][:, :, :, 0:HD],
                                            ring_heads[k][:, :, :, HD:HW].to_broadcast([P, TILES, HEADS, HD]),
                                            ALU.mult).then_inc(s["weighed"].sem, 1)
                if weigh:
                    bi, bk = weigh
                    bc, bslot = bi * SLOTS + bk, bk % 2
                    dve.wait_ge(s["xt"].sem, s["xt"].done(bc))
                    nc.vector.tensor_tensor_scan(m.run_max[:, bslot, :], m.flags[:, bk, 0:CHUNK],
                                                 m.ps[0:HEADS, 1:3, :].rearrange("p b n -> p (b n)")[:, 0:CHUNK],
                                                 m.run_max[:, 1 - bslot, CHUNK - 1:CHUNK], ALU.add, ALU.max).then_inc(s["fwd"].sem, 1)
                if weigh:
                    dve.wait_ge(s["fwd"].sem, s["fwd"].done(bc))
                    dve.wait_ge(s["mt"].sem, s["mt"].free(bc))
                    nc.vector.tensor_tensor_scan(m.seg_max[:, ::-1], m.flags[:, bk, 1:CHUNK + 1][:, ::-1], m.run_max[:, bslot, ::-1],
                                                 0.0, ALU.add, ALU.max).then_inc(s["bwd"].sem, 1)
                if weigh:
                    dve.wait_ge(s["bwd"].sem, s["bwd"].done(bc))
                    nc.vector.tensor_scalar(m.drop[:], m.run_max[:, 1 - bslot, CHUNK - 1:CHUNK], m.seg_max[:, 0:1], 0.0,
                                            ALU.subtract, ALU.min).then_inc(s["drop"].sem, 1)
                if score:
                    dve.wait_ge(s["right"].sem, s["right"].done(ac))
                    dve.wait_ge(s[f"rows{ak}"], 16 * TILES * (ai + 1))
                    nc.vector.tensor_tensor(m.kinds, m.ps[:, 0, 0:TILES * 32].rearrange("p (t c) -> p t c", c=32),
                                            m.ring[:, ak, :, WIDE:ROW], ALU.add).then_inc(s["kinds"].sem, 1)
                if score:
                    dve.wait_ge(s["kinds"].sem, s["kinds"].done(ac))
                    kinds4 = m.kinds.rearrange("p t (h n) -> p t h n", n=KINDS)
                    mask4 = m.e_mask[:, ak, :].rearrange("p (t n) -> p t n", n=KINDS)[:, :, None, :].to_broadcast([P, TILES, HEADS, KINDS])
                    nc.vector.tensor_tensor(kinds4, kinds4, mask4, ALU.mult).then_inc(s["masked"].sem, 1)
                if weigh:
                    dve.wait_ge(s["summed"].sem, s["summed"].free(bc))
                    nc.vector.tensor_scalar(m.shift_mat[:, bslot, :], m.step[:], m.shift_by[:, bass.ds(bc, 1)], None,
                                            ALU.is_equal).then_inc(s["shifted"].sem, 1)
                if score:
                    dve.wait_ge(s["masked"].sem, s["masked"].done(ac))
                    nc.vector.tensor_reduce(m.score0, kinds4, AX.X, ALU.add).then_inc(s["red"].sem, 1)
                if score:
                    dve.wait_ge(s["red"].sem, s["red"].done(ac))
                    nc.vector.scalar_tensor_tensor(m.score[:, aslot], m.score0, SLOPE, m.score0, ALU.mult, ALU.max).then_inc(s["leaky"].sem, 1)
                if total:
                    rescale(i, k)
                if weigh:
                    dve.wait_ge(s["mt"].sem, s["mt"].done(bc))
                    nc.vector.tensor_tensor(m.diff, m.score[:, bslot], m.ps[:, 3, 0:TILES * HEADS].rearrange("p (t h) -> p t h", h=HEADS),
                                            ALU.subtract).then_inc(s["diff"].sem, 1)
                if weigh:
                    nc.vector.memset(m.ring[:, bk, :, WIDE:SUMC], 1.0)

            def rescale(i, k):
                c = i * SLOTS + k
                slot = (k + 1) % 2
                dve.wait_ge(s["kept"].sem, s["kept"].done(c - 1))
                dve.wait_ge(s["fallen"].sem, s["fallen"].done(c))
                nc.vector.tensor_copy(m.carry[:, WIDE:SUMC], m.sums_out[:, slot, WIDE:SUMC])
                nc.vector.tensor_tensor(m.carry[:, 0:WIDE].rearrange("p (h c) -> p h c", c=HW),
                                        m.sums_out[:, slot, 0:WIDE].rearrange("p (h c) -> p h c", c=HW),
                                        m.fall[:, k % 2, :, None].to_broadcast([P, HEADS, HW]), ALU.mult).then_inc(s["scaled"].sem, 1)

            pipeline(dve, step, nodes.vector(nc, dve, m, s))

        @block.scalar
        def _(act):
            def keep(c, parity):
                act.wait_ge(s["summed"].sem, s["summed"].done(c))
                act.wait_ge(s["store"].sem, s["store"].free(c))
                act.wait_ge(s["scaled"].sem, s["scaled"].done(c - 1))
                nc.scalar.activation(m.sums_out[:, parity, 0:SUMC], m.ps[:, 6 + parity, 0:SUMC], ACT.Copy).then_inc(s["kept"].sem, 1)

            def step(score, weigh, total):
                if total and not (isinstance(total[0], int) and total == (0, 0)):
                    i, k = total
                    keep(i * SLOTS + k - 1, (k + 1) % 2)
                if weigh:
                    i, k = weigh
                    c = i * SLOTS + k
                    act.wait_ge(s["diff"].sem, s["diff"].done(c))
                    nc.scalar.activation(ring_heads[k][:, :, :, HD], m.diff, ACT.Exp, scale=1.0 / 3.0).then_inc(s["expd"].sem, 1)
                    act.wait_ge(s["scaled"].sem, s["scaled"].free(c))
                    nc.scalar.activation(m.fall[:, k % 2, :], m.ps[:, 3, FALL:FALL + HEADS], ACT.Exp, scale=1.0 / 3.0).then_inc(s["fallen"].sem, 1)
                    act.wait_ge(s["summed"].sem, s["summed"].free(c))
                    for t in range(TILES):
                        last = nc.scalar.activation(m.one_hot[:, k % 2, t, :], m.iota_row[:], ACT.Abs,
                                                    bias=m.dst_rel[:, bass.ds(c * TILES + t, 1)], scale=-1.0)
                    last.then_inc(s["apart"].sem, 1)
                    act.wait_ge(s["apart"].sem, s["apart"].done(c))
                    nc.scalar.activation(m.one_hot[:, k % 2], m.one_hot[:, k % 2], ACT.Relu, bias=1.0, scale=-1.0).then_inc(s["onehot"].sem, 1)
                elif total:
                    keep(CHUNKS - 1, (CHUNKS - 1) % 2)

            pipeline(act, step, nodes.scalar(nc, act, m, s))


def any_tile(nc, m, a, name, cols, table, into, attend):
    stack, block, s = phase(nc, name, edges=None, edges_free=1, index=0, got=None, scores=0, sT=0, sTc=0, rowmax=0,
                            same=0, first=0, uniq=0, work=0, ready=0, put=None, summed=0, merged=0, expd=0)
    weigh = attend == "sum"
    tiles = CHUNKS * TILES
    with stack:
        @block.sync
        def _(sp):
            with sp.Fori(0, tiles) as t:
                sp.wait_ge(s["edges_free"].sem, s["edges_free"].free(t))
                sp.dma_start(m.g_dst_bc, m.dst_tiles[bass.ds(t, 1)].to_broadcast([P, P])).then_inc(s["edges"], 16)
                sp.dma_start(m.g_featT, a["feat_tiles"][bass.ds(t, 1)].rearrange("o f e -> (o f) e")).then_inc(s["edges"], 16)
                sp.dma_start(m.g_mask, a["mask_tiles"][bass.ds(t, 1)].rearrange("o p n -> (o p) n")).then_inc(s["edges"], 16)

        @block.gpsimd
        def _(pool):
            with pool.Fori(0, tiles) as t:
                hold(pool, s["uniq"].sem, s["uniq"].done(t))
                pool.indirect_dma_start(m.g_rows[:, 0:cols], None, table,
                                        bass.IndirectOffsetOnAxis(ap=m.g_src, axis=0)).then_inc(s["got"], 16)
                if attend == "max":
                    pool.indirect_dma_start(m.g_right, None, m.right_dram,
                                            bass.IndirectOffsetOnAxis(ap=m.g_dst, axis=0)).then_inc(s["got"], 16)
                if attend == "sum":
                    pool.indirect_dma_start(m.g_max, None, m.max_dram,
                                            bass.IndirectOffsetOnAxis(ap=m.g_dst, axis=0)).then_inc(s["got"], 16)
                width = HEADS if attend == "max" else SUMC if weigh else D
                pool.indirect_dma_start(m.g_old[:, 0:width], None, into,
                                        bass.IndirectOffsetOnAxis(ap=m.g_dst, axis=0)).then_inc(s["got"], 16)
                hold(pool, s["merged"].sem, s["merged"].done(t))
                pool.indirect_dma_start(into, bass.IndirectOffsetOnAxis(ap=m.g_once, axis=0), m.g_old[:, 0:width], None,
                                        bounds_check=TABLE - 1, oob_is_err=False).then_inc(s["put"], 16)
                hold(pool, s["put"], 16 * t + 16)
                pool.sem_inc(s["edges_free"].sem, 1)

        @block.tensor
        def _(pe):
            with pe.Fori(0, tiles) as t:
                if attend == "max":
                    pe.wait_ge(s["edges"], 48 * t + 48)
                    nc.tensor.matmul(m.ps[:, 0, 0:32], m.g_featT, m.attn_edge[0:FEATS, 0, :],
                                     start=True, stop=True).then_inc(s["scores"].sem, 1)
                    pe.wait_ge(s["ready"].sem, s["ready"].done(t))
                    nc.tensor.transpose(m.ps[0:HEADS, 1, 0:P], m.g_score, m.ident[:]).then_inc(s["sT"].sem, 1)
                    pe.wait_ge(s["sTc"].sem, s["sTc"].done(t))
                    for h in range(HEADS):
                        last = nc.tensor.matmul(m.ps[:, 2 + h // 4, (h % 4) * P:(h % 4 + 1) * P],
                                                m.ident[0:HEADS, h:h + 1].to_broadcast([HEADS, P]), m.g_scoreT,
                                                start=True, stop=True)
                    last.then_inc(s["rowmax"].sem, 1)
                else:
                    pe.wait_ge(s["ready"].sem, s["ready"].done(t))
                    width = SUMC if weigh else D
                    nc.tensor.matmul(m.ps[:, 0, 0:width], m.g_same, m.g_rows[:, 0:width],
                                     start=True, stop=True).then_inc(s["summed"].sem, 1)

        @block.vector
        def _(dve):
            with dve.Fori(0, tiles) as t:
                n = [0]

                def link(ins):
                    n[0] += 1
                    ins.then_inc(s["work"].sem, 1)
                    dve.wait_ge(s["work"].sem, total * t + n[0])

                total = {"max": 13, "sum": 10, None: 7}[attend]
                dve.wait_ge(s["edges"], 48 * t + 48)
                nc.vector.tensor_copy(m.g_src, m.src[:, bass.ds(t, 1)])
                link(nc.vector.tensor_copy(m.g_dst, m.dst_all[:, bass.ds(t, 1)]))
                link(nc.vector.tensor_copy(m.g_dstf, m.g_dst))
                link(nc.vector.tensor_scalar(m.g_same, m.g_dst_bc, m.g_dstf, None, ALU.is_equal))
                link(nc.vector.scalar_tensor_tensor(m.g_masked, m.step[:], 0.0, m.g_same, ALU.is_gt, ALU.mult))
                link(nc.vector.tensor_reduce(m.g_dups, m.g_masked, AX.X, ALU.add))
                link(nc.vector.tensor_scalar(m.g_dups, m.g_dups, float(TABLE), None, ALU.mult))
                link(nc.vector.tensor_tensor(m.g_dups, m.g_dups, m.g_dstf, ALU.add))
                nc.vector.tensor_copy(m.g_once, m.g_dups).then_inc(s["uniq"].sem, 1)
                gets = 32 if attend is None else 48
                dve.wait_ge(s["got"], gets * t + gets)
                if attend == "max":
                    dve.wait_ge(s["scores"].sem, s["scores"].done(t))
                    kinds = m.g_kinds
                    link(nc.vector.tensor_tensor(kinds, m.ps[:, 0, 0:32], m.g_rows[:, WIDE:ROW], ALU.add))
                    link(nc.vector.tensor_tensor(kinds, kinds, m.g_right, ALU.add))
                    kinds3 = kinds.rearrange("p (h n) -> p h n", n=KINDS)
                    link(nc.vector.tensor_tensor(kinds3, kinds3, m.g_mask[:, None, :].to_broadcast([P, HEADS, KINDS]), ALU.mult))
                    link(nc.vector.tensor_reduce(m.g_score0, kinds3, AX.X, ALU.add))
                    nc.vector.scalar_tensor_tensor(m.g_score, m.g_score0, SLOPE, m.g_score0, ALU.mult, ALU.max).then_inc(s["ready"].sem, 1)
                    dve.wait_ge(s["ready"].sem, s["ready"].done(t))
                    nc.vector.tensor_copy(m.g_scores[:, bass.ds(t, 1), :].rearrange("p o h -> p (o h)"), m.g_score)
                    dve.wait_ge(s["sT"].sem, s["sT"].done(t))
                    nc.vector.tensor_copy(m.g_scoreT, m.ps[0:HEADS, 1, 0:P]).then_inc(s["sTc"].sem, 1)
                    link(nc.vector.tensor_scalar(m.g_masked, m.g_same, FAR, -FAR, ALU.mult, ALU.add))
                    dve.wait_ge(s["rowmax"].sem, s["rowmax"].done(t))
                    wide = m.ps[:, 2:4, :].rearrange("p b n -> p (b n)").rearrange("p (h e) -> p h e", h=HEADS)
                    nc.vector.tensor_tensor(m.g_wide, wide, m.g_masked[:, None, :].to_broadcast([P, HEADS, P]), ALU.add).then_inc(s["same"].sem, 1)
                    dve.wait_ge(s["same"].sem, s["same"].done(t))
                    link(nc.vector.tensor_reduce(m.g_score0, m.g_wide, AX.X, ALU.max))
                    nc.vector.tensor_tensor(m.g_old[:, 0:HEADS], m.g_old[:, 0:HEADS], m.g_score0, ALU.max).then_inc(s["merged"].sem, 1)
                else:
                    if weigh:
                        link(nc.vector.tensor_tensor(m.g_score0, m.g_scores[:, bass.ds(t, 1), :].rearrange("p o h -> p (o h)"),
                                                     m.g_max, ALU.subtract))
                        nc.vector.memset(m.g_rows[:, WIDE:SUMC], 1.0)
                        link(nc.vector.tensor_copy(m.g_score, m.g_score0))
                        nc.vector.memset(m.g_kinds, 0.0).then_inc(s["first"].sem, 1)
                        dve.wait_ge(s["expd"].sem, s["expd"].done(t))
                        heads = m.g_rows[:, 0:WIDE].rearrange("p (h c) -> p h c", c=HW)
                        link(nc.vector.tensor_tensor(heads[:, :, 0:HD], heads[:, :, 0:HD],
                                                     heads[:, :, HD:HW].to_broadcast([P, HEADS, HD]), ALU.mult))
                    nc.vector.memset(m.g_kinds, 0.0).then_inc(s["ready"].sem, 1)
                    dve.wait_ge(s["summed"].sem, s["summed"].done(t))
                    width = SUMC if weigh else D
                    nc.vector.tensor_tensor(m.g_old[:, 0:width], m.g_old[:, 0:width], m.ps[:, 0, 0:width], ALU.add).then_inc(s["merged"].sem, 1)
                hold(dve, s["edges_free"].sem, s["edges_free"].done(t))

        if weigh:
            @block.scalar
            def _(act):
                with act.Fori(0, tiles) as t:
                    act.wait_ge(s["first"].sem, s["first"].done(t))
                    nc.scalar.activation(m.g_rows[:, 0:WIDE].rearrange("p (h c) -> p h c", c=HW)[:, :, HD],
                                         m.g_score, ACT.Exp, scale=1.0 / 3.0).then_inc(s["expd"].sem, 1)


def load_destinations(nc, m, a):
    stack, block, s = phase(nc, "dests", loaded=None)
    with stack:
        @block.sync
        def _(sp):
            sp.dma_start(m.dst_all, a["dst"]).then_inc(s["loaded"], 16)
            sp.wait_ge(s["loaded"], 16)


def any_start(nc, m, a, table, cols, value):
    stack, block, s = phase(nc, "fill", filled=0, stored=None)
    with stack:
        @block.vector
        def _(dve):
            nc.vector.memset(m.g_old[:, 0:cols], value).then_inc(s["filled"].sem, 1)

        @block.sync
        def _(sp):
            sp.wait_ge(s["filled"].sem, 1)
            for b in range(BLOCKS + 1):
                sp.dma_start(table[b * P:(b + 1) * P], m.g_old[:, 0:cols]).then_inc(s["stored"], 16)
            sp.wait_ge(s["stored"], 16 * (BLOCKS + 1))


def build(nc, a):
    m = Mem()

    def dram(name, *shape):
        return nc.dram_tensor(name, shape, fp32, kind="Internal").ap()

    m.table0 = dram("attention_table", BLOCKS * P, ROW)
    m.right_dram = dram("right_scores", TABLE, HEADS * KINDS)
    m.sums = dram("attention_sums", TABLE, SUMC)
    m.agg_dram = dram("message_sums", TABLE, D)
    m.tables = [dram(f"message_table{l}", BLOCKS * P, D) for l in range(LAYERS)]
    m.x1 = dram("x_after_attention", BLOCKS * P, D)
    m.max_dram = dram("score_maxima", TABLE, HEADS)
    m.flag_dram = dram("run_flags", CHUNKS * CHUNK)
    m.dst_tiles = a["dst_edges"].rearrange("c (t e) -> (c t) e", e=P)
    m.flag_rows = m.flag_dram.rearrange("(c n) -> c n", n=CHUNK)
    with ExitStack() as ctx:
        def sb(name, shape, dt=fp32):
            return ctx.enter_context(nc.sbuf_tensor(name, shape, dt))

        m.iota_row = sb("iota_row", [P, P])
        m.iota_p = sb("iota_p", [P, 1])
        m.step = sb("step", [P, P])
        m.ident = sb("ident", [P, P])
        m.eps_ln = sb("eps_ln", [P, 1])
        m.ones = sb("ones", [P, 1])
        m.odd = sb("odd", [P, 1])
        m.irregular = sb("irregular", [1, 1], int32)
        m.w_node = sb("w_node", [P, 2, D + 64])
        m.attn_diag = sb("attn_diag", [P, 2, 64])
        m.attn_edge = sb("attn_edge", [TILES * FEATS, TILES, HEADS * KINDS])
        m.w_pr = sb("w_pr", [P, LAYERS, 2, 2 * D])
        m.w_l = sb("w_l", [P, LAYERS, 2, D])
        m.bias = sb("bias", [P, LAYERS, 2 * D])
        m.ln_w = sb("ln_w", [P, D])
        m.ln_b = sb("ln_b", [P, D])
        m.src = sb("src_index", [P, CHUNKS * TILES], int32)
        m.dst_rel = sb("dst_rel", [P, CHUNKS * TILES])
        m.first = sb("chunk_first", [1, CHUNKS], int32)
        m.window_p = sb("window_p", [P, CHUNKS])
        m.shift_by = sb("shift_by", [P, CHUNKS])
        m.inv_deg = sb("inv_deg", [P, BLOCKS])
        m.root = sb("root", [P, BLOCKS, D])
        m.index = sb("index", [P, 2, SLOTS * TILES], int32)
        m.one_hot = sb("one_hot", [P, 2, TILES, P])
        m.shift_mat = sb("shift_mat", [P, 2, P])
        m.sums_out_t = sb("sums_out", [P, 2, SUMC])
        m.sums_out = m.sums_out_t[:]
        m.carry = sb("carry", [P, SUMC])
        m.fall = sb("fall", [P, 2, HEADS])
        m.drop = sb("drop", [HEADS, 1])
        root = m.root[:].rearrange("p b c -> p (b c)")
        size = GROUP * D
        m.x_in = root[:, 0:2 * size].rearrange("p (k j c) -> p k j c", k=2, c=D)
        m.h = root[:, 2 * size:4 * size].rearrange("p (k j c) -> p k j c", k=2, c=D)
        m.bn = sb("bn", [P, 2, GROUP, 6])
        m.mv = sb("mv", [P, 2, GROUP, 2])
        m.std = sb("std", [P, 2, GROUP])
        m.rstd = sb("rstd", [P, 2, GROUP])
        m.shift = sb("shift", [P, 2, GROUP])
        m.b_sums = sb("block_sums", [P, SUMC])
        m.b_x = sb("block_x", [P, D])
        m.b_o = sb("block_o", [P, D])
        m.b_h = sb("block_h", [P, D])
        m.b_hT = sb("block_hT", [P, D])
        m.b_aT = sb("block_aT", [P, D])
        m.b_ey = sb("block_ey", [P, D])
        m.b_msg = sb("block_msg", [P, D])
        m.b_bn = sb("block_bn", [P, 6])
        m.b_mv = sb("block_mv", [P, 2])
        m.b_weight = sb("block_weight", [P, HEADS])
        m.b_std = sb("block_std", [P, 1])
        m.b_rstd = sb("block_rstd", [P, 1])
        m.b_shift = sb("block_shift", [P, 1])
        m.b_norm2 = sb("block_norm2", [P, 1])
        m.b_norm = sb("block_norm", [P, 1])
        m.b_inv_norm = sb("block_inv_norm", [P, 1])
        m.b_degree = sb("block_degree", [P, 1])
        ring_cols = SLOTS * TILES * ROW
        ring = sb("ring", [P, ring_cols])
        m.ring = ring[:].rearrange("p (k t c) -> p k t c", k=SLOTS, t=TILES)
        m.hT = ring[:, 0:size].rearrange("p (j k n) -> p j k n", j=GROUP, k=2)
        m.table_rows = ring[:, size:size + GROUP * ROW].rearrange("p (j c) -> p j c", c=ROW)
        m.right_rows = ring[:, size + GROUP * ROW:size + GROUP * (ROW + 32)].rearrange("p (j c) -> p j c", c=32)
        assert ring_cols >= size + GROUP * (ROW + 32)
        at = [0]

        def part(space, cols, dt=fp32):
            view = space[:, at[0]:at[0] + cols]
            at[0] += cols
            return view if dt is fp32 else view.bitcast(dt)

        m.w_nodeT = part(ring, 2 * D).rearrange("p (j n) -> p j n", j=2)
        m.dst = part(ring, CHUNKS * TILES, int32)
        m.lin_a = part(ring, CHUNKS * TILES, int32)
        m.lin_b = part(ring, CHUNKS * TILES, int32)
        m.lin_f = part(ring, CHUNKS * TILES)
        m.first_all = part(ring, CHUNKS, int32)
        m.first_f = part(ring, CHUNKS)
        m.zeros = part(ring, HEADS * KINDS)
        m.last_all = part(ring, CHUNKS, int32)
        m.floor_all = part(ring, CHUNKS, int32)
        m.odd_all = part(ring, CHUNKS * TILES + 3 * CHUNKS)
        m.odd_line = m.odd_all[:, 0:CHUNKS * TILES]
        m.odd_span = m.odd_all[:, CHUNKS * TILES:CHUNKS * TILES + CHUNKS]
        m.odd_floor = m.odd_all[:, CHUNKS * TILES + CHUNKS:CHUNKS * TILES + 2 * CHUNKS]
        m.odd_gap = m.odd_all[:, CHUNKS * TILES + 2 * CHUNKS:]
        work = sb("attention_work", [P, CHUNK * 4 + SLOTS * (2 * CHUNK + 1 + P + TILES * KINDS + HEADS * KINDS) + TILES * (32 + 4 * HEADS)])
        at[0] = 0
        m.one_hotT = part(work, CHUNK)
        m.dst_bc = part(work, SLOTS * CHUNK, int32).rearrange("p (k e) -> p k e", k=SLOTS)
        m.e_featT = part(work, SLOTS * P)[0:TILES * FEATS].rearrange("p (k e) -> p k e", k=SLOTS)
        m.run_max = part(work, 2 * CHUNK)[0:HEADS].rearrange("p (k e) -> p k e", k=2)
        m.seg_max = part(work, CHUNK)[0:HEADS]
        m.flags = part(work, SLOTS * (CHUNK + 1))[0:HEADS].rearrange("p (k e) -> p k e", k=SLOTS)
        m.e_mask = part(work, SLOTS * TILES * KINDS).rearrange("p (k e) -> p k e", k=SLOTS)
        m.right = part(work, SLOTS * HEADS * KINDS).rearrange("p (k e) -> p k e", k=SLOTS)
        m.kinds = part(work, TILES * 32).rearrange("p (t c) -> p t c", t=TILES)
        m.score0 = part(work, TILES * HEADS).rearrange("p (t c) -> p t c", t=TILES)
        m.score = part(work, 2 * TILES * HEADS).rearrange("p (k t c) -> p k t c", k=2, t=TILES)
        m.diff = part(work, TILES * HEADS).rearrange("p (t c) -> p t c", t=TILES)
        at[0] = 0
        m.g_scores = root[:, 0:CHUNKS * TILES * HEADS].rearrange("p (t h) -> p t h", h=HEADS)
        m.g_rows, m.g_old = part(work, ROW), part(work, SUMC)
        m.g_same, m.g_masked = part(work, P), part(work, P)
        m.g_dst_bc = part(work, P, int32)
        m.g_featT = part(work, P)[0:FEATS]
        m.g_scoreT = part(work, P)[0:HEADS]
        m.g_wide = part(work, HEADS * P).rearrange("p (h e) -> p h e", h=HEADS)
        m.g_mask, m.g_right, m.g_kinds = part(work, KINDS), part(work, 32), part(work, 32)
        m.g_score0, m.g_score, m.g_max = part(work, HEADS), part(work, HEADS), part(work, HEADS)
        m.g_src, m.g_dst, m.g_once = part(work, 1, int32), part(work, 1, int32), part(work, 1, int32)
        m.g_dstf, m.g_dups = part(work, 1), part(work, 1)
        m.dst_all = part(work, CHUNKS * TILES, int32)
        m.ps = ctx.enter_context(nc.psum_tensor("ps", [P, 8, 512], fp32))

        setup(nc, m, a)
        node_features(nc, m, a)
        irregular = nc.values_load(m.irregular[0:1, 0:1], min_val=0, max_val=CHUNKS * (CHUNK + 3 * P))
        with nc.If(irregular < 1):
            attention(nc, m, a)
            for l in range(LAYERS):
                layer(nc, m, a, l)
        with nc.Else():
            load_destinations(nc, m, a)
            any_start(nc, m, a, m.max_dram, HEADS, -FAR)
            any_tile(nc, m, a, "anymax", ROW, m.table0, m.max_dram, "max")
            any_start(nc, m, a, m.sums, SUMC, 0.0)
            any_tile(nc, m, a, "anysum", ROW, m.table0, m.sums, "sum")
            nodes_alone(nc, m, a, "attnodes", AttentionNodes)
            for l in range(LAYERS):
                any_start(nc, m, a, m.agg_dram, D, 0.0)
                load_destinations(nc, m, a)
                any_tile(nc, m, a, f"any{l}", D, m.tables[l], m.agg_dram, None)
                nodes_alone(nc, m, a, f"nodes{l}", LayerNodes(l))


def kernel(**inputs):
    import concourse.bacc as _bacc
    from concourse import mybir as _mybir
    from concourse.bass_utils import run_bass_kernel_spmd as _run

    rows = CHUNKS * CHUNK

    def padded(x, n, fill):
        x = np.asarray(x)
        out = np.full((n,) + x.shape[1:], fill, x.dtype)
        out[:x.shape[0]] = x
        return out

    floor = np.zeros((1, CHUNKS + 1), np.int32)
    for g in range(SUPERS):
        for q, start in enumerate(STARTS):
            floor[0, g * SUPER + start + 2] = (g * GROUP + q - DELAY + 2) * P
    arrays = {"chunk_floor": floor[:, 0:CHUNKS]}
    for name, value in inputs.items():
        value = np.asarray(value)
        if name == "x":
            arrays[name] = padded(value, BLOCKS * P, 0)
        elif name == "src":
            arrays[name] = padded(value, rows, 0).reshape(-1, P).T
        elif name == "dst":
            line = padded(value, rows, BLOCKS * P - 1)
            before = np.concatenate([np.full(1, -1, line.dtype), line[:-1]])
            arrays["dst_line"] = line.reshape(P, -1)
            arrays["dst_line_before"] = before.reshape(P, -1)
            arrays["dst_edges"] = line.reshape(CHUNKS, CHUNK)
            arrays["chunk_first"] = line[0::CHUNK].reshape(1, CHUNKS)
            arrays["chunk_last"] = line[CHUNK - 1::CHUNK].reshape(1, CHUNKS)
            arrays["dst"] = line.reshape(-1, P).T
        elif name == "edge_attr_16":
            arrays[name] = padded(value, rows, 0).reshape(CHUNKS, TILES, P, FEATS).transpose(0, 1, 3, 2).reshape(CHUNKS, TILES * FEATS, P)
            arrays["feat_tiles"] = padded(value, rows, 0).reshape(-1, P, FEATS).transpose(0, 2, 1)
        elif name == "edge_attr_4":
            arrays[name] = padded(value, rows, 0).reshape(CHUNKS, TILES, P, KINDS).transpose(0, 2, 1, 3).reshape(CHUNKS, P, TILES * KINDS)
            arrays["mask_tiles"] = padded(value, rows, 0).reshape(-1, P, KINDS)
        else:
            arrays[name] = value
    arrays = {f"in_{k}": np.ascontiguousarray(v) for k, v in arrays.items()}

    nc = _bacc.Bacc("TRN2", target_bir_lowering=False, num_devices=1)
    a = {k[3:]: nc.dram_tensor(k, v.shape, _mybir.dt.from_np(v.dtype), kind="ExternalInput").ap() for k, v in arrays.items()}
    a["out"] = nc.dram_tensor("out", (BLOCKS * P, D), _mybir.dt.float32, kind="ExternalOutput").ap()
    build(nc, a)
    r = _run(nc, [arrays], core_ids=[0])
    return r.results[0]["out"][:N]
```
